# Optimizing a Trainium2 kernel written in Bass

```python
import numpy as np
import jax
import jax.numpy as jnp

def _softmax(x, axis=-1):
    return jax.nn.softmax(x, axis=axis)

def _gelu(x):
    return jax.nn.gelu(x, approximate=True)

def _silu(x):
    return jax.nn.silu(x)

def _sigmoid(x):
    return jax.nn.sigmoid(x)

def _layernorm(x, axis=-1, eps=1e-05):
    m = jnp.mean(x, axis=axis, keepdims=True)
    v = jnp.var(x, axis=axis, keepdims=True)
    return (x - m) / jnp.sqrt(v + eps)

def _scatter_add(tgt, idx, src, axis=0):
    return tgt.at[idx].add(src)

def _segment_sum(src, seg, n):
    return jax.ops.segment_sum(src, seg, n)
kernel_name = 'mk_recurrent_d1_jaxref_r8_22ec8c'

def setup_inputs(seed: int=0):
    np.random.seed(seed)
    _w = jnp.asarray

    def _L0_attn_setup():
        import jax, jax.numpy as jnp
        import numpy as np
        N_HEADS = 16
        BLOCK_SIZE = 32

        def _rope(x):
            B, H, L, d = x.shape
            inv_freq = 1.0 / 10000.0 ** (jnp.arange(0, d, 2, dtype=jnp.float32) / d)
            t = jnp.arange(L, dtype=jnp.float32)[:, None] * inv_freq[None, :]
            cos, sin = (jnp.cos(t), jnp.sin(t))
            x1, x2 = (x[..., 0::2], x[..., 1::2])
            return jnp.concatenate([x1 * cos - x2 * sin, x2 * cos + x1 * sin], axis=-1)
        key = jax.random.key(seed)
        k1, k2, k3 = jax.random.split(key, 3)
        B, L, D = (2, 512, 128)
        x = jax.random.normal(k1, (B, L, D), dtype=jnp.float32)
        Wqkv = jax.random.normal(k2, (3 * D, D), dtype=jnp.float32) * 0.02
        Wout = jax.random.normal(k3, (D, D), dtype=jnp.float32) * 0.02
        return {'x': x, 'Wqkv': Wqkv, 'Wout': Wout}
    _L0_attn_in = _L0_attn_setup()

    def _L0_ffn_setup():
        import jax, jax.numpy as jnp
        import numpy as np
        DIM = 128
        DEPTH = 2
        HEADS = 8
        DIM_HEAD = 64
        WINDOW = 64
        INNER = HEADS * DIM_HEAD
        HID = int(DIM * 4 * 2 / 3)
        B, N = (2, 1024)
        QK_SCALE = 8.0

        def shift_token(t):
            t1, t2 = jnp.split(t, 2, axis=-1)
            t2 = jnp.pad(t2, ((0, 0), (1, 0), (0, 0)))[:, :-1]
            return jnp.concatenate([t1, t2], axis=-1)

        def l2norm(t):
            return t / jnp.clip(jnp.linalg.norm(t, axis=-1, keepdims=True), 1e-12)

        def rotate_half(x):
            x1, x2 = jnp.split(x, 2, axis=-1)
            return jnp.concatenate([-x2, x1], axis=-1)

        def rotary_xpos(q, k):
            n = q.shape[-2]
            half_idx = jnp.arange(0, DIM_HEAD, 2, dtype=jnp.float32)
            inv_freq = 1.0 / 10000.0 ** (half_idx / DIM_HEAD)
            t = jnp.arange(n, dtype=jnp.float32)
            freqs = t[:, None] * inv_freq[None, :]
            freqs = jnp.concatenate([freqs, freqs], axis=-1)
            base = (half_idx + 0.4 * DIM_HEAD) / (1.4 * DIM_HEAD)
            power = (t - n // 2) / float(WINDOW // 2)
            scale = base[None, :] ** power[:, None]
            scale = jnp.concatenate([scale, scale], axis=-1)
            cos, sin = (jnp.cos(freqs), jnp.sin(freqs))
            q = q * cos * scale + rotate_half(q) * sin * scale
            k = k * cos / scale + rotate_half(k) * sin / scale
            return (q, k)

        def local_attention(q, k, v):
            b, h, n, d = q.shape
            w = n // WINDOW
            bq = q.reshape(b, h, w, WINDOW, d) * QK_SCALE
            bk = k.reshape(b, h, w, WINDOW, d)
            bv = v.reshape(b, h, w, WINDOW, d)

            def look_around(t):
                p = jnp.pad(t, ((0, 0), (0, 0), (1, 0), (0, 0), (0, 0)))
                return jnp.concatenate([p[:, :, :w], p[:, :, 1:]], axis=3)
            bk, bv = (look_around(bk), look_around(bv))
            bt = jnp.arange(n).reshape(w, WINDOW)
            btp = jnp.pad(bt, ((1, 0), (0, 0)), constant_values=-1)
            btk = jnp.concatenate([btp[:w], btp[1:]], axis=1)
            sim = jnp.einsum('bhwid,bhwjd->bhwij', bq, bk)
            i = bt[:, :, None]
            j = btk[:, None, :]
            mask = (i < j) | (i > j + WINDOW) | (j == -1)
            sim = jnp.where(mask, -jnp.finfo(sim.dtype).max, sim)
            attn = jax.nn.softmax(sim, axis=-1)
            out = jnp.einsum('bhwij,bhwjd->bhwid', attn, bv)
            return out.reshape(b, h, n, d)

        def _layer(x, wqkv, qs, ksc, wo, lg, lb, w1, b1, w2, b2):
            b, n, _ = x.shape
            h = shift_token(x)
            qkv = h @ wqkv
            q, k, v = jnp.split(qkv, 3, axis=-1)
            to_heads = lambda t: t.reshape(b, n, HEADS, DIM_HEAD).transpose(0, 2, 1, 3)
            q, k, v = (to_heads(q), to_heads(k), to_heads(v))
            q = l2norm(q) * qs
            k = l2norm(k) * ksc
            q, k = rotary_xpos(q, k)
            o = local_attention(q, k, v)
            o = o.transpose(0, 2, 1, 3).reshape(b, n, INNER)
            x = x + o @ wo
            h = shift_token(x)
            mu = h.mean(-1, keepdims=True)
            var = h.var(-1, keepdims=True)
            h = (h - mu) / jnp.sqrt(var + 1e-05) * lg + lb
            h = h @ w1 + b1
            a, g = jnp.split(h, 2, axis=-1)
            h = a * jax.nn.gelu(g, approximate=False)
            x = x + h @ w2 + b2
            return x
        key = jax.random.key(seed)
        ks = jax.random.split(key, 6)
        return {'x': jax.random.normal(ks[0], (B, N, DIM), jnp.float32), 'wqkv': jax.random.normal(ks[1], (DEPTH, DIM, 3 * INNER), jnp.float32) * 0.02, 'q_scale': jnp.ones((DEPTH, DIM_HEAD), jnp.float32), 'k_scale': jnp.ones((DEPTH, DIM_HEAD), jnp.float32), 'wo': jax.random.normal(ks[2], (DEPTH, INNER, DIM), jnp.float32) * 0.02, 'ln_g': jnp.ones((DEPTH, DIM), jnp.float32), 'ln_b': jnp.zeros((DEPTH, DIM), jnp.float32), 'w1': jax.random.normal(ks[3], (DEPTH, DIM, 2 * HID), jnp.float32) * 0.02, 'b1': jnp.zeros((DEPTH, 2 * HID), jnp.float32), 'w2': jax.random.normal(ks[4], (DEPTH, HID, DIM), jnp.float32) * 0.02, 'b2': jnp.zeros((DEPTH, DIM), jnp.float32)}
    _L0_ffn_in = _L0_ffn_setup()
    _d = {'L0_attn_x': _L0_attn_in['x'], 'L0_attn_Wqkv': _L0_attn_in['Wqkv'], 'L0_attn_Wout': _L0_attn_in['Wout'], 'L0_ffn_wqkv': _L0_ffn_in['wqkv'], 'L0_ffn_q_scale': _L0_ffn_in['q_scale'], 'L0_ffn_k_scale': _L0_ffn_in['k_scale'], 'L0_ffn_wo': _L0_ffn_in['wo'], 'L0_ffn_ln_g': _L0_ffn_in['ln_g'], 'L0_ffn_ln_b': _L0_ffn_in['ln_b'], 'L0_ffn_w1': _L0_ffn_in['w1'], 'L0_ffn_b1': _L0_ffn_in['b1'], 'L0_ffn_w2': _L0_ffn_in['w2'], 'L0_ffn_b2': _L0_ffn_in['b2']}
    _x0 = _d['L0_attn_x']
    _d['L0_attn_x'] = jax.random.normal(jax.random.fold_in(jax.random.key(seed), 1), (4, 1024, 128), dtype=_x0.dtype)
    del _x0
    return _d

def reference(L0_attn_x, L0_attn_Wqkv, L0_attn_Wout, L0_ffn_wqkv, L0_ffn_q_scale, L0_ffn_k_scale, L0_ffn_wo, L0_ffn_ln_g, L0_ffn_ln_b, L0_ffn_w1, L0_ffn_b1, L0_ffn_w2, L0_ffn_b2):

    def _L0_attn_ref(x, Wqkv, Wout):
        import jax, jax.numpy as jnp
        import numpy as np
        N_HEADS = 16
        BLOCK_SIZE = 32

        def _rope(x):
            B, H, L, d = x.shape
            inv_freq = 1.0 / 10000.0 ** (jnp.arange(0, d, 2, dtype=jnp.float32) / d)
            t = jnp.arange(L, dtype=jnp.float32)[:, None] * inv_freq[None, :]
            cos, sin = (jnp.cos(t), jnp.sin(t))
            x1, x2 = (x[..., 0::2], x[..., 1::2])
            return jnp.concatenate([x1 * cos - x2 * sin, x2 * cos + x1 * sin], axis=-1)
        H, BS = (N_HEADS, BLOCK_SIZE)
        B, L, D = x.shape
        HD = D // H
        scale = HD ** (-0.5)
        nb = L // BS
        qkv = (x @ Wqkv.T).reshape(B, L, 3, H, HD).transpose(2, 0, 3, 1, 4)
        q, k, v = (qkv[0], qkv[1], qkv[2])
        q, k = (_rope(q), _rope(k))
        qb = q.reshape(B, H, nb, BS, HD)
        kb = k.reshape(B, H, nb, BS, HD)
        vb = v.reshape(B, H, nb, BS, HD)
        att = jnp.einsum('bhnqd,bhnkd->bhnqk', qb, kb) * scale
        causal = jnp.tril(jnp.ones((BS, BS), dtype=bool))
        att = jnp.where(causal, att, jnp.finfo(att.dtype).min)
        att = jax.nn.softmax(att, axis=-1)
        out = jnp.einsum('bhnqk,bhnkd->bhnqd', att, vb)
        out = out.reshape(B, H, L, HD).transpose(0, 2, 1, 3).reshape(B, L, D)
        return out @ Wout.T

    def _L0_ffn_ref(x, wqkv, q_scale, k_scale, wo, ln_g, ln_b, w1, b1, w2, b2):
        import jax, jax.numpy as jnp
        import numpy as np
        DIM = 128
        DEPTH = 2
        HEADS = 8
        DIM_HEAD = 64
        WINDOW = 64
        INNER = HEADS * DIM_HEAD
        HID = int(DIM * 4 * 2 / 3)
        B, N = (2, 1024)
        QK_SCALE = 8.0

        def shift_token(t):
            t1, t2 = jnp.split(t, 2, axis=-1)
            t2 = jnp.pad(t2, ((0, 0), (1, 0), (0, 0)))[:, :-1]
            return jnp.concatenate([t1, t2], axis=-1)

        def l2norm(t):
            return t / jnp.clip(jnp.linalg.norm(t, axis=-1, keepdims=True), 1e-12)

        def rotate_half(x):
            x1, x2 = jnp.split(x, 2, axis=-1)
            return jnp.concatenate([-x2, x1], axis=-1)

        def rotary_xpos(q, k):
            n = q.shape[-2]
            half_idx = jnp.arange(0, DIM_HEAD, 2, dtype=jnp.float32)
            inv_freq = 1.0 / 10000.0 ** (half_idx / DIM_HEAD)
            t = jnp.arange(n, dtype=jnp.float32)
            freqs = t[:, None] * inv_freq[None, :]
            freqs = jnp.concatenate([freqs, freqs], axis=-1)
            base = (half_idx + 0.4 * DIM_HEAD) / (1.4 * DIM_HEAD)
            power = (t - n // 2) / float(WINDOW // 2)
            scale = base[None, :] ** power[:, None]
            scale = jnp.concatenate([scale, scale], axis=-1)
            cos, sin = (jnp.cos(freqs), jnp.sin(freqs))
            q = q * cos * scale + rotate_half(q) * sin * scale
            k = k * cos / scale + rotate_half(k) * sin / scale
            return (q, k)

        def local_attention(q, k, v):
            b, h, n, d = q.shape
            w = n // WINDOW
            bq = q.reshape(b, h, w, WINDOW, d) * QK_SCALE
            bk = k.reshape(b, h, w, WINDOW, d)
            bv = v.reshape(b, h, w, WINDOW, d)

            def look_around(t):
                p = jnp.pad(t, ((0, 0), (0, 0), (1, 0), (0, 0), (0, 0)))
                return jnp.concatenate([p[:, :, :w], p[:, :, 1:]], axis=3)
            bk, bv = (look_around(bk), look_around(bv))
            bt = jnp.arange(n).reshape(w, WINDOW)
            btp = jnp.pad(bt, ((1, 0), (0, 0)), constant_values=-1)
            btk = jnp.concatenate([btp[:w], btp[1:]], axis=1)
            sim = jnp.einsum('bhwid,bhwjd->bhwij', bq, bk)
            i = bt[:, :, None]
            j = btk[:, None, :]
            mask = (i < j) | (i > j + WINDOW) | (j == -1)
            sim = jnp.where(mask, -jnp.finfo(sim.dtype).max, sim)
            attn = jax.nn.softmax(sim, axis=-1)
            out = jnp.einsum('bhwij,bhwjd->bhwid', attn, bv)
            return out.reshape(b, h, n, d)

        def _layer(x, wqkv, qs, ksc, wo, lg, lb, w1, b1, w2, b2):
            b, n, _ = x.shape
            h = shift_token(x)
            qkv = h @ wqkv
            q, k, v = jnp.split(qkv, 3, axis=-1)
            to_heads = lambda t: t.reshape(b, n, HEADS, DIM_HEAD).transpose(0, 2, 1, 3)
            q, k, v = (to_heads(q), to_heads(k), to_heads(v))
            q = l2norm(q) * qs
            k = l2norm(k) * ksc
            q, k = rotary_xpos(q, k)
            o = local_attention(q, k, v)
            o = o.transpose(0, 2, 1, 3).reshape(b, n, INNER)
            x = x + o @ wo
            h = shift_token(x)
            mu = h.mean(-1, keepdims=True)
            var = h.var(-1, keepdims=True)
            h = (h - mu) / jnp.sqrt(var + 1e-05) * lg + lb
            h = h @ w1 + b1
            a, g = jnp.split(h, 2, axis=-1)
            h = a * jax.nn.gelu(g, approximate=False)
            x = x + h @ w2 + b2
            return x
        for l in range(DEPTH):
            x = _layer(x, wqkv[l], q_scale[l], k_scale[l], wo[l], ln_g[l], ln_b[l], w1[l], b1[l], w2[l], b2[l])
        return x
    x = L0_attn_x
    xn = _layernorm(x, axis=-1)
    s = _L0_attn_ref(xn, L0_attn_Wqkv, L0_attn_Wout)
    g = _silu(_L0_ffn_ref(xn, L0_ffn_wqkv, L0_ffn_q_scale, L0_ffn_k_scale, L0_ffn_wo, L0_ffn_ln_g, L0_ffn_ln_b, L0_ffn_w1, L0_ffn_b1, L0_ffn_w2, L0_ffn_b2))
    x = x + s * g
    return x

_drawn_inputs = setup_inputs


def setup_inputs(seed=0):
    import zlib

    import numpy as np

    out = dict(_drawn_inputs(seed))
    spreads = {'L0_ffn_q_scale': (1.0, 0.6),
     'L0_ffn_k_scale': (1.0, 0.6),
     'L0_ffn_ln_g': (1.0, 0.6),
     'L0_ffn_ln_b': (0.0, 0.8),
     'L0_ffn_b1': (0.0, 0.8),
     'L0_ffn_b2': (0.0, 0.8)}
    factors = {'L0_attn_Wqkv': 5.064,
     'L0_attn_Wout': 5.05,
     'L0_ffn_wqkv': 8.0,
     'L0_ffn_wo': 8.0,
     'L0_ffn_w1': 8.0,
     'L0_ffn_w2': 8.0}
    for name, (base, spread) in spreads.items():
        noise = np.random.default_rng([zlib.crc32(name.encode()), seed]).standard_normal(out[name].shape)
        drawn = base * np.exp(spread * noise) if base else spread * noise
        out[name] = jnp.asarray(drawn.astype(out[name].dtype))
    for name, factor in factors.items():
        out[name] = (out[name] * factor).astype(out[name].dtype)
    return out
```

```python
from contextlib import ExitStack

import numpy as np

import concourse.bass as bass
from concourse import mybir
from concourse.alu_op_type import AluOpType as ALU

ACT = mybir.ActivationFunctionType
AX_X = mybir.AxisListType.X
F32 = mybir.dt.float32
F32R = mybir.dt.float32r
BF16 = mybir.dt.bfloat16
I32 = mybir.dt.int32

P = 128
BATCH, SEQ, DIM = 4, 1024, 128
TOKENS = BATCH * SEQ
TILES = TOKENS // P
TPB = SEQ // P
CHUNK = 512
CHUNKS = TOKENS // CHUNK
CPB = SEQ // CHUNK
ROW = SEQ + 1
DEPTH = 2

HEADS, HD, WIN = 8, 64, 64
INNER = HEADS * HD
HID = int(DIM * 4 * 2 / 3)
PARTS = [(c, min(P, HID - c)) for c in range(0, HID, P)]
NPART = len(PARTS)

AH, AHD, ABLK = 16, 8, 32
GROUPS, INGRP = 4, 4
BLKS = P // ABLK
VW = AHD + 1

NEG = -1e30
EPS = 1e-5
MAGIC = float(0x5F3759DF)


def live(n, k, count):
    return not isinstance(n, int) or 0 <= n + k < count


def wait(eng, sem, value):
    if not isinstance(value, int) or value > 0:
        eng.wait_ge(sem, value)


def steps(eng, first, start, stop, last, step):
    for n in range(first, start):
        step(n, n % 2)
    with eng.Fori(0, (stop - start) // 2) as it:
        for u in range(2):
            step(it * 2 + (start + u), (start + u) % 2)
    for n in range(stop, last + 1):
        step(n, n % 2)


def pairs(eng, count, body):
    body(0)
    with eng.Fori(1, count) as it:
        body(it)


def build(nc, a, out):
    with ExitStack() as ctx:
        def sb(name, shape, dt=F32):
            return ctx.enter_context(nc.sbuf_tensor(name, shape, dt))

        def sem(name):
            return ctx.enter_context(nc.semaphore(name))

        X = sb("X", [P, TOKENS])
        XS = [sb(f"XS{i}", [P, BATCH * ROW]) for i in range(2)]
        D = sb("D", [P, TOKENS])
        A_OUT = sb("A_OUT", [P, TOKENS])
        ident = sb("ident", [P, P])
        ident_bf = sb("ident_bf", [P, P], BF16)
        ones = sb("ones", [P, P])
        mean_w = sb("mean_w", [P, P], F32R)
        mean_c = sb("mean_c", [P, 1])
        lmask = sb("lmask", [P, 2 * CHUNK], BF16)
        amask = sb("amask", [P, P], BF16)
        hmask = sb("hmask", [P, INGRP])
        pmask = sb("pmask", [P, INGRP])
        ltab = sb("ltab", [P, 4, TPB * HD])
        lrot = sb("lrot", [P, 4, TPB * HD])
        arot = sb("arot", [P, 2, SEQ])
        raw = sb("raw", [P, 3 * INNER])
        wqkv = sb("wqkv", [P, 2, 3 * INNER], F32R)
        awt = sb("awt", [P, 2, 4 * P], F32R)
        awv = sb("awv", [P, P])
        awo = sb("awo", [P, P])
        wo = sb("wo", [P, INNER // P, DIM])
        raw1 = sb("raw1", [P, 2 * HID])
        w1 = sb("w1", [P, 2, 2 * HID], F32R)
        w2 = sb("w2", [P, NPART, DIM])
        vecs = sb("vecs", [P, 3])
        b1 = sb("b1", [P, 2 * NPART])
        bias1 = sb("bias1", [P, 2 * NPART])
        scales = sb("scales", [P, 2, HD])
        split = sb("split", [P, 2, 2, CHUNK], F32R)
        sq = sb("sq", [P, 2, CHUNK])
        rstd = sb("rstd", [P, TILES])
        newt = sb("newt", [P, 2, TILES])
        tA = sb("tA", [P, CHUNK])
        tB = sb("tB", [P, CHUNK])
        kA = sb("kA", [P, CHUNK])
        kB = sb("kB", [P, CHUNK])
        kn = sb("kn", [P, CHUNK])
        qr = sb("qr", [P, 2, CHUNK])
        kr = sb("kr", [P, 2, CHUNK])
        qT = sb("qT", [P, 2, HEADS // 2, P])
        kT = sb("kT", [P, 2, HEADS // 2, WIN + P])
        V = sb("V", [P, 2, INNER])
        VB = sb("VB", [P, 2, INNER])
        ss = sb("ss", [P, 2, 2 * HEADS])
        nt = sb("nt", [P, 2, 2 * HEADS])
        nmax = sb("nmax", [P, 2, HEADS])
        ebias = sb("ebias", [P, 2, HEADS])
        rsum = sb("rsum", [P, 2, HEADS])
        rinv = sb("rinv", [P, 2, HEADS])
        prob = sb("prob", [P, 2, 2, CHUNK])
        pT = sb("pT", [P, 2, CHUNK])
        oT = sb("oT", [P, 2, CHUNK])
        mask_in = A_OUT[:, 0:2 * CHUNK + P]
        gel = raw[:].rearrange("p (c t) -> p c t", t=CHUNK)
        hid = prob[:].rearrange("p a b t -> p (a b) t")
        io, diag = kr, qr
        qA, kR = XS[1], D
        qst, xst = kT[:, :, 0, 0:P], qT
        kexp = prob[:, 0]
        pA = prob[:, 1]
        vexp = sb("vexp", [P, 2, BLKS * GROUPS * INGRP * VW])
        amax = nt
        rinvA = sb("rinvA", [P, 2, AH])
        oA = sb("oA", [P, 2, P])
        oAT = sb("oAT", [P, 2, P])

        ps = ctx.enter_context(nc.psum_tensor("ps", [P, 8, CHUNK], F32))

        const_in = sem("const_in")
        lnx_in = sem("lnx_in")
        layer_in = sem("layer_in")
        ones_made = sem("ones_made")
        zeros_made = sem("zeros_made")
        windows_zero = sem("windows_zero")
        vones_made = sem("vones_made")
        const_made = sem("const_made")
        split_hi = sem("split_hi")
        prep_hi = sem("prep_hi")
        prep_done = sem("prep_done")
        bias_mm = sem("bias_mm")
        ln_split = sem("ln_split")
        ln_mean = sem("ln_mean")
        ln_centred = sem("ln_centred")
        ln_squared = sem("ln_squared")
        ln_var = sem("ln_var")
        ln_rstd = sem("ln_rstd")
        ln_diag = sem("ln_diag")
        ln_bcast = sem("ln_bcast")
        ln_scaled = sem("ln_scaled")
        xs_dma = sem("xs_dma")
        ffn_hi = sem("ffn_hi")
        ffn_lo = sem("ffn_lo")
        ffn_g = sem("ffn_g")
        ffn_a = sem("ffn_a")
        ffn_gelu = sem("ffn_gelu")
        ffn_hid = sem("ffn_hid")
        ffn_y = sem("ffn_y")
        x_new = sem("x_new")
        a_split = sem("a_split")
        a_qk_mm = sem("a_qk_mm")
        a_tab = sem("a_tab")
        a_rot = sem("a_rot")
        a_stat = sem("a_stat")
        a_kexp = sem("a_kexp")
        a_score = sem("a_score")
        a_max = sem("a_max")
        a_sub = sem("a_sub")
        a_exp = sem("a_exp")
        a_v = sem("a_v")
        a_vexp = sem("a_vexp")
        a_pT = sem("a_pT")
        a_pTe = sem("a_pTe")
        a_o = sem("a_o")
        a_rinv = sem("a_rinv")
        a_on = sem("a_on")
        a_oT = sem("a_oT")
        a_oTe = sem("a_oTe")
        a_s = sem("a_s")
        a_done = sem("a_done")
        l_split = sem("l_split")
        l_qk = sem("l_qk")
        l_v = sem("l_v")
        l_sq = sem("l_sq")
        l_qm = sem("l_qm")
        l_norm = sem("l_norm")
        l_newton = sem("l_newton")
        l_kn = sem("l_kn")
        l_km = sem("l_km")
        l_qr = sem("l_qr")
        l_kr = sem("l_kr")
        l_tr = sem("l_tr")
        l_tre = sem("l_tre")
        k_prev = [sem("k_prev0"), sem("k_prev1")]
        v_prev = [sem("v_prev0"), sem("v_prev1")]
        l_ve = sem("l_ve")
        l_score = sem("l_score")
        l_max = sem("l_max")
        l_bias = sem("l_bias")
        l_exp = sem("l_exp")
        l_rinv = sem("l_rinv")
        l_prob = sem("l_prob")
        l_pT = sem("l_pT")
        l_pTe = sem("l_pTe")
        l_o = sem("l_o")
        l_oe = sem("l_oe")
        l_y = sem("l_y")
        gate_x = [sem("gate_x0"), sem("gate_x1")]
        gate_silu = sem("gate_silu")
        gate_mul = sem("gate_mul")
        gate_out = sem("gate_out")
        stored = [sem("stored0"), sem("stored1")]

        block = ctx.enter_context(nc.Block())

        def x_before_local(L):
            return CHUNKS + L * (TILES + CHUNKS)

        def x_before_ffn(L):
            return x_before_local(L) + TILES

        N_CONST = 9
        N_LAYER = 6 + NPART
        NEWTON = 12

        def xs_before_local(L):
            return 32 * (CHUNKS + L * (TILES + CHUNKS))

        def xs_before_ffn(L):
            return xs_before_local(L) + 32 * TILES

        SPLITS_BEFORE_A = CHUNKS
        SPLITS_BEFORE_L = [2 * CHUNKS + L * (TILES + CHUNKS) for L in range(DEPTH)]
        SPLITS_BEFORE = [0] + [n + TILES for n in SPLITS_BEFORE_L]

        def shifted(xs, j, width):
            per = SEQ // width
            return xs[:, bass.ds((j // per) * ROW + (j % per) * width, width)]

        def part(t, j, width):
            return t[:, bass.ds(j * width, width)]

        def hd(ap):
            return ap.rearrange("p (h d) -> p h d", h=HEADS)

        @block.sync
        def _(sp):
            for j in range(CHUNKS):
                sp.dma_start(part(D, j, CHUNK), part(a["xT"], j, CHUNK)).then_inc(lnx_in, 16)
            loads = [(ident[:], a["ident"]), (mask_in, a["masks"]), (hmask[:], a["hmask"]), (pmask[:], a["pmask"]),
                     (arot[:], a["arot"]), (raw[:, 0:4 * P], a["awt"][:, 0:4 * P]),
                     (awv[:], a["awt"][:, 4 * P:5 * P]), (awo[:], a["awo"]), (ltab[:], a["ltab"])]
            for dst, src in loads:
                sp.dma_start(dst, src).then_inc(const_in, 16)

            def load_layer(L):
                sp.dma_start(raw[:], a["wqkv"][L]).then_inc(layer_in, 16)
                sp.dma_start(wo[:], a["wo"][L].rearrange("(c p) n -> p c n", p=P)).then_inc(layer_in, 16)
                sp.dma_start(raw1[:], a["w1"][L]).then_inc(layer_in, 16)
                for c, (u, n) in enumerate(PARTS):
                    sp.dma_start(w2[0:n, c, :], a["w2"][L, u:u + n, :]).then_inc(layer_in, 16)
                sp.dma_start(vecs[:], a["vecs"][L]).then_inc(layer_in, 16)
                sp.dma_start(b1[:], a["b1"][L]).then_inc(layer_in, 16)
                sp.dma_start(scales[:], a["scales"][L]).then_inc(layer_in, 16)

            def held(value):
                return value if isinstance(value, int) else sp.snap(value)

            def copy_shifted(xs, j, width, done):
                per = SEQ // width
                col, src, done = held((j // per) * ROW + (j % per) * width), held(j * width), held(done)
                late = held(col + 1)
                sp.wait_ge(x_new, done)
                sp.dma_start(xs[0:64, bass.ds(col, width)], X[0:64, bass.ds(src, width)]).then_inc(xs_dma, 16)
                sp.dma_start(xs[64:P, bass.ds(late, width)], X[64:P, bass.ds(src, width)]).then_inc(xs_dma, 16)

            with sp.Fori(0, CHUNKS) as j:
                copy_shifted(XS[0], j, CHUNK, j + 1)
            for L in range(DEPTH):
                if L == 0:
                    sp.wait_ge(prep_done, 1)
                else:
                    sp.wait_ge(x_new, x_before_local(L))
                load_layer(L)

                def back(n, par):
                    nxt = 1 - par
                    base = L * TILES
                    turned, done = held(2 * (base + n + 1)), held(base + n + 1)
                    scored, pv1 = held(2 * (base + n)), held(base + n)
                    if live(n, 0, TILES):
                        sp.wait_ge(l_tre, turned)
                        wait(sp, l_score, scored)
                        sp.dma_start(kT[:, nxt, :, 0:WIN], kT[:, par, :, P:P + WIN]).then_inc(k_prev[nxt], 16)
                        sp.wait_ge(l_ve, done)
                        sp.dma_start(VB[64:P, par, :], V[0:64, par, :]).then_inc(v_prev[par], 16)
                        wait(sp, l_o, pv1)
                        sp.dma_start(VB[0:64, nxt, :], V[64:P, par, :]).then_inc(v_prev[nxt], 16)
                    if live(n, -2, TILES):
                        copy_shifted(XS[1], n - 2, P, x_before_local(L) + n - 1)

                if L == 0:
                    sp.wait_ge(zeros_made, 2)
                    sp.wait_ge(windows_zero, 1)
                    sp.dma_start(kT[:, 0, :, 0:WIN], kT[:, 1, :, P:P + WIN]).then_inc(k_prev[0], 16)
                    sp.dma_start(VB[0:64, 0, :], V[64:P, 1, :]).then_inc(v_prev[0], 16)
                steps(sp, 0, 2, TILES, TILES + 1, back)
                if L + 1 < DEPTH:
                    with sp.Fori(0, CHUNKS) as j:
                        copy_shifted(XS[0], j, CHUNK, x_before_ffn(L) + 1 + j)

            def gate(j, par):
                used, made, now, before = held(j - 1), held(j), held(j * CHUNK), held((j - 1) * CHUNK)
                if live(j, 0, CHUNKS):
                    wait(sp, gate_out, used)
                    sp.dma_start(io[:, par, :], a["xT"][:, bass.ds(now, CHUNK)]).then_inc(gate_x[par], 16)
                if live(j, -1, CHUNKS):
                    sp.wait_ge(gate_out, made)
                    sp.dma_start(out[:, bass.ds(before, CHUNK)], sq[:, 1 - par, :]).then_inc(stored[1 - par], 16)

            sp.wait_ge(x_new, x_before_local(DEPTH))
            steps(sp, 0, 2, CHUNKS, CHUNKS, gate)
            sp.wait_ge(k_prev[0], 16 * (TILES * DEPTH // 2 + 1))
            sp.wait_ge(v_prev[0], 32 * TILES * DEPTH // 2 + 16)
            for s in stored:
                sp.wait_ge(s, 16 * CHUNKS // 2)

        @block.tensor
        def _(pe):
            def mm(o, l, r, start=True, stop=True):
                return nc.tensor.matmul(o, l, r, start=start, stop=stop, skip_group_check=True)

            def mm3(o, l_hi, l_lo, r_hi, r_lo):
                mm(o, l_hi, r_hi, True, False)
                mm(o, l_hi, r_lo, False, False)
                return mm(o, l_lo, r_hi, False, True)

            def turn(o, i):
                return nc.tensor.matmul(o, i, ident[:], is_transpose=True, start=True, stop=True,
                                        skip_group_check=True)

            def norm_stats(r):
                base = r * CHUNKS
                def pair(it):
                    for u in range(2):
                        j = it * 2 + u
                        pe.wait_ge(ln_split, base + j + 1)
                        mm(ps[:, u, :], mean_w[:], split[:, u, 0, :], True, False)
                        mm(ps[:, u, :], mean_w[:], split[:, u, 1, :], False, True).then_inc(ln_mean, 1)
                    for u in range(2):
                        j = it * 2 + u
                        pe.wait_ge(ln_squared, base + j + 1)
                        for k in range(4):
                            last = mm(ps[:, 2, bass.ds(j * 4 + k, 1)], sq[:, u, k * P:(k + 1) * P], mean_c[:])
                        last.then_inc(ln_var, 1)

                pairs(pe, CHUNKS // 2, pair)

            def norm_bcast(n, par, base, bank, used, used_base):
                pe.wait_ge(ln_diag, base + n + 1)
                wait(pe, used, used_base + n)
                mm(ps[:, bank, :], ones[:], diag[:, par, :]).then_inc(ln_bcast, 1)

            pe.wait_ge(const_made, 1)
            norm_stats(0)
            pe.wait_ge(ln_rstd, NEWTON)
            def pair(it):
                for u in range(2):
                    norm_bcast(it * 2 + u, u, 0, 3, x_new, 0)

            pairs(pe, CHUNKS // 2, pair)

            def a_project(j, par):
                pe.wait_ge(a_split, j + 1)
                for c in range(4):
                    wait(pe, a_tab, 4 * j + c - 3)
                    mm3(ps[:, c, :], awt[:, 0, c * P:(c + 1) * P], awt[:, 1, c * P:(c + 1) * P],
                        split[:, par, 0, :], split[:, par, 1, :]).then_inc(a_qk_mm, 1)

            pe.wait_ge(const_in, 16 * N_CONST)
            pe.wait_ge(vones_made, 1)
            pe.wait_ge(prep_done, 1)
            steps(pe, 0, 2, CHUNKS, CHUNKS - 1, a_project)

            def a_tile(n, par):
                nxt = 1 - par
                if live(n, 1, TILES):
                    pe.wait_ge(a_stat, n + 2)
                    pe.wait_ge(a_kexp, n + 2)
                    wait(pe, a_sub, n + 1)
                    for g in range(GROUPS):
                        mm(ps[:, g, 0:P], ident_bf[:], amask[:], True, False)
                    for g in range(GROUPS):
                        for b in range(BLKS):
                            last = mm(ps[32 * b:32 * b + 32, g, 0:P],
                                      qst[32 * g:32 * g + 32, nxt, 32 * b:32 * b + 32],
                                      kexp[32 * g:32 * g + 32, nxt, P * b:P * b + P], False, True)
                    last.then_inc(a_score, 1)
                if live(n, -1, TILES):
                    pe.wait_ge(a_on, n)
                    wait(pe, a_done, n - 1)
                    turn(ps[:, 7, 0:P], oA[:, nxt, :]).then_inc(a_oT, 1)
                if live(n, 0, TILES):
                    pe.wait_ge(a_exp, n + 1)
                    wait(pe, a_pTe, n)
                    for g in range(GROUPS):
                        last = turn(ps[:, 5, g * P:(g + 1) * P], pA[:, par, g * P:(g + 1) * P])
                    last.then_inc(a_pT, 1)
                if live(n, 1, TILES):
                    wait(pe, a_vexp, n + 1)
                    for b in range(BLKS):
                        last = mm(ps[:, 4, P * b:P * b + P], xst[:, nxt, b, :], awv[:])
                    last.then_inc(a_v, 1)
                if live(n, -1, TILES):
                    pe.wait_ge(a_oTe, n)
                    mm(ps[:, 7, 0:P], awo[:], oAT[:, nxt, :]).then_inc(a_s, 1)
                if live(n, 0, TILES):
                    pe.wait_ge(a_pTe, n + 1)
                    pe.wait_ge(a_vexp, n + 1)
                    wait(pe, a_on, n)
                    ve = vexp[:, par, :].rearrange("p (b g c) -> p b g c", b=BLKS, g=GROUPS)
                    for g in range(GROUPS):
                        for b in range(BLKS):
                            last = mm(ps[32 * b:32 * b + 32, 6, g * 4 * VW:(g + 1) * 4 * VW],
                                      pT[:, par, g * P + 32 * b:g * P + 32 * b + 32], ve[:, b, g, :])
                    last.then_inc(a_o, 1)

            steps(pe, -1, 3, TILES - 1, TILES, a_tile)

            for L in range(DEPTH):
                pe.wait_ge(layer_in, 16 * N_LAYER * (L + 1))
                if L == 0:
                    pe.wait_ge(a_done, TILES)
                for c in range(2 * NPART):
                    u, n = PARTS[c % NPART]
                    u += (c // NPART) * HID
                    last = mm(ps[0:n, 7, c:c + 1], raw1[:, u:u + n], vecs[:, 1:2])
                last.then_inc(bias_mm, 1)
                pe.wait_ge(prep_done, 2 + L)

                base = L * TILES

                def project(c, hi, lo, made):
                    mm3(ps[:, c, :], hi, lo, wqkv[:, 0, c * INNER:(c + 1) * INNER],
                        wqkv[:, 1, c * INNER:(c + 1) * INNER]).then_inc(made, 1)

                def transposed(n, par, src, ready):
                    pe.wait_ge(ready, base + n + 1)
                    for c in range(4):
                        last = turn(ps[:, 3, c * P:(c + 1) * P], src[:, par, c * P:(c + 1) * P])
                    last.then_inc(l_tr, 1)

                def local(n, par):
                    nxt = 1 - par
                    now, ahead = [(split[:, i, 0, 0:P], split[:, i, 1, 0:P]) for i in (par, nxt)]
                    if live(n, 0, TILES):
                        wait(pe, x_new, (x_before_local(L) + n - 2) if not isinstance(n, int) or n > 2 else 0)
                        transposed(n, par, qr, l_qr)
                    if live(n, 2, TILES):
                        pe.wait_ge(l_split, base + n + 3)
                        wait(pe, l_qm, base + n + 2)
                        project(0, *now, l_qk)
                    if live(n, 0, TILES):
                        pe.wait_ge(l_tre, 2 * (base + n) + 1)
                        transposed(n, par, kr, l_kr)
                    if live(n, 2, TILES):
                        wait(pe, l_kn, base + n + 2)
                        project(1, *now, l_qk)

                    def scores(grp):
                        if live(n, 0, TILES):
                            if grp == 0:
                                pe.wait_ge(l_tre, 2 * (base + n + 1))
                                pe.wait_ge(k_prev[par], 16 * ((base + n) // 2 + 1))
                            wait(pe, l_exp, 8 * (base + n - 1) + 4 * grp + 4)
                            first = 1 if par else live_mask(n)
                            mm(ps[:, 4 + grp, :], ident_bf[:], lmask[:, bass.ds(first * CHUNK, CHUNK)], True, False)
                            r = slice(64 * grp, 64 * grp + 64)
                            for s in range(4):
                                for w in range(2):
                                    last = mm(ps[64 * w:64 * w + 64, 4 + grp, s * P:(s + 1) * P],
                                              qT[r, par, s, 64 * w:64 * w + 64],
                                              kT[r, par, s, 64 * w:64 * w + P], False, True)
                            last.then_inc(l_score, 1)

                    def turned_probs(grp):
                        if live(n, -1, TILES):
                            pe.wait_ge(l_prob, 2 * (base + n - 1) + grp + 1)
                            wait(pe, l_pTe, 2 * (base + n - 1) + grp)
                            for s in range(4):
                                last = turn(ps[:, 6, s * P:(s + 1) * P], prob[:, nxt, grp, s * P:(s + 1) * P])
                            last.then_inc(l_pT, 1)

                    scores(0)
                    turned_probs(0)
                    if live(n, 1, TILES):
                        wait(pe, l_ve, base + n + 1)
                        project(2, *ahead, l_v)
                    turned_probs(1)
                    scores(1)
                    if live(n, -2, TILES):
                        if not live(n, 0, TILES):
                            pe.wait_ge(x_new, x_before_local(L) + n - 2)
                        pe.wait_ge(l_oe, base + n - 1)
                        if live(n, 0, TILES):
                            pe.wait_ge(l_tre, 2 * (base + n + 1))
                        for c in range(4):
                            last = mm(ps[:, 3, 0:P], wo[:, c, :], oT[:, par, c * P:(c + 1) * P], c == 0, c == 3)
                        last.then_inc(l_y, 1)
                    if live(n, -1, TILES):
                        wait(pe, l_oe, base + n - 1)
                        m = base + n - 1
                        pe.wait_ge(l_pTe, 2 * m + 2)
                        pe.wait_ge(l_ve, m + 1)
                        pe.wait_ge(v_prev[nxt], 32 * (m // 2 + 1))
                        for s in range(4):
                            for w in range(2):
                                for grp in range(2):
                                    h = 2 * s + grp
                                    vv = (V if w else VB)[:, nxt, h * HD:(h + 1) * HD]
                                    last = mm(ps[64 * grp:64 * grp + 64, 7, s * P + 64 * w:s * P + 64 * w + 64],
                                              vv, pT[:, grp, s * P + 64 * w:s * P + 64 * w + 64])
                        last.then_inc(l_o, 1)

                def live_mask(n):
                    if isinstance(n, int):
                        return min(n % TPB, 1)
                    k = n % TPB
                    return ((k + TPB - 1) // TPB)

                steps(pe, -2, 2, TILES - 2, TILES + 1, local)

                norm_stats(1 + L)
                pe.wait_ge(ln_rstd, NEWTON * (2 + L))
                fb = L * CHUNKS

                def ffn(j, par):
                    if live(j, 1, CHUNKS):
                        norm_bcast(j + 1, 1 - par, (1 + L) * CHUNKS, 0, ln_scaled, fb)
                    if live(j, 0, CHUNKS):
                        pe.wait_ge(ffn_lo, fb + j + 1)
                        for c, (u, n) in enumerate(PARTS):
                            for side, off in ((0, HID), (1, 0)):
                                if side == 0:
                                    wait(pe, ffn_gelu, NPART * (fb + j - 1) + c + 1)
                                else:
                                    wait(pe, ffn_hid, NPART * (fb + j - 1) + c + 1)
                                w = slice(off + u, off + u + n)
                                mm3(ps[0:n, 2 + 2 * c + side, :], w1[:, 0, w], w1[:, 1, w], split[:, par, 0, :],
                                    split[:, par, 1, :]).then_inc(ffn_a if side else ffn_g, 1)
                    if live(j, 0, CHUNKS):
                        wait(pe, x_new, (x_before_ffn(L) + j) if not isinstance(j, int) or j else 0)
                        for c, (u, n) in enumerate(PARTS):
                            pe.wait_ge(ffn_hid, NPART * (fb + j) + c + 1)
                            last = mm(ps[:, 1, :], w2[0:n, c, :], hid[0:n, c, :], c == 0, c == NPART - 1)
                        last.then_inc(ffn_y, 1)

                steps(pe, -1, 1, CHUNKS - 1, CHUNKS - 1, ffn)

        @block.scalar
        def _(act):
            def norm_stats(r):
                base = r * CHUNKS
                def pair(it):
                    for u in range(2):
                        j = it * 2 + u
                        act.wait_ge(ln_centred, base + j + 1)
                        wait(act, ln_var, base + it * 2)
                        nc.scalar.activation(sq[:, u, :], part(D, j, CHUNK), ACT.Square).then_inc(ln_squared, 1)

                pairs(act, CHUNKS // 2, pair)

            norm_stats(0)

            def a_tile(n, par):
                nxt = 1 - par
                if live(n, 2, TILES):
                    wait(act, a_score, n + 1)
                    wait(act, a_v, n + 1)
                    nc.scalar.activation(qst[:, par, :], part(qA, n + 2, P), ACT.Copy)
                    nc.scalar.activation(xst[:, par].rearrange("p b (r t) -> p b r t", r=INGRP),
                                         part(X, n + 2, P).rearrange("p (b t) -> p b t", b=BLKS).unsqueeze(2)
                                         .broadcast_to([P, BLKS, INGRP, ABLK]), ACT.Copy).then_inc(a_stat, 1)
                if live(n, -1, TILES):
                    act.wait_ge(a_oT, n)
                    nc.scalar.activation(oAT[:, nxt, :], ps[:, 7, 0:P], ACT.Copy).then_inc(a_oTe, 1)
                if live(n, 0, TILES):
                    act.wait_ge(a_pT, n + 1)
                    wait(act, a_o, n - 1)
                    nc.scalar.activation(pT[:, par, :], ps[:, 5, :], ACT.Copy).then_inc(a_pTe, 1)
                if live(n, 1, TILES):
                    act.wait_ge(a_sub, n + 2)
                    nc.scalar.activation(pA[:, nxt, :], pA[:, nxt, :], ACT.Exp,
                                         scale=float(AHD) ** -0.5).then_inc(a_exp, 1)
                if live(n, -1, TILES):
                    act.wait_ge(a_s, n)
                    nc.scalar.activation(part(A_OUT, n - 1, P), ps[:, 7, 0:P], ACT.Copy).then_inc(a_done, 1)

            act.wait_ge(a_rot, 2 * CHUNKS)
            steps(act, -2, 2, TILES - 2, TILES, a_tile)

            for L in range(DEPTH):
                base = L * TILES

                def local(n, par):
                    nxt = 1 - par

                    def square(c):
                        act.wait_ge(l_qk, 2 * (base + n + 2) + c + 1)
                        wait(act, l_norm, base + n + 2)
                        nc.scalar.activation(sq[:, c, :], ps[:, c, :], ACT.Square).then_inc(l_sq, 1)

                    if live(n, 0, TILES):
                        act.wait_ge(l_tr, 2 * (base + n) + 1)
                        nc.scalar.activation(qT[:, par, :, :], ps[:, 3, :].rearrange("p (c t) -> p c t", c=4),
                                             ACT.Copy).then_inc(l_tre, 1)
                        act.wait_ge(l_v, base + n + 1)
                        wait(act, l_o, base + n - 1)
                        if live(n, -1, TILES):
                            act.wait_ge(v_prev[nxt], 32 * ((base + n - 1) // 2 + 1))
                        nc.scalar.activation(V[:, par, :], ps[:, 2, :], ACT.Copy).then_inc(l_ve, 1)
                    if live(n, 2, TILES):
                        square(0)
                    if live(n, 0, TILES):
                        act.wait_ge(l_tr, 2 * (base + n) + 2)
                        nc.scalar.activation(kT[:, par, :, WIN:WIN + P], ps[:, 3, :].rearrange("p (c t) -> p c t", c=4),
                                             ACT.Copy).then_inc(l_tre, 1)
                    if live(n, 2, TILES):
                        square(1)
                    if live(n, -2, TILES):
                        act.wait_ge(l_o, base + n - 1)
                        wait(act, l_y, base + n - 3)
                        nc.scalar.activation(oT[:, par, :], ps[:, 7, :], ACT.Copy).then_inc(l_oe, 1)
                    if live(n, -1, TILES):
                        wait(act, l_o, base + n - 1)
                        for grp in range(2):
                            act.wait_ge(l_pT, 2 * (base + n - 1) + grp + 1)
                            nc.scalar.activation(pT[:, grp, :], ps[:, 6, :], ACT.Copy).then_inc(l_pTe, 1)
                    if live(n, 0, TILES):
                        for grp in range(2):
                            act.wait_ge(l_bias, 2 * (base + n) + grp + 1)
                            for s in range(4):
                                h = 2 * s + grp
                                nc.scalar.activation(prob[:, par, grp, s * P:(s + 1) * P],
                                                     ps[:, 4 + grp, s * P:(s + 1) * P], ACT.Exp,
                                                     bias=ebias[:, par, grp * 4 + s:grp * 4 + s + 1],
                                                     scale=ss[:, par, h:h + 1],
                                                     accum_out=rsum[:, par, grp * 4 + s:grp * 4 + s + 1]).then_inc(l_exp, 1)

                steps(act, -2, 4, TILES - 2, TILES + 1, local)

                norm_stats(1 + L)
                fb = L * CHUNKS

                def ffn(j, par):
                    if live(j, 1, CHUNKS):
                        act.wait_ge(ln_scaled, fb + j + 2)
                        wait(act, ffn_a, NPART * (fb + j))
                        nc.scalar.activation(split[:, 1 - par, 0, :], tA[:], ACT.Copy).then_inc(ffn_hi, 1)
                    if live(j, 0, CHUNKS):
                        for c, (u, n) in enumerate(PARTS):
                            act.wait_ge(ffn_g, NPART * (fb + j) + c + 1)
                            wait(act, ffn_hid, NPART * (fb + j - 1) + c + 1)
                            nc.scalar.activation(gel[0:n, c, :], ps[0:n, 2 + 2 * c, :], ACT.Gelu,
                                                 bias=bias1[0:n, NPART + c:NPART + c + 1]).then_inc(ffn_gelu, 1)

                act.wait_ge(prep_done, 2 + L)
                steps(act, -1, 1, CHUNKS - 1, CHUNKS - 1, ffn)

            act.wait_ge(x_new, x_before_local(DEPTH))
            def pair(it):
                for u in range(2):
                    j = it * 2 + u
                    wait(act, gate_mul, it * 2)
                    nc.scalar.activation(diag[:, u, :], part(X, j, CHUNK), ACT.Silu).then_inc(gate_silu, 1)

            pairs(act, CHUNKS // 2, pair)

        @block.vector
        def _(dve):
            v = nc.vector

            def rsqrt(s, t, sem, uses, s_in, low=None):
                links = [0]

                def link(ins):
                    links[0] += 1
                    ins.then_inc(sem, 1)
                    dve.wait_ge(sem, uses * NEWTON + links[0])

                if low is None:
                    link(v.tensor_scalar(s, s_in, EPS, None, ALU.add))
                else:
                    link(v.tensor_scalar(s, s_in, low, None, ALU.max))
                link(v.tensor_scalar(t.bitcast(I32), s.bitcast(I32), 1, None, ALU.logical_shift_right))
                link(v.tensor_scalar(t.bitcast(I32), t.bitcast(I32), -1.0, MAGIC, ALU.mult, ALU.add))
                y, u = t, newt_u(s)
                for k in range(3):
                    link(v.tensor_tensor(u, s, y, ALU.mult))
                    link(v.scalar_tensor_tensor(u, u, -0.5, y, ALU.mult, ALU.mult))
                    link(v.scalar_tensor_tensor(s if k == 2 else y, u, 1.5, y, ALU.add, ALU.mult))
                assert links[0] == NEWTON

            def newt_u(s):
                return newt[:, 1, 0:s.shape[1]]

            def split_into(slot, src, width, made, value):
                hi, lo = split[:, slot, 0, 0:width], split[:, slot, 1, 0:width]
                v.tensor_copy(hi, src).then_inc(split_hi, 1)
                dve.wait_ge(split_hi, value + 1)
                v.tensor_tensor(lo, src, hi.bitcast(F32), ALU.subtract).then_inc(made, 1)

            def norm_stats(r, src):
                base = r * CHUNKS
                def pair(it):
                    for u in range(2):
                        j = it * 2 + u
                        split_into(u, src(j), CHUNK, ln_split, SPLITS_BEFORE[r] + j)
                    for u in range(2):
                        j = it * 2 + u
                        dve.wait_ge(ln_mean, base + j + 1)
                        v.tensor_tensor(part(D, j, CHUNK), src(j), ps[:, u, :], ALU.subtract).then_inc(ln_centred, 1)

                pairs(dve, CHUNKS // 2, pair)
                dve.wait_ge(ln_var, base + CHUNKS)
                rsqrt(rstd[:], newt[:, 0, :], ln_rstd, r, ps[:, 2, 0:TILES])

            def norm_diag(j, slot, used):
                wait(dve, ln_bcast, used)
                v.tensor_tensor(diag[:, slot, :].rearrange("p (k t) -> p k t", k=4),
                                ident[:].unsqueeze(1).broadcast_to([P, 4, P]),
                                rstd[:, bass.ds(j * 4, 4)].unsqueeze(2).broadcast_to([P, 4, P]),
                                ALU.mult).then_inc(ln_diag, 1)

            dve.wait_ge(ones_made, 1)
            v.tensor_scalar(mean_c[:], ones[:, 0:1], 1.0 / DIM, None, ALU.mult)
            v.tensor_scalar(mean_w[:], ones[:], 1.0 / DIM, None, ALU.mult).then_inc(const_made, 1)

            def clear_first(xs):
                for b in range(BATCH):
                    last = v.memset(xs[64:P, b * ROW:b * ROW + 1], 0.0)
                last.then_inc(zeros_made, 1)

            clear_first(XS[0])

            dve.wait_ge(lnx_in, 16 * CHUNKS)
            norm_stats(0, lambda j: part(D, j, CHUNK))
            dve.wait_ge(const_in, 16 * N_CONST)
            def pair(it):
                for u in range(2):
                    j = it * 2 + u
                    norm_diag(j, u, it * 2)
                    dve.wait_ge(ln_bcast, j + 1)
                    v.tensor_tensor(part(X, j, CHUNK), part(D, j, CHUNK), ps[:, 3, :], ALU.mult).then_inc(x_new, 1)

            pairs(dve, CHUNKS // 2, pair)

            v.tensor_copy(ident_bf[:], ident[:])
            v.tensor_copy(lmask[:], mask_in[:, 0:2 * CHUNK])
            v.tensor_copy(amask[:], mask_in[:, 2 * CHUNK:2 * CHUNK + P])
            v.tensor_copy(awt[:, 0, :], raw[:, 0:4 * P]).then_inc(prep_hi, 1)
            dve.wait_ge(prep_hi, 1)
            v.tensor_tensor(awt[:, 1, :], raw[:, 0:4 * P], awt[:, 0, :].bitcast(F32), ALU.subtract).then_inc(prep_done, 1)
            dve.wait_ge(x_new, CHUNKS)

            def a_project(j, par):
                if live(j, 1, CHUNKS):
                    wait(dve, a_qk_mm, 4 * j)
                    split_into(1 - par, part(X, j + 1, CHUNK), CHUNK, a_split, SPLITS_BEFORE_A + j + 1)
                if live(j, 0, CHUNKS):
                    for c, t in enumerate((tA, tB, kA, kB)):
                        dve.wait_ge(a_qk_mm, 4 * j + c + 1)
                        wait(dve, a_rot, 2 * j + (c // 2) - 1)
                        v.tensor_tensor(t[:], ps[:, c, :], arot[:, c % 2, bass.ds((j % CPB) * CHUNK, CHUNK)],
                                        ALU.mult).then_inc(a_tab, 1)

            steps(dve, -1, 1, CHUNKS - 1, CHUNKS - 1, a_project)

            def a_tile(n, par):
                nxt = 1 - par
                if live(n, 1, TILES):
                    dve.wait_ge(a_score, n + 2)
                    sc = ps[:, 0:4, 0:P].rearrange("p g (h k) -> p g h k", h=INGRP)
                    v.tensor_reduce(amax[:, nxt, :], sc, AX_X, ALU.max).then_inc(a_max, 1)
                    dve.wait_ge(a_max, n + 2)
                    wait(dve, a_pT, n)
                    v.tensor_tensor(pA[:, nxt, :].rearrange("p (g h k) -> p g h k", g=GROUPS, h=INGRP), sc,
                                    amax[:, nxt, :].rearrange("p (g h) -> p g h", g=GROUPS).unsqueeze(3)
                                    .broadcast_to([P, GROUPS, INGRP, ABLK]), ALU.subtract).then_inc(a_sub, 1)
                    dve.wait_ge(a_v, n + 2)
                    wait(dve, a_o, n)
                    v.tensor_tensor(vexp[:, nxt, :].rearrange("p (b h c) -> p b h c", h=INGRP, c=VW)[:, :, :, 0:AHD],
                                    ps[:, 4, :].rearrange("p (b h c) -> p b h c", h=INGRP, c=AHD),
                                    pmask[:].unsqueeze(1).unsqueeze(3).broadcast_to([P, BLKS * GROUPS, INGRP, AHD]),
                                    ALU.mult).then_inc(a_vexp, 1)
                if live(n, 0, TILES):
                    dve.wait_ge(a_o, n + 1)
                    o = ps[:, 6, 0:AH * VW].rearrange("p (h c) -> p h c", h=AH)
                    v.reciprocal(rinvA[:, par, :], o[:, :, AHD]).then_inc(a_rinv, 1)
                    dve.wait_ge(a_rinv, n + 1)
                    wait(dve, a_oT, n - 1)
                    v.tensor_tensor(oA[:, par, :].rearrange("p (h c) -> p h c", h=AH), o[:, :, 0:AHD],
                                    rinvA[:, par, :].unsqueeze(2).broadcast_to([P, AH, AHD]), ALU.mult).then_inc(a_on, 1)

            steps(dve, -1, 3, TILES - 1, TILES - 1, a_tile)

            dve.wait_ge(a_done, TILES)
            clear_first(XS[1])

            for L in range(DEPTH):
                dve.wait_ge(layer_in, 16 * N_LAYER * (L + 1))
                v.tensor_copy(wqkv[:, 0, :], raw[:])
                v.tensor_scalar(w1[:, 0, :], raw1[:], vecs[:, 0:1], None, ALU.mult).then_inc(prep_hi, 1)
                for i in range(2):
                    sc = scales[:, i, :].unsqueeze(1).broadcast_to([P, TPB, HD])
                    tab, rot = [t.rearrange("p i (n d) -> p i n d", d=HD) for t in (ltab, lrot)]
                    v.tensor_tensor(rot[:, 2 * i], tab[:, 2 * i], sc, ALU.mult)
                    for half in range(2):
                        d, o = slice(32 * half, 32 * half + 32), slice(32 - 32 * half, 64 - 32 * half)
                        last = v.tensor_tensor(rot[:, 2 * i + 1, :, d], tab[:, 2 * i + 1, :, d], sc[:, :, o], ALU.mult)
                dve.wait_ge(prep_hi, 2 + L)
                v.tensor_tensor(wqkv[:, 1, :], raw[:], wqkv[:, 0, :].bitcast(F32), ALU.subtract)
                v.scalar_tensor_tensor(w1[:, 1, :], raw1[:], vecs[:, 0:1], w1[:, 0, :].bitcast(F32), ALU.mult, ALU.subtract)
                dve.wait_ge(bias_mm, 1 + L)
                n_last = PARTS[-1][1]
                full = lambda t: t.rearrange("p (s c) -> p s c", s=2)[:, :, 0:NPART - 1]
                rest = lambda t: t.rearrange("p (s c) -> p s c", s=2)[0:n_last, :, NPART - 1:NPART]
                v.tensor_tensor(full(bias1[:]), full(ps[:, 7, 0:2 * NPART]), full(b1[:]), ALU.add)
                v.tensor_tensor(rest(bias1[:]), rest(ps[:, 7, 0:2 * NPART]), rest(b1[:]), ALU.add).then_inc(prep_done, 1)
                dve.wait_ge(prep_done, 2 + L)
                dve.wait_ge(xs_dma, xs_before_local(L))
                base = L * TILES

                def link(m, k, slot=0):
                    y, s, u = nt[:, 0, :], nt[:, 1, :], newt[:, 1, 0:2 * HEADS]
                    if k == 1:
                        dve.wait_ge(l_norm, base + m + 1)
                        ins = v.tensor_scalar(s, s, 1e-24, None, ALU.max)
                    else:
                        dve.wait_ge(l_newton, (base + m) * NEWTON + k - 1)
                    if k == 2:
                        ins = v.tensor_scalar(y.bitcast(I32), s.bitcast(I32), 1, None, ALU.logical_shift_right)
                    elif k == 3:
                        ins = v.tensor_scalar(y.bitcast(I32), y.bitcast(I32), -1.0, MAGIC, ALU.mult, ALU.add)
                    elif k > 3 and k % 3 == 1:
                        ins = v.tensor_tensor(u, s, y, ALU.mult)
                    elif k > 3 and k % 3 == 2:
                        ins = v.scalar_tensor_tensor(u, u, -0.5, y, ALU.mult, ALU.mult)
                    elif k > 3:
                        ins = v.scalar_tensor_tensor(ss[:, slot, :] if k == NEWTON else y, u, 1.5, y, ALU.add, ALU.mult)
                    ins.then_inc(l_newton, 1)

                def local(n, par):
                    nxt = 1 - par

                    def links(first, last):
                        if live(n, 2, TILES):
                            for k in range(first, last + 1):
                                link(n + 2, k)

                    def maxima(grp):
                        if live(n, 0, TILES):
                            dve.wait_ge(l_score, 2 * (base + n) + grp + 1)
                            v.tensor_reduce(nmax[:, par, 4 * grp:4 * grp + 4],
                                            ps[:, 4 + grp, :].rearrange("p (s k) -> p s k", s=4),
                                            AX_X, ALU.max, negate=True).then_inc(l_max, 1)

                    def bias(grp):
                        if live(n, 0, TILES):
                            dve.wait_ge(l_max, 2 * (base + n) + grp + 1)
                            g4 = slice(4 * grp, 4 * grp + 4)
                            v.tensor_tensor(ebias[:, par, g4], nmax[:, par, g4], ss[:, par, grp:8:2],
                                            ALU.mult).then_inc(l_bias, 1)

                    wait(dve, l_exp, 8 * (base + n) if live(n, -1, TILES) or live(n, 1, TILES) else 0)
                    if live(n, -1, TILES):
                        v.reciprocal(rinv[:, nxt, 4:8], rsum[:, nxt, 4:8]).then_inc(l_rinv, 1)
                    if live(n, 1, TILES):
                        link(n + 1, NEWTON, nxt)
                        wait(dve, l_km, base + n + 1)
                        dve.wait_ge(l_newton, (base + n + 2) * NEWTON)
                        v.tensor_tensor(hd(kn[:]), hd(ps[:, 1, :]),
                                        ss[:, nxt, 8:16].unsqueeze(2).broadcast_to([P, HEADS, HD]),
                                        ALU.mult).then_inc(l_kn, 1)
                    if live(n, 2, TILES):
                        pos = ((n + 2) % TPB) * HD
                        dve.wait_ge(l_sq, 2 * (base + n + 2) + 1)
                        wait(dve, l_qr, base + n + 2)
                        v.tensor_tensor(hd(tA[:]), hd(ps[:, 0, :]), row8(0, pos, 0, HD), ALU.mult)
                        v.tensor_tensor(hd(tB[:])[:, :, 0:32], hd(ps[:, 0, :])[:, :, 32:64], row8(1, pos, 0, 32), ALU.mult)
                        v.tensor_tensor(hd(tB[:])[:, :, 32:64], hd(ps[:, 0, :])[:, :, 0:32], row8(1, pos, 32, 32),
                                        ALU.mult).then_inc(l_qm, 1)
                        v.tensor_reduce(nt[:, 1, 0:8], hd(sq[:, 0, :]), AX_X, ALU.add)
                        dve.wait_ge(l_sq, 2 * (base + n + 2) + 2)
                        v.tensor_reduce(nt[:, 1, 8:16], hd(sq[:, 1, :]), AX_X, ALU.add).then_inc(l_norm, 1)
                    maxima(0)
                    links(1, 1)
                    bias(0)
                    if live(n, 3, TILES):
                        wait(dve, l_v, base + n + 2)
                        split_into(nxt, shifted(XS[0], n + 3, P), P, l_split, SPLITS_BEFORE_L[L] + n + 3)
                    links(2, 3)
                    maxima(1)
                    links(4, 4)
                    bias(1)
                    if live(n, 2, TILES):
                        wait(dve, l_tr, 2 * (base + n) + 1)
                        dve.wait_ge(l_qm, base + n + 3)
                        v.tensor_tensor(qr[:, par, :], tA[:], tB[:], ALU.add).then_inc(l_qr, 1)
                    links(5, 8)
                    if live(n, -2, TILES):
                        dve.wait_ge(l_y, base + n - 1)
                        x = part(X, n - 2, P)
                        v.tensor_tensor(x, x, ps[:, 3, 0:P], ALU.add).then_inc(x_new, 1)
                    links(9, 9)
                    if live(n, 0, TILES):
                        dve.wait_ge(l_exp, 8 * (base + n) + 4)
                        v.reciprocal(rinv[:, par, 0:4], rsum[:, par, 0:4]).then_inc(l_rinv, 1)
                    links(10, 11)

                def row8(tab, pos, off, width):
                    return lrot[:, tab, bass.ds(pos + off, width)].unsqueeze(1).broadcast_to([P, HEADS, width])

                steps(dve, -3, 2, TILES - 4, TILES + 1, local)

                dve.wait_ge(xs_dma, xs_before_ffn(L))
                norm_stats(1 + L, lambda j: shifted(XS[1], j, CHUNK))
                fb, nb = L * CHUNKS, (1 + L) * CHUNKS

                def ffn(j, par):
                    nxt = 1 - par
                    if live(j, 1, CHUNKS):
                        norm_diag(j + 1, nxt, nb + j)
                        dve.wait_ge(ln_bcast, nb + j + 2)
                        wait(dve, ffn_hi, fb + j + 1)
                        v.tensor_tensor(tA[:], part(D, j + 1, CHUNK), ps[:, 0, :], ALU.mult).then_inc(ln_scaled, 1)
                        dve.wait_ge(ln_scaled, fb + j + 2)
                        dve.wait_ge(ffn_hi, fb + j + 2)
                        v.tensor_tensor(split[:, nxt, 1, :], tA[:], split[:, nxt, 0, :].bitcast(F32),
                                        ALU.subtract).then_inc(ffn_lo, 1)
                    if live(j, 0, CHUNKS):
                        wait(dve, ffn_y, fb + j)
                        for c, (u, n) in enumerate(PARTS):
                            dve.wait_ge(ffn_gelu, NPART * (fb + j) + c + 1)
                            dve.wait_ge(ffn_a, NPART * (fb + j) + c + 1)
                            v.scalar_tensor_tensor(hid[0:n, c, :], ps[0:n, 3 + 2 * c, :], bias1[0:n, c:c + 1],
                                                   gel[0:n, c, :], ALU.add, ALU.mult).then_inc(ffn_hid, 1)
                        dve.wait_ge(ffn_y, fb + j + 1)
                        x = part(X, j, CHUNK)
                        v.scalar_tensor_tensor(x, ps[:, 1, :], vecs[:, 2:3], x, ALU.add, ALU.add).then_inc(x_new, 1)

                steps(dve, -1, 1, CHUNKS - 1, CHUNKS - 1, ffn)

            def pair(it):
                for u in range(2):
                    j = it * 2 + u
                    dve.wait_ge(gate_silu, j + 1)
                    wait(dve, gate_out, it * 2)
                    t = (tA, tB)[u]
                    v.tensor_tensor(t[:], diag[:, u, :], part(A_OUT, j, CHUNK), ALU.mult).then_inc(gate_mul, 1)
                    dve.wait_ge(gate_mul, j + 1)
                    dve.wait_ge(gate_x[u], 16 * (it + 1))
                    wait(dve, stored[u], it * 16)
                    v.tensor_tensor(sq[:, u, :], t[:], io[:, u, :], ALU.add).then_inc(gate_out, 1)

            pairs(dve, CHUNKS // 2, pair)

        @block.gpsimd
        def _(pool):
            g = nc.gpsimd
            g.memset(ones[:], 1.0).then_inc(ones_made, 1)
            g.memset(V[:, 1, :], 0.0)
            g.memset(kT[:, 1, :, P:P + WIN], 0.0).then_inc(windows_zero, 1)
            pool.wait_ge(const_in, 16 * N_CONST)
            for s in range(2):
                last = g.tensor_copy(vexp[:, s, :].rearrange("p (b h c) -> p b h c", h=INGRP, c=VW)[:, :, :, AHD],
                                     pmask[:].unsqueeze(1).broadcast_to([P, BLKS * GROUPS, INGRP]))
            last.then_inc(vones_made, 1)

            def a_project(j, par):
                if live(j, 0, CHUNKS):
                    for i, (dst, s, t) in enumerate(((qA, tA, tB), (kR, kA, kB))):
                        pool.wait_ge(a_tab, 4 * j + 2 * i + 2)
                        g.tensor_tensor(part(dst, j, CHUNK), s[:], t[:], ALU.add).then_inc(a_rot, 1)

            steps(pool, 0, 0, CHUNKS, CHUNKS - 1, a_project)
            pool.wait_ge(a_rot, 2 * CHUNKS)

            def a_tile(n, par):
                if live(n, 0, TILES):
                    wait(pool, a_score, n - 1)
                    g.tensor_tensor(kexp[:, par, :].rearrange("p (b h k) -> p b h k", b=BLKS, h=INGRP),
                                    part(kR, n, P).rearrange("p (b k) -> p b k", b=BLKS).unsqueeze(2)
                                    .broadcast_to([P, BLKS, INGRP, ABLK]),
                                    hmask[:].unsqueeze(1).unsqueeze(3).broadcast_to([P, BLKS, INGRP, ABLK]),
                                    ALU.mult).then_inc(a_kexp, 1)

            steps(pool, 0, 2, TILES, TILES - 1, a_tile)

            for L in range(DEPTH):
                base = L * TILES

                def row8(tab, pos, off, width):
                    return lrot[:, tab, bass.ds(pos + off, width)].unsqueeze(1).broadcast_to([P, HEADS, width])

                def normalise(m, slot, grp):
                    pool.wait_ge(l_rinv, 2 * (base + m) + grp + 1)
                    p4 = prob[:, slot, grp, :].rearrange("p (s k) -> p s k", s=4)
                    g.tensor_tensor(p4, p4, rinv[:, slot, 4 * grp:4 * grp + 4].unsqueeze(2).broadcast_to([P, 4, P]),
                                    ALU.mult).then_inc(l_prob, 1)

                def local(n, par):
                    nxt = 1 - par
                    if live(n, -1, TILES):
                        normalise(n - 1, nxt, 1)
                    if live(n, 1, TILES):
                        pos = ((n + 1) % TPB) * HD
                        pool.wait_ge(l_kn, base + n + 2)
                        wait(pool, l_kr, base + n + 1)
                        g.tensor_tensor(hd(kA[:]), hd(kn[:]), row8(2, pos, 0, HD), ALU.mult)
                        g.tensor_tensor(hd(kB[:])[:, :, 0:32], hd(kn[:])[:, :, 32:64], row8(3, pos, 0, 32), ALU.mult)
                        g.tensor_tensor(hd(kB[:])[:, :, 32:64], hd(kn[:])[:, :, 0:32], row8(3, pos, 32, 32),
                                        ALU.mult).then_inc(l_km, 1)
                        pool.wait_ge(l_km, base + n + 2)
                        wait(pool, l_tr, 2 * (base + n))
                        g.tensor_tensor(kr[:, nxt, :], kA[:], kB[:], ALU.add).then_inc(l_kr, 1)
                    if live(n, 0, TILES):
                        normalise(n, par, 0)

                steps(pool, -1, 2, TILES - 2, TILES, local)


def shape_constants():
    f = np.float32
    c = {}
    c["ident"] = np.eye(P, dtype=f)
    i = np.arange(P) % WIN
    k = np.arange(2 * WIN)
    ok = np.where(k[None] < WIN, k[None] >= i[:, None], k[None] - WIN <= i[:, None])
    first = ok & ~((np.arange(P)[:, None] < WIN) & (k[None] < WIN))
    local = [np.tile(np.where(m, 0, NEG), (1, 4)) for m in (first, ok)]
    i, k = np.arange(P) % ABLK, np.arange(ABLK)
    c["masks"] = np.concatenate(local + [np.tile(np.where(k[None] <= i[:, None], 0, NEG), (1, INGRP))], 1).astype(f)
    p = np.arange(P)
    c["hmask"] = (p[:, None] // AHD % INGRP == np.arange(INGRP)[None]).astype(f)
    c["pmask"] = (p[:, None] // ABLK == np.arange(INGRP)[None]).astype(f)
    inv = (f(1.0) / f(10000.0) ** (np.arange(0, AHD, 2, dtype=f) / f(AHD))).astype(f)
    t = (np.arange(SEQ, dtype=f)[None] * inv[p % (AHD // 2)][:, None]).astype(f)
    sign = np.where(p % AHD < AHD // 2, -1, 1).astype(f)[:, None]
    c["arot"] = np.stack([np.cos(t), np.sin(t) * sign], 1).astype(f)
    half = np.arange(0, HD, 2, dtype=f)
    inv = (f(1.0) / f(10000.0) ** (half / f(HD))).astype(f)
    t = np.arange(SEQ, dtype=f)
    fr = (t[:, None] * inv[None]).astype(f)
    b = ((half + f(0.4 * HD)) / f(1.4 * HD)).astype(f)
    power = ((t - SEQ // 2) / f(WIN // 2)).astype(f)
    sc = (b[None] ** power[:, None]).astype(f)
    two = lambda x: np.concatenate([x, x], -1)
    cos, sin, sc = two(np.cos(fr)), np.concatenate([-np.sin(fr), np.sin(fr)], -1), two(sc)
    tabs = np.stack([cos * sc * 8, sin * sc * 8, cos / sc, sin / sc]).astype(f)
    c["ltab"] = np.ascontiguousarray(tabs.reshape(4, TPB, P, HD).transpose(2, 0, 1, 3).reshape(P, 4, TPB * HD))
    return c


def kernel(L0_attn_x, L0_attn_Wqkv, L0_attn_Wout, L0_ffn_wqkv, L0_ffn_q_scale, L0_ffn_k_scale, L0_ffn_wo,
           L0_ffn_ln_g, L0_ffn_ln_b, L0_ffn_w1, L0_ffn_b1, L0_ffn_w2, L0_ffn_b2):
    import concourse.bacc as bacc
    from concourse.bass_utils import run_bass_kernel_spmd

    con = np.ascontiguousarray
    arrays = dict(shape_constants())
    arrays["xT"] = con(np.asarray(L0_attn_x).reshape(TOKENS, DIM).T)
    w = np.asarray(L0_attn_Wqkv).T
    even = np.concatenate([h * AHD + np.r_[0:AHD:2, 1:AHD:2] for h in range(AH)])
    odd = np.concatenate([h * AHD + np.r_[1:AHD:2, 0:AHD:2] for h in range(AH)])
    q, k, v = w[:, 0:P], w[:, P:2 * P], w[:, 2 * P:3 * P]
    arrays["awt"] = con(np.concatenate([q[:, even], q[:, odd], k[:, even], k[:, odd], v], 1))
    arrays["awo"] = con(np.asarray(L0_attn_Wout).T)
    arrays["wqkv"] = con(L0_ffn_wqkv)
    arrays["wo"] = con(L0_ffn_wo)
    arrays["w1"] = con(L0_ffn_w1)
    arrays["w2"] = con(L0_ffn_w2)
    arrays["vecs"] = con(np.stack([L0_ffn_ln_g, L0_ffn_ln_b, L0_ffn_b2], -1))
    b = np.zeros((DEPTH, 2, NPART * P), np.asarray(L0_ffn_b1).dtype)
    b[:, :, 0:HID] = np.asarray(L0_ffn_b1).reshape(DEPTH, 2, HID)
    arrays["b1"] = con(b.reshape(DEPTH, 2 * NPART, P).transpose(0, 2, 1))
    s = np.stack([L0_ffn_q_scale, L0_ffn_k_scale], 1)
    arrays["scales"] = con(np.broadcast_to(s[:, None], (DEPTH, P, 2, HD)))

    nc = bacc.Bacc("TRN2", target_bir_lowering=False, num_devices=1, dynamic_dma_scratch_size=1024)
    ins = {n: nc.dram_tensor(f"in_{n}", x.shape, mybir.dt.from_np(x.dtype), kind="ExternalInput").ap()
           for n, x in arrays.items()}
    out = nc.dram_tensor("out_T", (DIM, TOKENS), F32, kind="ExternalOutput").ap()
    build(nc, ins, out)
    r = run_bass_kernel_spmd(nc, [{f"in_{n}": x for n, x in arrays.items()}], core_ids=[0])
    return con(r.results[0]["out_T"].T).reshape(BATCH, SEQ, DIM)
```

```python
from contextlib import ExitStack

import numpy as np

import concourse.bass as bass
from concourse import mybir
from concourse.alu_op_type import AluOpType as ALU

ACT = mybir.ActivationFunctionType
AX_X = mybir.AxisListType.X
F32 = mybir.dt.float32
F32R = mybir.dt.float32r
BF16 = mybir.dt.bfloat16
I32 = mybir.dt.int32

P = 128
BATCH, SEQ, DIM = 4, 1024, 128
TOKENS = BATCH * SEQ
TILES = TOKENS // P
TPB = SEQ // P
CHUNK = 512
CHUNKS = TOKENS // CHUNK
CPB = SEQ // CHUNK
TPC = CHUNK // P
ROW = SEQ + 1
DEPTH = 2

HEADS, HD, WIN = 8, 64, 64
INNER = HEADS * HD
HID = int(DIM * 4 * 2 / 3)
PARTS = [(c, min(P, HID - c)) for c in range(0, HID, P)]
NPART = len(PARTS)

AH, AHD, ABLK = 16, 8, 32
GROUPS, INGRP = 4, 4
BLKS = P // ABLK
VW = AHD + 1

NEG = -1e30
EPS = 1e-5
MAGIC = float(0x5F3759DF)


def live(n, k, count):
    return not isinstance(n, int) or 0 <= n + k < count


def wait(eng, sem, value):
    if not isinstance(value, int) or value > 0:
        eng.wait_ge(sem, value)


def steps(eng, first, start, stop, last, step):
    for n in range(first, start):
        step(n, n % 2)
    with eng.Fori(0, (stop - start) // 2) as it:
        for u in range(2):
            step(it * 2 + (start + u), (start + u) % 2)
    for n in range(stop, last + 1):
        step(n, n % 2)


def pairs(eng, count, body):
    body(0)
    with eng.Fori(1, count) as it:
        body(it)


def build(nc, a, out):
    with ExitStack() as ctx:
        def sb(name, shape, dt=F32):
            return ctx.enter_context(nc.sbuf_tensor(name, shape, dt))

        def sem(name):
            return ctx.enter_context(nc.semaphore(name))

        X = sb("X", [P, TOKENS])
        XS = [sb(f"XS{i}", [P, BATCH * ROW]) for i in range(2)]
        D = sb("D", [P, TOKENS])
        A_OUT = sb("A_OUT", [P, TOKENS])
        ident = sb("ident", [P, P])
        ident_bf = sb("ident_bf", [P, P], BF16)
        ones = sb("ones", [P, P])
        mean_w = sb("mean_w", [P, P])
        mean_c = sb("mean_c", [P, 1])
        lmask = sb("lmask", [P, 2 * CHUNK], BF16)
        amask = sb("amask", [P, P], BF16)
        hmask = sb("hmask", [P, INGRP])
        pmask = sb("pmask", [P, INGRP])
        ltab = sb("ltab", [P, 4, TPB * HD])
        lrot = sb("lrot", [P, 4, TPB * HD])
        arot = sb("arot", [P, 2, SEQ])
        raw = sb("raw", [P, 3 * INNER])
        wqkv = sb("wqkv", [P, 2, 3 * INNER], F32R)
        awt = sb("awt", [P, 2, 4 * P], F32R)
        awv = sb("awv", [P, P])
        awo = sb("awo", [P, P])
        wo = sb("wo", [P, INNER // P, DIM])
        raw1 = sb("raw1", [P, 2 * HID])
        w1 = sb("w1", [P, 2, 2 * HID], F32R)
        w2 = sb("w2", [P, NPART, DIM])
        vecs = sb("vecs", [P, 3])
        b1 = sb("b1", [P, 2 * NPART])
        bias1 = sb("bias1", [P, 2 * NPART])
        scales = sb("scales", [P, 2, HD])
        split = sb("split", [P, 2, 2, CHUNK], F32R)
        sq = sb("sq", [P, 2, CHUNK])
        rstd = sb("rstd", [P, TILES])
        newt = sb("newt", [P, 2, TILES])
        tA = sb("tA", [P, CHUNK])
        tB = sb("tB", [P, CHUNK])
        kA = sb("kA", [P, CHUNK])
        kB = sb("kB", [P, CHUNK])
        kn = sb("kn", [P, CHUNK])
        qr = sb("qr", [P, 2, CHUNK])
        kr = sb("kr", [P, 2, CHUNK])
        qT = sb("qT", [P, 2, HEADS // 2, P])
        kT = sb("kT", [P, 2, HEADS // 2, WIN + P])
        V = sb("V", [P, 2, INNER])
        VB = sb("VB", [P, 2, INNER])
        ss = sb("ss", [P, 2, 2 * HEADS])
        nt = sb("nt", [P, 2, 2 * HEADS])
        nmax = sb("nmax", [P, 2, HEADS])
        rsum = sb("rsum", [P, 2, HEADS])
        rinv = sb("rinv", [P, 2, HEADS])
        prob = sb("prob", [P, 2, 2, CHUNK])
        pT = sb("pT", [P, 2, CHUNK])
        oT = sb("oT", [P, 2, CHUNK])
        mask_in = A_OUT[:, 0:2 * CHUNK + P]
        gel = (kA, kB, kn)
        hid = prob[:].rearrange("p a b t -> p (a b) t")
        diag = qr
        x_in = XS[0]
        qA, kR = XS[1], D
        qst, xst = kT[:, :, 0, 0:P], qT
        kexp = prob[:, 0]
        pA = prob[:, 1]
        vexp = sb("vexp", [P, 2, BLKS * GROUPS * INGRP * VW])
        amax = nt
        rinvA = sb("rinvA", [P, 2, AH])
        oA = sb("oA", [P, 2, P])
        oAT = sb("oAT", [P, 2, P])

        ps = ctx.enter_context(nc.psum_tensor("ps", [P, 8, CHUNK], F32))

        const_in = sem("const_in")
        lnx_in = sem("lnx_in")
        attn_in = sem("attn_in")
        wo_in = sem("wo_in")
        ffn_in = sem("ffn_in")
        ones_made = sem("ones_made")
        zeros_made = sem("zeros_made")
        windows_zero = sem("windows_zero")
        vones_made = sem("vones_made")
        const_made = sem("const_made")
        split_hi = sem("split_hi")
        awt_hi = sem("awt_hi")
        awt_made = sem("awt_made")
        wqkv_hi = sem("wqkv_hi")
        wqkv_made = sem("wqkv_made")
        w1_hi = sem("w1_hi")
        w1_made = sem("w1_made")
        bias_mm = sem("bias_mm")
        ln_mean = sem("ln_mean")
        ln_centred = sem("ln_centred")
        ln_squared = sem("ln_squared")
        ln_var = sem("ln_var")
        ln_rstd = sem("ln_rstd")
        ln_diag = sem("ln_diag")
        ln_bcast = sem("ln_bcast")
        ln_scaled = sem("ln_scaled")
        xs_dma = sem("xs_dma")
        ffn_hi = sem("ffn_hi")
        ffn_lo = sem("ffn_lo")
        ffn_g = sem("ffn_g")
        ffn_a = sem("ffn_a")
        ffn_gelu = sem("ffn_gelu")
        ffn_hid = sem("ffn_hid")
        ffn_y = sem("ffn_y")
        x_new = sem("x_new")
        a_hi = sem("a_hi")
        a_split = sem("a_split")
        a_qk_mm = sem("a_qk_mm")
        a_tab = sem("a_tab")
        a_rot = sem("a_rot")
        a_stat = sem("a_stat")
        a_kexp = sem("a_kexp")
        a_score = sem("a_score")
        a_max = sem("a_max")
        a_sub = sem("a_sub")
        a_exp = sem("a_exp")
        a_v = sem("a_v")
        a_vexp = sem("a_vexp")
        a_pT = sem("a_pT")
        a_pTe = sem("a_pTe")
        a_o = sem("a_o")
        a_rinv = sem("a_rinv")
        a_on = sem("a_on")
        a_oT = sem("a_oT")
        a_oTe = sem("a_oTe")
        a_s = sem("a_s")
        a_done = sem("a_done")
        l_split = sem("l_split")
        l_qk = sem("l_qk")
        l_v = sem("l_v")
        l_sq = sem("l_sq")
        l_qm = sem("l_qm")
        l_norm = sem("l_norm")
        l_newton = sem("l_newton")
        l_kn = sem("l_kn")
        l_km = sem("l_km")
        l_qr = sem("l_qr")
        l_qn = sem("l_qn")
        l_kr = sem("l_kr")
        l_tr = sem("l_tr")
        l_tre = sem("l_tre")
        k_prev = [sem("k_prev0"), sem("k_prev1")]
        v_prev = [sem("v_prev0"), sem("v_prev1")]
        l_ve = sem("l_ve")
        l_score = sem("l_score")
        l_max = sem("l_max")
        l_exp = sem("l_exp")
        l_rinv = sem("l_rinv")
        l_prob = sem("l_prob")
        l_pT = sem("l_pT")
        l_pTe = sem("l_pTe")
        l_o = sem("l_o")
        l_oe = sem("l_oe")
        l_y = sem("l_y")
        gate_x = sem("gate_x")
        gate_silu = sem("gate_silu")
        gate_mul = sem("gate_mul")
        gate_out = sem("gate_out")
        stored = sem("stored")

        block = ctx.enter_context(nc.Block())

        def x_before_local(L):
            return CHUNKS + L * (TILES + CHUNKS)

        def x_before_ffn(L):
            return x_before_local(L) + TILES

        N_CONST = 9
        N_FFN = 3 + NPART
        NEWTON = 12

        def rstd_before(L, j):
            return NEWTON * (L * (CHUNKS - 1) + j) if not isinstance(j, int) or j else NEWTON * (L * (CHUNKS - 1) + 1)

        def xs_before_local(L):
            return 32 * (CHUNKS + L * (TILES + CHUNKS))

        def xs_before_ffn(L):
            return xs_before_local(L) + 32 * TILES

        SPLITS_BEFORE_L = [L * TILES for L in range(DEPTH)]

        def shifted(xs, j, width):
            per = SEQ // width
            return xs[:, bass.ds((j // per) * ROW + (j % per) * width, width)]

        def part(t, j, width):
            return t[:, bass.ds(j * width, width)]

        def hd(ap):
            return ap.rearrange("p (h d) -> p h d", h=HEADS)

        @block.sync
        def _(sp):
            for j in range(CHUNKS):
                sp.dma_start(part(D, j, CHUNK), part(a["xT"], j, CHUNK)).then_inc(lnx_in, 16)
            loads = [(ident[:], a["ident"]), (raw[:, 0:4 * P], a["awt"][:, 0:4 * P]), (mask_in, a["masks"]),
                     (hmask[:], a["hmask"]), (pmask[:], a["pmask"]), (arot[:], a["arot"]),
                     (awv[:], a["awt"][:, 4 * P:5 * P]), (awo[:], a["awo"]), (ltab[:], a["ltab"])]
            for dst, src in loads:
                sp.dma_start(dst, src).then_inc(const_in, 16)

            def load_attn(L):
                sp.dma_start(raw[:], a["wqkv"][L]).then_inc(attn_in, 16)
                sp.dma_start(scales[:], a["scales"][L]).then_inc(attn_in, 16)

            def load_wo(L):
                sp.dma_start(wo[:], a["wo"][L].rearrange("(c p) n -> p c n", p=P)).then_inc(wo_in, 16)

            def load_ffn(L):
                sp.dma_start(raw1[:], a["w1"][L]).then_inc(ffn_in, 16)
                for c, (u, n) in enumerate(PARTS):
                    sp.dma_start(w2[0:n, c, :], a["w2"][L, u:u + n, :]).then_inc(ffn_in, 16)
                sp.dma_start(vecs[:], a["vecs"][L]).then_inc(ffn_in, 16)
                sp.dma_start(b1[:], a["b1"][L]).then_inc(ffn_in, 16)

            def held(value):
                return value if isinstance(value, int) else sp.snap(value)

            def copy_shifted(xs, j, width, done):
                per = SEQ // width
                col, src, done = held((j // per) * ROW + (j % per) * width), held(j * width), held(done)
                late = held(col + 1)
                sp.wait_ge(x_new, done)
                sp.dma_start(xs[0:64, bass.ds(col, width)], X[0:64, bass.ds(src, width)]).then_inc(xs_dma, 16)
                sp.dma_start(xs[64:P, bass.ds(late, width)], X[64:P, bass.ds(src, width)]).then_inc(xs_dma, 16)

            load_wo(0)
            load_ffn(0)
            sp.wait_ge(awt_made, 1)
            load_attn(0)
            with sp.Fori(0, CHUNKS) as j:
                copy_shifted(XS[0], j, CHUNK, j + 1)
            for L in range(DEPTH):
                if L + 1 < DEPTH:
                    sp.wait_ge(wqkv_made, 1 + L)
                    load_attn(L + 1)

                def back(n, par):
                    nxt = 1 - par
                    base = L * TILES
                    turned, done = held(2 * (base + n + 1)), held(base + n + 1)
                    scored, pv1 = held(2 * (base + n)), held(base + n)
                    copied = held(xs_before_local(L) + 32 * (n - 2))
                    if live(n, -3, TILES):
                        sp.wait_ge(xs_dma, copied)
                    if live(n, 0, TILES):
                        sp.wait_ge(l_tre, turned)
                        wait(sp, l_score, scored)
                        sp.dma_start(kT[:, nxt, :, 0:WIN], kT[:, par, :, P:P + WIN]).then_inc(k_prev[nxt], 16)
                        sp.wait_ge(l_ve, done)
                        sp.dma_start(VB[64:P, par, :], V[0:64, par, :]).then_inc(v_prev[par], 16)
                        wait(sp, l_o, pv1)
                        sp.dma_start(VB[0:64, nxt, :], V[64:P, par, :]).then_inc(v_prev[nxt], 16)
                    if live(n, -2, TILES):
                        copy_shifted(XS[1], n - 2, P, x_before_local(L) + n - 1)

                if L == 0:
                    sp.wait_ge(zeros_made, 2)
                    sp.wait_ge(windows_zero, 1)
                    sp.dma_start(kT[:, 0, :, 0:WIN], kT[:, 1, :, P:P + WIN]).then_inc(k_prev[0], 16)
                    sp.dma_start(VB[0:64, 0, :], V[64:P, 1, :]).then_inc(v_prev[0], 16)
                steps(sp, 0, 4, TILES, TILES + 1, back)
                sp.wait_ge(x_new, x_before_ffn(L))
                sp.wait_ge(xs_dma, xs_before_ffn(L))
                if L + 1 < DEPTH:
                    load_wo(L + 1)
                    with sp.Fori(0, CHUNKS) as j:
                        copy_shifted(XS[0], j, CHUNK, x_before_ffn(L) + 1 + j)
                    load_ffn(L + 1)

            for half in range(2):
                sp.dma_start(part(x_in, half, TOKENS // 2), part(a["xT"], half, TOKENS // 2)).then_inc(gate_x, 16)
            with sp.Fori(0, CHUNKS) as j:
                col, made = held(j * CHUNK), held(j + 1)
                sp.wait_ge(gate_out, made)
                sp.dma_start(out[:, bass.ds(col, CHUNK)], x_in[:, bass.ds(col, CHUNK)]).then_inc(stored, 16)
            sp.wait_ge(k_prev[0], 16 * (TILES * DEPTH // 2 + 1))
            sp.wait_ge(v_prev[0], 32 * TILES * DEPTH // 2 + 16)
            sp.wait_ge(stored, 16 * CHUNKS)

        @block.tensor
        def _(pe):
            def mm(o, l, r, start=True, stop=True):
                return nc.tensor.matmul(o, l, r, start=start, stop=stop, skip_group_check=True)

            def mm3(o, l_hi, l_lo, r_hi, r_lo):
                mm(o, l_hi, r_hi, True, False)
                mm(o, l_hi, r_lo, False, False)
                return mm(o, l_lo, r_hi, False, True)

            def turn(o, i):
                return nc.tensor.matmul(o, i, ident[:], is_transpose=True, start=True, stop=True,
                                        skip_group_check=True)

            def norm_stats(r, src):
                base = r * CHUNKS

                def step(j, par):
                    if live(j, 0, CHUNKS):
                        wait(pe, ln_centred, (base + j - 1) if not isinstance(j, int) or j > 1 else 0)
                        mm(ps[:, par, :], mean_w[:], src(j)).then_inc(ln_mean, 1)
                    if live(j, -1, CHUNKS):
                        pe.wait_ge(ln_squared, base + j)
                        for k in range(4):
                            last = mm(ps[:, 2, bass.ds((j - 1) * 4 + k, 1)], sq[:, 1 - par, k * P:(k + 1) * P], mean_c[:])
                        last.then_inc(ln_var, 1)

                steps(pe, 0, 2, CHUNKS, CHUNKS, step)

            def norm_bcast(n, par, base, bank):
                pe.wait_ge(ln_diag, base + n + 1)
                mm(ps[:, bank, :], ones[:], diag[:, par, :]).then_inc(ln_bcast, 1)

            pe.wait_ge(const_made, 1)
            pe.wait_ge(lnx_in, 16 * CHUNKS)
            norm_stats(0, lambda j: part(D, j, CHUNK))

            def a_project(j, par):
                if live(j, 0, CHUNKS):
                    pe.wait_ge(a_split, j + 1)
                    for c in range(4):
                        wait(pe, a_tab, 4 * j + c - 3)
                        mm3(ps[:, c, :], awt[:, 0, c * P:(c + 1) * P], awt[:, 1, c * P:(c + 1) * P],
                            split[:, par, 0, :], split[:, par, 1, :]).then_inc(a_qk_mm, 1)
                if live(j, 2, CHUNKS):
                    wait(pe, x_new, j + 1)
                    norm_bcast(j + 2, par, 0, 4 + par)

            pe.wait_ge(const_in, 16 * N_CONST)
            pe.wait_ge(vones_made, 1)
            pe.wait_ge(awt_made, 1)
            steps(pe, -2, 2, CHUNKS - 2, CHUNKS - 1, a_project)

            def a_tile(n, par):
                nxt = 1 - par
                if live(n, 1, TILES):
                    pe.wait_ge(a_stat, n + 2)
                    pe.wait_ge(a_kexp, n + 2)
                    wait(pe, a_sub, n + 1)
                    for g in range(GROUPS):
                        mm(ps[:, g, 0:P], ident_bf[:], amask[:], True, False)
                    for g in range(GROUPS):
                        for b in range(BLKS):
                            last = mm(ps[32 * b:32 * b + 32, g, 0:P],
                                      qst[32 * g:32 * g + 32, nxt, 32 * b:32 * b + 32],
                                      kexp[32 * g:32 * g + 32, nxt, P * b:P * b + P], False, True)
                    last.then_inc(a_score, 1)
                if live(n, -1, TILES):
                    pe.wait_ge(a_on, n)
                    wait(pe, a_done, n - 1)
                    turn(ps[:, 7, 0:P], oA[:, nxt, :]).then_inc(a_oT, 1)
                if live(n, 0, TILES):
                    pe.wait_ge(a_exp, n + 1)
                    wait(pe, a_pTe, n)
                    for g in range(GROUPS):
                        last = turn(ps[:, 5, g * P:(g + 1) * P], pA[:, par, g * P:(g + 1) * P])
                    last.then_inc(a_pT, 1)
                if live(n, 1, TILES):
                    wait(pe, a_vexp, n + 1)
                    for b in range(BLKS):
                        last = mm(ps[:, 4, P * b:P * b + P], xst[:, nxt, b, :], awv[:])
                    last.then_inc(a_v, 1)
                if live(n, -1, TILES):
                    pe.wait_ge(a_oTe, n)
                    mm(ps[:, 7, 0:P], awo[:], oAT[:, nxt, :]).then_inc(a_s, 1)
                if live(n, 0, TILES):
                    pe.wait_ge(a_pTe, n + 1)
                    pe.wait_ge(a_vexp, n + 1)
                    wait(pe, a_on, n)
                    ve = vexp[:, par, :].rearrange("p (b g c) -> p b g c", b=BLKS, g=GROUPS)
                    for g in range(GROUPS):
                        for b in range(BLKS):
                            last = mm(ps[32 * b:32 * b + 32, 6, g * 4 * VW:(g + 1) * 4 * VW],
                                      pT[:, par, g * P + 32 * b:g * P + 32 * b + 32], ve[:, b, g, :])
                    last.then_inc(a_o, 1)

            steps(pe, -1, 3, TILES - 1, TILES, a_tile)

            for L in range(DEPTH):
                if L == 0:
                    pe.wait_ge(a_done, TILES)
                pe.wait_ge(wo_in, 16 * (L + 1))
                pe.wait_ge(wqkv_made, 1 + L)

                base = L * TILES

                def project(c, hi, lo, made):
                    mm3(ps[:, c, :], hi, lo, wqkv[:, 0, c * INNER:(c + 1) * INNER],
                        wqkv[:, 1, c * INNER:(c + 1) * INNER]).then_inc(made, 1)

                def transposed(n, par, src, ready):
                    pe.wait_ge(ready, base + n + 1)
                    for c in range(4):
                        last = turn(ps[:, 3, c * P:(c + 1) * P], src[:, par, c * P:(c + 1) * P])
                    last.then_inc(l_tr, 1)

                def local(n, par):
                    nxt = 1 - par
                    now, ahead = [(split[:, i, 0, 0:P], split[:, i, 1, 0:P]) for i in (par, nxt)]
                    if live(n, 2, TILES):
                        pe.wait_ge(l_split, base + n + 3)
                        wait(pe, l_qm, base + n + 2)
                        project(0, *now, l_qk)
                    if live(n, 0, TILES):
                        wait(pe, x_new, (x_before_local(L) + n - 2) if not isinstance(n, int) or n > 2 else 0)
                        transposed(n, par, qr, l_qn)

                    def scores(grp):
                        if live(n, 0, TILES):
                            if grp == 0:
                                pe.wait_ge(l_tre, 2 * (base + n + 1))
                                pe.wait_ge(k_prev[par], 16 * ((base + n) // 2 + 1))
                            wait(pe, l_exp, 8 * (base + n - 1) + 4 * grp + 4)
                            first = 1 if par else live_mask(n)
                            mm(ps[:, 4 + grp, :], ident_bf[:], lmask[:, bass.ds(first * CHUNK, CHUNK)], True, False)
                            r = slice(64 * grp, 64 * grp + 64)
                            for s in range(4):
                                for w in range(2):
                                    last = mm(ps[64 * w:64 * w + 64, 4 + grp, s * P:(s + 1) * P],
                                              qT[r, par, s, 64 * w:64 * w + 64],
                                              kT[r, par, s, 64 * w:64 * w + P], False, True)
                            last.then_inc(l_score, 1)

                    def turned_probs(grp):
                        if live(n, -1, TILES):
                            pe.wait_ge(l_prob, 2 * (base + n - 1) + grp + 1)
                            wait(pe, l_pTe, 2 * (base + n - 1) + grp)
                            for s in range(4):
                                last = turn(ps[:, 6, s * P:(s + 1) * P], prob[:, nxt, grp, s * P:(s + 1) * P])
                            last.then_inc(l_pT, 1)

                    turned_probs(0)
                    if live(n, 2, TILES):
                        wait(pe, l_kn, base + n + 2)
                        project(1, *now, l_qk)
                    if live(n, 0, TILES):
                        pe.wait_ge(l_tre, 2 * (base + n) + 1)
                        transposed(n, par, kr, l_kr)
                    if live(n, 1, TILES):
                        wait(pe, l_ve, base + n + 1)
                        project(2, *ahead, l_v)
                    turned_probs(1)
                    scores(0)
                    scores(1)
                    if live(n, -2, TILES):
                        if not live(n, 0, TILES):
                            pe.wait_ge(x_new, x_before_local(L) + n - 2)
                        pe.wait_ge(l_oe, base + n - 1)
                        if live(n, 0, TILES):
                            pe.wait_ge(l_tre, 2 * (base + n + 1))
                        for c in range(4):
                            last = mm(ps[:, 3, 0:P], wo[:, c, :], oT[:, par, c * P:(c + 1) * P], c == 0, c == 3)
                        last.then_inc(l_y, 1)
                    if live(n, -1, TILES):
                        wait(pe, l_oe, base + n - 1)
                        m = base + n - 1
                        pe.wait_ge(l_pTe, 2 * m + 2)
                        pe.wait_ge(l_ve, m + 1)
                        pe.wait_ge(v_prev[nxt], 32 * (m // 2 + 1))
                        for s in range(4):
                            for w in range(2):
                                for grp in range(2):
                                    h = 2 * s + grp
                                    vv = (V if w else VB)[:, nxt, h * HD:(h + 1) * HD]
                                    last = mm(ps[64 * grp:64 * grp + 64, 7, s * P + 64 * w:s * P + 64 * w + 64],
                                              vv, pT[:, grp, s * P + 64 * w:s * P + 64 * w + 64])
                        last.then_inc(l_o, 1)

                def live_mask(n):
                    if isinstance(n, int):
                        return min(n % TPB, 1)
                    k = n % TPB
                    return ((k + TPB - 1) // TPB)

                steps(pe, -2, 2, TILES - 2, TILES - 2, local)

                fb, nb = L * CHUNKS, (1 + L) * CHUNKS

                def mean(j, bank):
                    pe.wait_ge(xs_dma, xs_before_local(L) + 32 * TPC * (j + 1))
                    mm(ps[:, bank, :], mean_w[:], shifted(XS[1], j, CHUNK)).then_inc(ln_mean, 1)

                def variance(j, bank, slot):
                    pe.wait_ge(ln_squared, nb + j + 1)
                    for k in range(4):
                        last = mm(ps[:, bank, k:k + 1], sq[:, slot, k * P:(k + 1) * P], mean_c[:])
                    last.then_inc(ln_var, 1)

                pe.wait_ge(l_qm, base + TILES)
                pe.wait_ge(l_kn, base + TILES)
                mean(0, 0)
                mean(1, 1)
                local(TILES - 1, 1)
                variance(0, 0, 0)
                variance(1, 1, 1)
                pe.wait_ge(l_ve, base + TILES)
                mean(2, 2)
                local(TILES, 0)
                pe.wait_ge(ffn_in, 16 * N_FFN * (L + 1))
                pe.wait_ge(l_pTe, 2 * (base + TILES))
                for c in range(2 * NPART):
                    u, n = PARTS[c % NPART]
                    u += (c // NPART) * HID
                    last = mm(ps[0:n, 6, c:c + 1], raw1[:, u:u + n], vecs[:, 1:2])
                last.then_inc(bias_mm, 1)
                variance(2, 2, 0)
                pe.wait_ge(ln_rstd, rstd_before(L, 0) + 1)
                norm_bcast(0, 0, nb, 0)
                norm_bcast(1, 1, nb, 1)
                local(TILES + 1, 1)

                def ffn(j, par):
                    def up(c):
                        if live(j, 0, CHUNKS):
                            u, n = PARTS[c]
                            for side, off in ((0, HID), (1, 0)):
                                if side == 0:
                                    wait(pe, ffn_gelu, NPART * (fb + j - 1) + c + 1)
                                else:
                                    wait(pe, ffn_hid, NPART * (fb + j - 1) + c + 1)
                                w = slice(off + u, off + u + n)
                                mm3(ps[0:n, 2 + 2 * c + side, :], w1[:, 0, w], w1[:, 1, w], split[:, par, 0, :],
                                    split[:, par, 1, :]).then_inc(ffn_a if side else ffn_g, 1)

                    if live(j, 3, CHUNKS):
                        wait(pe, ln_scaled, fb + j + 2)
                        mean(j + 3, 0)
                    if live(j, 0, CHUNKS):
                        pe.wait_ge(w1_made, 1 + L)
                        pe.wait_ge(ffn_lo, fb + j + 1)
                    up(0)
                    up(1)
                    if live(j, 3, CHUNKS):
                        variance(j + 3, 0, 1 - par)
                    up(2)
                    if live(j, 2, CHUNKS):
                        if live(j, 3, CHUNKS):
                            pe.wait_ge(ln_rstd, rstd_before(L, j + 3) + 1)
                        norm_bcast(j + 2, par, nb, 0)
                    if live(j, -1, CHUNKS):
                        wait(pe, x_new, (x_before_ffn(L) + j - 1) if not isinstance(j, int) or j > 1 else 0)
                        for c, (u, n) in enumerate(PARTS):
                            pe.wait_ge(ffn_hid, NPART * (fb + j - 1) + c + 1)
                            last = mm(ps[:, 1, :], w2[0:n, c, :], hid[0:n, c, :], c == 0, c == NPART - 1)
                        last.then_inc(ffn_y, 1)

                pe.wait_ge(x_new, x_before_ffn(L))
                pe.wait_ge(ln_rstd, rstd_before(L, 2) + 1)
                steps(pe, 0, 3, CHUNKS - 3, CHUNKS, ffn)

        @block.scalar
        def _(act):
            def norm_stats(r):
                base = r * CHUNKS

                def step(j, par):
                    act.wait_ge(ln_centred, base + j + 1)
                    wait(act, ln_var, base + j - 1)
                    nc.scalar.activation(sq[:, par, :], part(D, j, CHUNK), ACT.Square).then_inc(ln_squared, 1)

                steps(act, 0, 2, CHUNKS, CHUNKS - 1, step)

            norm_stats(0)

            def a_project(j, par):
                act.wait_ge(x_new, j + 1)
                wait(act, a_qk_mm, 4 * (j - 1))
                nc.scalar.activation(split[:, par, 0, :], part(X, j, CHUNK), ACT.Copy).then_inc(a_hi, 1)

            steps(act, 0, 2, CHUNKS, CHUNKS - 1, a_project)

            def a_tile(n, par):
                nxt = 1 - par
                if live(n, 2, TILES):
                    wait(act, a_score, n + 1)
                    wait(act, a_v, n + 1)
                    nc.scalar.activation(qst[:, par, :], part(qA, n + 2, P), ACT.Copy)
                    nc.scalar.activation(xst[:, par].rearrange("p b (r t) -> p b r t", r=INGRP),
                                         part(X, n + 2, P).rearrange("p (b t) -> p b t", b=BLKS).unsqueeze(2)
                                         .broadcast_to([P, BLKS, INGRP, ABLK]), ACT.Copy).then_inc(a_stat, 1)
                if live(n, -1, TILES):
                    act.wait_ge(a_oT, n)
                    nc.scalar.activation(oAT[:, nxt, :], ps[:, 7, 0:P], ACT.Copy).then_inc(a_oTe, 1)
                if live(n, 0, TILES):
                    act.wait_ge(a_pT, n + 1)
                    wait(act, a_o, n - 1)
                    nc.scalar.activation(pT[:, par, :], ps[:, 5, :], ACT.Copy).then_inc(a_pTe, 1)
                if live(n, 1, TILES):
                    act.wait_ge(a_sub, n + 2)
                    nc.scalar.activation(pA[:, nxt, :], pA[:, nxt, :], ACT.Exp,
                                         scale=float(AHD) ** -0.5).then_inc(a_exp, 1)
                if live(n, -1, TILES):
                    act.wait_ge(a_s, n)
                    nc.scalar.activation(part(A_OUT, n - 1, P), ps[:, 7, 0:P], ACT.Copy).then_inc(a_done, 1)

            act.wait_ge(a_rot, 2 * CHUNKS)
            steps(act, -2, 2, TILES - 2, TILES, a_tile)

            for L in range(DEPTH):
                base = L * TILES

                def local(n, par):
                    nxt = 1 - par

                    def square(c):
                        act.wait_ge(l_qk, 2 * (base + n + 2) + c + 1)
                        wait(act, l_norm, base + n + 2)
                        nc.scalar.activation(sq[:, c, :], ps[:, c, :], ACT.Square).then_inc(l_sq, 1)

                    def turned_probs(grp):
                        act.wait_ge(l_pT, 2 * (base + n - 1) + grp + 1)
                        nc.scalar.activation(pT[:, grp, :], ps[:, 6, :], ACT.Copy).then_inc(l_pTe, 1)

                    if live(n, 2, TILES):
                        square(0)
                    if live(n, 0, TILES):
                        act.wait_ge(l_tr, 2 * (base + n) + 1)
                        nc.scalar.activation(qT[:, par, :, :], ps[:, 3, :].rearrange("p (c t) -> p c t", c=4),
                                             ACT.Copy).then_inc(l_tre, 1)
                    if live(n, 0, TILES):
                        act.wait_ge(l_v, base + n + 1)
                        wait(act, l_o, base + n - 1)
                        if live(n, -1, TILES):
                            act.wait_ge(v_prev[nxt], 32 * ((base + n - 1) // 2 + 1))
                        nc.scalar.activation(V[:, par, :], ps[:, 2, :], ACT.Copy).then_inc(l_ve, 1)
                    if live(n, -1, TILES):
                        wait(act, l_o, base + n - 1)
                        turned_probs(0)
                    if live(n, 0, TILES):
                        act.wait_ge(l_tr, 2 * (base + n) + 2)
                        nc.scalar.activation(kT[:, par, :, WIN:WIN + P], ps[:, 3, :].rearrange("p (c t) -> p c t", c=4),
                                             ACT.Copy).then_inc(l_tre, 1)
                    if live(n, 2, TILES):
                        square(1)
                    if live(n, -1, TILES):
                        turned_probs(1)
                    if live(n, -2, TILES):
                        act.wait_ge(l_o, base + n - 1)
                        wait(act, l_y, base + n - 3)
                        nc.scalar.activation(oT[:, par, :], ps[:, 7, :], ACT.Copy).then_inc(l_oe, 1)
                    if live(n, 0, TILES):
                        for grp in range(2):
                            act.wait_ge(l_max, 2 * (base + n) + grp + 1)
                            for s in range(4):
                                nc.scalar.activation(prob[:, par, grp, s * P:(s + 1) * P],
                                                     ps[:, 4 + grp, s * P:(s + 1) * P], ACT.Exp,
                                                     bias=nmax[:, par, grp * 4 + s:grp * 4 + s + 1],
                                                     accum_out=rsum[:, par, grp * 4 + s:grp * 4 + s + 1]).then_inc(l_exp, 1)

                steps(act, -2, 4, TILES - 2, TILES - 2, local)

                fb, nb = L * CHUNKS, (1 + L) * CHUNKS

                def squares(j, slot):
                    act.wait_ge(ln_centred, nb + j + 1)
                    act.wait_ge(ln_var, nb + j - 1)
                    nc.scalar.activation(sq[:, slot, :], part(D, j, CHUNK), ACT.Square).then_inc(ln_squared, 1)

                def ffn(j, par):
                    if live(j, 3, CHUNKS):
                        squares(j + 3, 1 - par)
                    if live(j, 0, CHUNKS):
                        for c, (u, n) in enumerate(PARTS):
                            act.wait_ge(ffn_g, NPART * (fb + j) + c + 1)
                            wait(act, ffn_hid, NPART * (fb + j - 1) + c + 1)
                            nc.scalar.activation(gel[c][0:n, :], ps[0:n, 2 + 2 * c, :], ACT.Gelu,
                                                 bias=bias1[0:n, NPART + c:NPART + c + 1]).then_inc(ffn_gelu, 1)
                    if live(j, 2, CHUNKS):
                        act.wait_ge(ln_scaled, fb + j + 3)
                        wait(act, ffn_a, NPART * (fb + j + 1))
                        nc.scalar.activation(split[:, par, 0, :], tA[:], ACT.Copy).then_inc(ffn_hi, 1)

                squares(0, 0)
                squares(1, 1)
                local(TILES - 1, 1)
                local(TILES, 0)
                squares(2, 0)
                local(TILES + 1, 1)
                for j, t in enumerate((tA, tB)):
                    act.wait_ge(ln_scaled, fb + j + 1)
                    nc.scalar.activation(split[:, j, 0, :], t[:], ACT.Copy).then_inc(ffn_hi, 1)
                act.wait_ge(w1_made, 1 + L)
                steps(act, 0, 1, CHUNKS - 3, CHUNKS - 1, ffn)

            def silu(j, par):
                act.wait_ge(x_new, x_before_ffn(DEPTH - 1) + j + 1)
                nc.scalar.activation(part(X, j, CHUNK), part(X, j, CHUNK), ACT.Silu).then_inc(gate_silu, 1)

            steps(act, 0, 0, CHUNKS, CHUNKS - 1, silu)

        @block.vector
        def _(dve):
            v = nc.vector

            def rsqrt(s, t, sem, uses, s_in, low=None):
                links = [0]

                def link(ins):
                    links[0] += 1
                    ins.then_inc(sem, 1)
                    dve.wait_ge(sem, uses * NEWTON + links[0])

                if low is None:
                    link(v.tensor_scalar(s, s_in, EPS, None, ALU.add))
                else:
                    link(v.tensor_scalar(s, s_in, low, None, ALU.max))
                link(v.tensor_scalar(t.bitcast(I32), s.bitcast(I32), 1, None, ALU.logical_shift_right))
                link(v.tensor_scalar(t.bitcast(I32), t.bitcast(I32), -1.0, MAGIC, ALU.mult, ALU.add))
                y, u = t, newt_u(s)
                for k in range(3):
                    link(v.tensor_tensor(u, s, y, ALU.mult))
                    link(v.scalar_tensor_tensor(u, u, -0.5, y, ALU.mult, ALU.mult))
                    link(v.scalar_tensor_tensor(s if k == 2 else y, u, 1.5, y, ALU.add, ALU.mult))
                assert links[0] == NEWTON

            def newt_u(s):
                return newt[:, 1, 0:s.shape[1]]

            def split_into(slot, src, width, made, value):
                hi, lo = split[:, slot, 0, 0:width], split[:, slot, 1, 0:width]
                v.tensor_copy(hi, src).then_inc(split_hi, 1)
                dve.wait_ge(split_hi, value + 1)
                v.tensor_tensor(lo, src, hi.bitcast(F32), ALU.subtract).then_inc(made, 1)

            def norm_stats(r, src):
                base = r * CHUNKS

                def step(j, par):
                    dve.wait_ge(ln_mean, base + j + 1)
                    v.tensor_tensor(part(D, j, CHUNK), src(j), ps[:, par, :], ALU.subtract).then_inc(ln_centred, 1)

                steps(dve, 0, 0, CHUNKS, CHUNKS - 1, step)

            def norm_rstd(r):
                dve.wait_ge(ln_var, (r + 1) * CHUNKS)
                rsqrt(rstd[:], newt[:, 0, :], ln_rstd, r, ps[:, 2, 0:TILES])

            dve.wait_ge(ones_made, 1)
            v.tensor_scalar(mean_c[:], ones[:, 0:1], 1.0 / DIM, None, ALU.mult)
            v.tensor_scalar(mean_w[:], ones[:], 1.0 / DIM, None, ALU.mult).then_inc(const_made, 1)

            def clear_first(xs):
                for b in range(BATCH):
                    last = v.memset(xs[64:P, b * ROW:b * ROW + 1], 0.0)
                last.then_inc(zeros_made, 1)

            clear_first(XS[0])

            dve.wait_ge(lnx_in, 16 * CHUNKS)
            norm_stats(0, lambda j: part(D, j, CHUNK))

            dve.wait_ge(const_in, 16 * N_CONST)
            v.tensor_copy(awt[:, 0, :], raw[:, 0:4 * P]).then_inc(awt_hi, 1)
            v.tensor_copy(ident_bf[:], ident[:])
            v.tensor_copy(lmask[:], mask_in[:, 0:2 * CHUNK])
            v.tensor_copy(amask[:], mask_in[:, 2 * CHUNK:2 * CHUNK + P])
            dve.wait_ge(awt_hi, 1)
            v.tensor_tensor(awt[:, 1, :], raw[:, 0:4 * P], awt[:, 0, :].bitcast(F32), ALU.subtract).then_inc(awt_made, 1)
            norm_rstd(0)

            def a_project(j, par):
                nxt = 1 - par

                def rotated(c, t):
                    if live(j, 0, CHUNKS):
                        dve.wait_ge(a_qk_mm, 4 * j + c + 1)
                        wait(dve, a_rot, 2 * j + (c // 2) - 1)
                        v.tensor_tensor(t[:], ps[:, c, :], arot[:, c % 2, bass.ds((j % CPB) * CHUNK, CHUNK)],
                                        ALU.mult).then_inc(a_tab, 1)

                if live(j, 1, CHUNKS):
                    dve.wait_ge(ln_bcast, j + 2)
                    v.tensor_tensor(part(X, j + 1, CHUNK), part(D, j + 1, CHUNK), ps[:, 4 + nxt, :],
                                    ALU.mult).then_inc(x_new, 1)
                rotated(0, tA)
                rotated(1, tB)
                if live(j, 1, CHUNKS):
                    dve.wait_ge(a_hi, j + 2)
                    dve.wait_ge(x_new, j + 2)
                    v.tensor_tensor(split[:, nxt, 1, :], part(X, j + 1, CHUNK), split[:, nxt, 0, :].bitcast(F32),
                                    ALU.subtract).then_inc(a_split, 1)
                rotated(2, kA)
                rotated(3, kB)

            steps(dve, -1, 1, CHUNKS - 1, CHUNKS - 1, a_project)

            def a_tile(n, par):
                nxt = 1 - par
                if live(n, 1, TILES):
                    dve.wait_ge(a_score, n + 2)
                    sc = ps[:, 0:4, 0:P].rearrange("p g (h k) -> p g h k", h=INGRP)
                    v.tensor_reduce(amax[:, nxt, :], sc, AX_X, ALU.max).then_inc(a_max, 1)
                    dve.wait_ge(a_max, n + 2)
                    wait(dve, a_pT, n)
                    v.tensor_tensor(pA[:, nxt, :].rearrange("p (g h k) -> p g h k", g=GROUPS, h=INGRP), sc,
                                    amax[:, nxt, :].rearrange("p (g h) -> p g h", g=GROUPS).unsqueeze(3)
                                    .broadcast_to([P, GROUPS, INGRP, ABLK]), ALU.subtract).then_inc(a_sub, 1)
                    dve.wait_ge(a_v, n + 2)
                    wait(dve, a_o, n)
                    v.tensor_tensor(vexp[:, nxt, :].rearrange("p (b h c) -> p b h c", h=INGRP, c=VW)[:, :, :, 0:AHD],
                                    ps[:, 4, :].rearrange("p (b h c) -> p b h c", h=INGRP, c=AHD),
                                    pmask[:].unsqueeze(1).unsqueeze(3).broadcast_to([P, BLKS * GROUPS, INGRP, AHD]),
                                    ALU.mult).then_inc(a_vexp, 1)
                if live(n, 0, TILES):
                    dve.wait_ge(a_o, n + 1)
                    o = ps[:, 6, 0:AH * VW].rearrange("p (h c) -> p h c", h=AH)
                    v.reciprocal(rinvA[:, par, :], o[:, :, AHD]).then_inc(a_rinv, 1)
                    dve.wait_ge(a_rinv, n + 1)
                    wait(dve, a_oT, n - 1)
                    v.tensor_tensor(oA[:, par, :].rearrange("p (h c) -> p h c", h=AH), o[:, :, 0:AHD],
                                    rinvA[:, par, :].unsqueeze(2).broadcast_to([P, AH, AHD]), ALU.mult).then_inc(a_on, 1)

            steps(dve, -1, 3, TILES - 1, TILES - 1, a_tile)

            dve.wait_ge(a_done, TILES)
            clear_first(XS[1])

            def attn_tables(L):
                dve.wait_ge(attn_in, 32 * (L + 1))
                for i in range(2):
                    sc = scales[:, i, :].unsqueeze(1).broadcast_to([P, TPB, HD])
                    tab, rot = [t.rearrange("p i (n d) -> p i n d", d=HD) for t in (ltab, lrot)]
                    v.tensor_tensor(rot[:, 2 * i], tab[:, 2 * i], sc, ALU.mult)
                    for half in range(2):
                        d, o = slice(32 * half, 32 * half + 32), slice(32 - 32 * half, 64 - 32 * half)
                        v.tensor_tensor(rot[:, 2 * i + 1, :, d], tab[:, 2 * i + 1, :, d], sc[:, :, o], ALU.mult)

            def attn_weights(L):
                v.tensor_copy(wqkv[:, 0, :], raw[:]).then_inc(wqkv_hi, 1)
                dve.wait_ge(wqkv_hi, 1 + L)
                v.tensor_tensor(wqkv[:, 1, :], raw[:], wqkv[:, 0, :].bitcast(F32), ALU.subtract).then_inc(wqkv_made, 1)

            def ffn_weights(L):
                dve.wait_ge(ffn_in, 16 * N_FFN * (L + 1))
                v.tensor_scalar(w1[:, 0, :], raw1[:], vecs[:, 0:1], None, ALU.mult).then_inc(w1_hi, 1)
                dve.wait_ge(bias_mm, 1 + L)
                n_last = PARTS[-1][1]
                full = lambda t: t.rearrange("p (s c) -> p s c", s=2)[:, :, 0:NPART - 1]
                rest = lambda t: t.rearrange("p (s c) -> p s c", s=2)[0:n_last, :, NPART - 1:NPART]
                v.tensor_tensor(full(bias1[:]), full(ps[:, 6, 0:2 * NPART]), full(b1[:]), ALU.add)
                v.tensor_tensor(rest(bias1[:]), rest(ps[:, 6, 0:2 * NPART]), rest(b1[:]), ALU.add)
                dve.wait_ge(w1_hi, 1 + L)
                v.scalar_tensor_tensor(w1[:, 1, :], raw1[:], vecs[:, 0:1], w1[:, 0, :].bitcast(F32), ALU.mult,
                                       ALU.subtract).then_inc(w1_made, 1)

            attn_tables(0)
            attn_weights(0)
            for L in range(DEPTH):
                dve.wait_ge(wqkv_made, 1 + L)
                dve.wait_ge(xs_dma, xs_before_local(L))
                base = L * TILES

                def link(m, k, slot=0):
                    y, s, u = nt[:, 0, :], nt[:, 1, :], newt[:, 1, 0:2 * HEADS]
                    if k == 1:
                        dve.wait_ge(l_norm, base + m + 1)
                        ins = v.tensor_scalar(s, s, 1e-24, None, ALU.max)
                    else:
                        dve.wait_ge(l_newton, (base + m) * NEWTON + k - 1)
                    if k == 2:
                        ins = v.tensor_scalar(y.bitcast(I32), s.bitcast(I32), 1, None, ALU.logical_shift_right)
                    elif k == 3:
                        ins = v.tensor_scalar(y.bitcast(I32), y.bitcast(I32), -1.0, MAGIC, ALU.mult, ALU.add)
                    elif k == NEWTON:
                        ins = v.scalar_tensor_tensor(ss[:, slot, :], u, 1.5, y, ALU.add, ALU.mult)
                    elif k > 3 and k % 3 == 1:
                        ins = v.tensor_tensor(u, s, y, ALU.mult)
                    elif k > 3 and k % 3 == 2:
                        ins = v.scalar_tensor_tensor(u, u, -0.5, y, ALU.mult, ALU.mult)
                    elif k > 3:
                        ins = v.scalar_tensor_tensor(y, u, 1.5, y, ALU.add, ALU.mult)
                    ins.then_inc(l_newton, 1)

                def local(n, par):
                    nxt = 1 - par

                    def links(first, last):
                        if live(n, 2, TILES):
                            for k in range(first, last + 1):
                                link(n + 2, k)

                    def maxima(grp):
                        if live(n, 0, TILES):
                            dve.wait_ge(l_score, 2 * (base + n) + grp + 1)
                            v.tensor_reduce(nmax[:, par, 4 * grp:4 * grp + 4],
                                            ps[:, 4 + grp, :].rearrange("p (s k) -> p s k", s=4),
                                            AX_X, ALU.max, negate=True).then_inc(l_max, 1)

                    if live(n, 1, TILES):
                        wait(dve, l_km, base + n + 1)
                        dve.wait_ge(l_newton, (base + n + 2) * NEWTON)
                        v.tensor_tensor(hd(kn[:]), hd(ps[:, 1, :]),
                                        ss[:, nxt, 8:16].unsqueeze(2).broadcast_to([P, HEADS, HD]),
                                        ALU.mult).then_inc(l_kn, 1)
                        wait(dve, l_tr, 2 * (base + n) - 1)
                        dve.wait_ge(l_qm, base + n + 2)
                        v.tensor_tensor(qr[:, nxt, :], tA[:], tB[:], ALU.add).then_inc(l_qr, 1)
                    if live(n, -1, TILES):
                        dve.wait_ge(l_exp, 8 * (base + n))
                        v.reciprocal(rinv[:, nxt, 4:8], rsum[:, nxt, 4:8]).then_inc(l_rinv, 1)
                    if live(n, 2, TILES):
                        pos = ((n + 2) % TPB) * HD
                        dve.wait_ge(l_sq, 2 * (base + n + 2) + 1)
                        wait(dve, l_qr, base + n + 2)
                        v.tensor_tensor(hd(tA[:]), hd(ps[:, 0, :]), row8(0, pos, 0, HD), ALU.mult)
                        v.tensor_tensor(hd(tB[:])[:, :, 0:32], hd(ps[:, 0, :])[:, :, 32:64], row8(1, pos, 0, 32), ALU.mult)
                        v.tensor_tensor(hd(tB[:])[:, :, 32:64], hd(ps[:, 0, :])[:, :, 0:32], row8(1, pos, 32, 32),
                                        ALU.mult).then_inc(l_qm, 1)
                        v.tensor_reduce(nt[:, 1, 0:8], hd(sq[:, 0, :]), AX_X, ALU.add)
                        dve.wait_ge(l_sq, 2 * (base + n + 2) + 2)
                        v.tensor_reduce(nt[:, 1, 8:16], hd(sq[:, 1, :]), AX_X, ALU.add).then_inc(l_norm, 1)
                    links(1, 1)
                    maxima(0)
                    links(2, 2)
                    if live(n, 3, TILES):
                        wait(dve, l_v, base + n + 2)
                        split_into(nxt, shifted(XS[0], n + 3, P), P, l_split, SPLITS_BEFORE_L[L] + n + 3)
                    links(3, 4)
                    maxima(1)
                    links(5, 6)
                    if live(n, -2, TILES):
                        dve.wait_ge(l_y, base + n - 1)
                        x = part(X, n - 2, P)
                        v.tensor_tensor(x, x, ps[:, 3, 0:P], ALU.add).then_inc(x_new, 1)
                    links(7, 8)
                    links(9, 9)
                    if live(n, 0, TILES):
                        dve.wait_ge(l_exp, 8 * (base + n) + 4)
                        v.reciprocal(rinv[:, par, 0:4], rsum[:, par, 0:4]).then_inc(l_rinv, 1)
                    links(10, 11)
                    if live(n, 2, TILES):
                        wait(dve, l_qn, base + n + 1)
                        wait(dve, l_kn, base + n + 1)
                        link(n + 2, NEWTON, par)

                def row8(tab, pos, off, width):
                    return lrot[:, tab, bass.ds(pos + off, width)].unsqueeze(1).broadcast_to([P, HEADS, width])

                steps(dve, -3, 2, TILES - 4, TILES - 2, local)

                fb, nb = L * CHUNKS, (1 + L) * CHUNKS

                def centre(j, bank):
                    dve.wait_ge(ln_mean, nb + j + 1)
                    v.tensor_tensor(part(D, j, CHUNK), shifted(XS[1], j, CHUNK), ps[:, bank, :],
                                    ALU.subtract).then_inc(ln_centred, 1)

                def rstd_links(j, first, last, bank, chunks=1):
                    w = 4 * chunks
                    y, s, u = newt[:, 0, 0:w], newt[:, 0, 8:8 + w], newt[:, 1, 0:w]
                    for k in range(first, last + 1):
                        if k == 1:
                            dve.wait_ge(ln_var, nb + j + chunks)
                        dve.wait_ge(ln_rstd, rstd_before(L, j) + k - 1)
                        if k == 1:
                            ins = v.tensor_scalar(s.rearrange("p (c k) -> p c k", c=chunks), ps[:, bank:bank + chunks, 0:4],
                                                  EPS, None, ALU.add)
                        elif k == 2:
                            ins = v.tensor_scalar(y.bitcast(I32), s.bitcast(I32), 1, None, ALU.logical_shift_right)
                        elif k == 3:
                            ins = v.tensor_scalar(y.bitcast(I32), y.bitcast(I32), -1.0, MAGIC, ALU.mult, ALU.add)
                        elif k % 3 == 1:
                            ins = v.tensor_tensor(u, s, y, ALU.mult)
                        elif k % 3 == 2:
                            ins = v.scalar_tensor_tensor(u, u, -0.5, y, ALU.mult, ALU.mult)
                        else:
                            to = rstd[:, bass.ds(j * 4, w)] if k == NEWTON else y
                            ins = v.scalar_tensor_tensor(to, u, 1.5, y, ALU.add, ALU.mult)
                        ins.then_inc(ln_rstd, 1)

                def lows(j, slot, t):
                    dve.wait_ge(ln_scaled, fb + j + 1)
                    dve.wait_ge(ffn_hi, fb + j + 1)
                    v.tensor_tensor(split[:, slot, 1, :], t[:], split[:, slot, 0, :].bitcast(F32),
                                    ALU.subtract).then_inc(ffn_lo, 1)

                def ffn(j, par):
                    def hidden(c):
                        if live(j, -1, CHUNKS):
                            u, n = PARTS[c]
                            dve.wait_ge(ffn_gelu, NPART * (fb + j - 1) + c + 1)
                            dve.wait_ge(ffn_a, NPART * (fb + j - 1) + c + 1)
                            v.scalar_tensor_tensor(hid[0:n, c, :], ps[0:n, 3 + 2 * c, :], bias1[0:n, c:c + 1],
                                                   gel[c][0:n, :], ALU.add, ALU.mult).then_inc(ffn_hid, 1)

                    def links(first, last):
                        if live(j, 3, CHUNKS):
                            rstd_links(j + 3, first, last, 0)

                    wait(dve, ffn_y, (fb + j - 1) if live(j, -1, CHUNKS) else 0)
                    hidden(0)
                    if live(j, 3, CHUNKS):
                        centre(j + 3, 0)
                    hidden(1)
                    hidden(2)
                    if live(j, -2, CHUNKS):
                        dve.wait_ge(ffn_y, fb + j - 1)
                        x = part(X, j - 2, CHUNK)
                        v.scalar_tensor_tensor(x, ps[:, 1, :], vecs[:, 2:3], x, ALU.add, ALU.add).then_inc(x_new, 1)
                    links(1, 6)
                    if live(j, 2, CHUNKS):
                        dve.wait_ge(ln_bcast, nb + j + 3)
                        wait(dve, ffn_hi, fb + j + 2)
                        wait(dve, ffn_lo, fb + j + 2)
                        v.tensor_tensor(tA[:], part(D, j + 2, CHUNK), ps[:, 0, :], ALU.mult).then_inc(ln_scaled, 1)
                    links(7, 9)
                    if live(j, 2, CHUNKS):
                        lows(j + 2, par, tA)
                    links(10, 12)

                centre(0, 0)
                centre(1, 1)
                local(TILES - 1, 1)
                rstd_links(0, 1, 6, 0, 2)
                local(TILES, 0)
                rstd_links(0, 7, NEWTON, 0, 2)
                centre(2, 2)
                ffn_weights(L)
                for j, t in enumerate((tA, tB)):
                    dve.wait_ge(ln_bcast, nb + j + 1)
                    v.tensor_tensor(t[:], part(D, j, CHUNK), ps[:, j, :], ALU.mult).then_inc(ln_scaled, 1)
                local(TILES + 1, 1)
                lows(0, 0, tA)
                lows(1, 1, tB)
                rstd_links(2, 1, NEWTON, 2)
                dve.wait_ge(w1_made, 1 + L)
                steps(dve, 0, 3, CHUNKS - 3, CHUNKS - 3, ffn)
                if L + 1 < DEPTH:
                    attn_tables(L + 1)
                ffn(CHUNKS - 2, 0)
                if L + 1 < DEPTH:
                    attn_weights(L + 1)
                for j in range(CHUNKS - 1, CHUNKS + 2):
                    ffn(j, j % 2)

            dve.wait_ge(gate_x, 32)

            def gate(j, par):
                if live(j, 0, CHUNKS):
                    dve.wait_ge(gate_silu, j + 1)
                    g = part(A_OUT, j, CHUNK)
                    v.tensor_tensor(g, g, part(X, j, CHUNK), ALU.mult).then_inc(gate_mul, 1)
                if live(j, -1, CHUNKS):
                    dve.wait_ge(gate_mul, j)
                    x = part(x_in, j - 1, CHUNK)
                    v.tensor_tensor(x, x, part(A_OUT, j - 1, CHUNK), ALU.add).then_inc(gate_out, 1)

            steps(dve, 0, 2, CHUNKS, CHUNKS, gate)

        @block.gpsimd
        def _(pool):
            g = nc.gpsimd
            g.memset(ones[:], 1.0).then_inc(ones_made, 1)
            g.memset(V[:, 1, :], 0.0)
            g.memset(kT[:, 1, :, P:P + WIN], 0.0).then_inc(windows_zero, 1)
            pool.wait_ge(const_in, 16 * N_CONST)
            for s in range(2):
                last = g.tensor_copy(vexp[:, s, :].rearrange("p (b h c) -> p b h c", h=INGRP, c=VW)[:, :, :, AHD],
                                     pmask[:].unsqueeze(1).broadcast_to([P, BLKS * GROUPS, INGRP]))
            last.then_inc(vones_made, 1)

            def norm_diag(j, slot, used):
                wait(pool, ln_bcast, used)
                g.tensor_tensor(diag[:, slot, :].rearrange("p (k t) -> p k t", k=4),
                                ident[:].unsqueeze(1).broadcast_to([P, 4, P]),
                                rstd[:, bass.ds(j * 4, 4)].unsqueeze(2).broadcast_to([P, 4, P]),
                                ALU.mult).then_inc(ln_diag, 1)

            pool.wait_ge(ln_rstd, NEWTON)

            def a_project(j, par):
                if live(j, 2, CHUNKS):
                    norm_diag(j + 2, par, j + 1)
                if live(j, 0, CHUNKS):
                    for i, (dst, s, t) in enumerate(((qA, tA, tB), (kR, kA, kB))):
                        pool.wait_ge(a_tab, 4 * j + 2 * i + 2)
                        g.tensor_tensor(part(dst, j, CHUNK), s[:], t[:], ALU.add).then_inc(a_rot, 1)

            steps(pool, -2, 0, CHUNKS - 2, CHUNKS - 1, a_project)
            pool.wait_ge(a_rot, 2 * CHUNKS)

            def a_tile(n, par):
                if live(n, 0, TILES):
                    wait(pool, a_score, n - 1)
                    g.tensor_tensor(kexp[:, par, :].rearrange("p (b h k) -> p b h k", b=BLKS, h=INGRP),
                                    part(kR, n, P).rearrange("p (b k) -> p b k", b=BLKS).unsqueeze(2)
                                    .broadcast_to([P, BLKS, INGRP, ABLK]),
                                    hmask[:].unsqueeze(1).unsqueeze(3).broadcast_to([P, BLKS, INGRP, ABLK]),
                                    ALU.mult).then_inc(a_kexp, 1)

            steps(pool, 0, 2, TILES, TILES - 1, a_tile)

            for L in range(DEPTH):
                base = L * TILES

                def row8(tab, pos, off, width):
                    return lrot[:, tab, bass.ds(pos + off, width)].unsqueeze(1).broadcast_to([P, HEADS, width])

                def normalise(m, slot, grp):
                    pool.wait_ge(l_rinv, 2 * (base + m) + grp + 1)
                    p4 = prob[:, slot, grp, :].rearrange("p (s k) -> p s k", s=4)
                    g.tensor_tensor(p4, p4, rinv[:, slot, 4 * grp:4 * grp + 4].unsqueeze(2).broadcast_to([P, 4, P]),
                                    ALU.mult).then_inc(l_prob, 1)

                def local(n, par):
                    nxt = 1 - par
                    if live(n, -1, TILES):
                        normalise(n - 1, nxt, 1)
                    if live(n, 1, TILES):
                        pos = ((n + 1) % TPB) * HD
                        pool.wait_ge(l_qr, base + n + 2)
                        g.tensor_tensor(hd(qr[:, nxt, :]), hd(qr[:, nxt, :]),
                                        ss[:, nxt, 0:8].unsqueeze(2).broadcast_to([P, HEADS, HD]),
                                        ALU.mult).then_inc(l_qn, 1)
                        pool.wait_ge(l_kn, base + n + 2)
                        wait(pool, l_kr, base + n + 1)
                        g.tensor_tensor(hd(kA[:]), hd(kn[:]), row8(2, pos, 0, HD), ALU.mult)
                        g.tensor_tensor(hd(kB[:])[:, :, 0:32], hd(kn[:])[:, :, 32:64], row8(3, pos, 0, 32), ALU.mult)
                        g.tensor_tensor(hd(kB[:])[:, :, 32:64], hd(kn[:])[:, :, 0:32], row8(3, pos, 32, 32),
                                        ALU.mult).then_inc(l_km, 1)
                        pool.wait_ge(l_km, base + n + 2)
                        wait(pool, l_tr, 2 * (base + n))
                        g.tensor_tensor(kr[:, nxt, :], kA[:], kB[:], ALU.add).then_inc(l_kr, 1)
                    if live(n, 0, TILES):
                        normalise(n, par, 0)

                steps(pool, -1, 2, TILES - 2, TILES - 2, local)
                local(TILES - 1, 1)
                local(TILES, 0)
                pool.wait_ge(l_tr, 2 * (base + TILES))
                nb = (1 + L) * CHUNKS
                pool.wait_ge(ln_rstd, rstd_before(L, 2))
                norm_diag(0, 0, nb - 1)
                norm_diag(1, 1, nb)

                def ffn_norm(j, par):
                    pool.wait_ge(ln_rstd, rstd_before(L, j + 1))
                    norm_diag(j, par, nb + j - 1)

                steps(pool, 2, 2, CHUNKS, CHUNKS - 1, ffn_norm)


def shape_constants():
    f = np.float32
    c = {}
    c["ident"] = np.eye(P, dtype=f)
    i = np.arange(P) % WIN
    k = np.arange(2 * WIN)
    ok = np.where(k[None] < WIN, k[None] >= i[:, None], k[None] - WIN <= i[:, None])
    first = ok & ~((np.arange(P)[:, None] < WIN) & (k[None] < WIN))
    local = [np.tile(np.where(m, 0, NEG), (1, 4)) for m in (first, ok)]
    i, k = np.arange(P) % ABLK, np.arange(ABLK)
    c["masks"] = np.concatenate(local + [np.tile(np.where(k[None] <= i[:, None], 0, NEG), (1, INGRP))], 1).astype(f)
    p = np.arange(P)
    c["hmask"] = (p[:, None] // AHD % INGRP == np.arange(INGRP)[None]).astype(f)
    c["pmask"] = (p[:, None] // ABLK == np.arange(INGRP)[None]).astype(f)
    inv = (f(1.0) / f(10000.0) ** (np.arange(0, AHD, 2, dtype=f) / f(AHD))).astype(f)
    t = (np.arange(SEQ, dtype=f)[None] * inv[p % (AHD // 2)][:, None]).astype(f)
    sign = np.where(p % AHD < AHD // 2, -1, 1).astype(f)[:, None]
    c["arot"] = np.stack([np.cos(t), np.sin(t) * sign], 1).astype(f)
    half = np.arange(0, HD, 2, dtype=f)
    inv = (f(1.0) / f(10000.0) ** (half / f(HD))).astype(f)
    t = np.arange(SEQ, dtype=f)
    fr = (t[:, None] * inv[None]).astype(f)
    b = ((half + f(0.4 * HD)) / f(1.4 * HD)).astype(f)
    power = ((t - SEQ // 2) / f(WIN // 2)).astype(f)
    sc = (b[None] ** power[:, None]).astype(f)
    two = lambda x: np.concatenate([x, x], -1)
    cos, sin, sc = two(np.cos(fr)), np.concatenate([-np.sin(fr), np.sin(fr)], -1), two(sc)
    tabs = np.stack([cos * sc * 8, sin * sc * 8, cos / sc, sin / sc]).astype(f)
    c["ltab"] = np.ascontiguousarray(tabs.reshape(4, TPB, P, HD).transpose(2, 0, 1, 3).reshape(P, 4, TPB * HD))
    return c


def kernel(L0_attn_x, L0_attn_Wqkv, L0_attn_Wout, L0_ffn_wqkv, L0_ffn_q_scale, L0_ffn_k_scale, L0_ffn_wo,
           L0_ffn_ln_g, L0_ffn_ln_b, L0_ffn_w1, L0_ffn_b1, L0_ffn_w2, L0_ffn_b2):
    import concourse.bacc as bacc
    from concourse.bass_utils import run_bass_kernel_spmd

    con = np.ascontiguousarray
    arrays = dict(shape_constants())
    arrays["xT"] = con(np.asarray(L0_attn_x).reshape(TOKENS, DIM).T)
    w = np.asarray(L0_attn_Wqkv).T
    even = np.concatenate([h * AHD + np.r_[0:AHD:2, 1:AHD:2] for h in range(AH)])
    odd = np.concatenate([h * AHD + np.r_[1:AHD:2, 0:AHD:2] for h in range(AH)])
    q, k, v = w[:, 0:P], w[:, P:2 * P], w[:, 2 * P:3 * P]
    arrays["awt"] = con(np.concatenate([q[:, even], q[:, odd], k[:, even], k[:, odd], v], 1))
    arrays["awo"] = con(np.asarray(L0_attn_Wout).T)
    arrays["wqkv"] = con(L0_ffn_wqkv)
    arrays["wo"] = con(L0_ffn_wo)
    arrays["w1"] = con(L0_ffn_w1)
    arrays["w2"] = con(L0_ffn_w2)
    arrays["vecs"] = con(np.stack([L0_ffn_ln_g, L0_ffn_ln_b, L0_ffn_b2], -1))
    b = np.zeros((DEPTH, 2, NPART * P), np.asarray(L0_ffn_b1).dtype)
    b[:, :, 0:HID] = np.asarray(L0_ffn_b1).reshape(DEPTH, 2, HID)
    arrays["b1"] = con(b.reshape(DEPTH, 2 * NPART, P).transpose(0, 2, 1))
    s = np.stack([L0_ffn_q_scale, L0_ffn_k_scale], 1)
    arrays["scales"] = con(np.broadcast_to(s[:, None], (DEPTH, P, 2, HD)))

    nc = bacc.Bacc("TRN2", target_bir_lowering=False, num_devices=1, dynamic_dma_scratch_size=1024)
    ins = {n: nc.dram_tensor(f"in_{n}", x.shape, mybir.dt.from_np(x.dtype), kind="ExternalInput").ap()
           for n, x in arrays.items()}
    out = nc.dram_tensor("out_T", (DIM, TOKENS), F32, kind="ExternalOutput").ap()
    build(nc, ins, out)
    r = run_bass_kernel_spmd(nc, [{f"in_{n}": x for n, x in arrays.items()}], core_ids=[0])
    return con(r.results[0]["out_T"].T).reshape(BATCH, SEQ, DIM)
```

```python
from contextlib import ExitStack

import numpy as np

import concourse.bass as bass
from concourse import mybir
from concourse.alu_op_type import AluOpType as ALU

ACT = mybir.ActivationFunctionType
AX_X = mybir.AxisListType.X
F32 = mybir.dt.float32
F32R = mybir.dt.float32r
BF16 = mybir.dt.bfloat16
I32 = mybir.dt.int32

P = 128
BATCH, SEQ, DIM = 4, 1024, 128
TOKENS = BATCH * SEQ
TILES = TOKENS // P
TPB = SEQ // P
CHUNK = 512
CHUNKS = TOKENS // CHUNK
CPB = SEQ // CHUNK
TPC = CHUNK // P
ROW = SEQ + 1
DEPTH = 2

HEADS, HD, WIN = 8, 64, 64
INNER = HEADS * HD
HID = int(DIM * 4 * 2 / 3)
PARTS = [(c, min(P, HID - c)) for c in range(0, HID, P)]
NPART = len(PARTS)

AH, AHD, ABLK = 16, 8, 32
GROUPS, INGRP = 4, 4
BLKS = P // ABLK
VW = AHD + 1

NEG = -1e30
EPS = 1e-5
MAGIC = float(0x5F3759DF)


def live(n, k, count):
    return not isinstance(n, int) or 0 <= n + k < count


def wait(eng, sem, value):
    if not isinstance(value, int) or value > 0:
        eng.wait_ge(sem, value)


def steps(eng, first, start, stop, last, step, unroll=2):
    assert unroll % 2 == 0 and (stop - start) % unroll == 0
    for n in range(first, start):
        step(n, n % 2)
    with eng.Fori(0, (stop - start) // unroll) as it:
        for u in range(unroll):
            step(it * unroll + (start + u), (start + u) % 2)
    for n in range(stop, last + 1):
        step(n, n % 2)


def pairs(eng, count, body):
    body(0)
    with eng.Fori(1, count) as it:
        body(it)


def build(nc, a, out):
    with ExitStack() as ctx:
        def sb(name, shape, dt=F32):
            return ctx.enter_context(nc.sbuf_tensor(name, shape, dt))

        def sem(name):
            return ctx.enter_context(nc.semaphore(name))

        X = sb("X", [P, TOKENS])
        XS = [sb(f"XS{i}", [P, BATCH * ROW]) for i in range(2)]
        D = sb("D", [P, TOKENS])
        A_OUT = sb("A_OUT", [P, TOKENS])
        ident = sb("ident", [P, P])
        ident_bf = sb("ident_bf", [P, P], BF16)
        ones = sb("ones", [P, P])
        mean_w = sb("mean_w", [P, P])
        mean_c = sb("mean_c", [P, 1])
        lmask = sb("lmask", [P, 2 * CHUNK], BF16)
        amask = sb("amask", [P, P], BF16)
        hmask = sb("hmask", [P, INGRP])
        pmask = sb("pmask", [P, INGRP])
        ltab = sb("ltab", [P, 4, TPB * HD])
        lrot = sb("lrot", [P, 4, TPB * HD])
        arot = sb("arot", [P, 2, SEQ])
        raw = sb("raw", [P, 3 * INNER])
        wqkv = sb("wqkv", [P, 2, 3 * INNER], F32R)
        awt = sb("awt", [P, 2, 4 * P], F32R)
        awv = sb("awv", [P, P])
        awo = sb("awo", [P, P])
        wo = sb("wo", [P, INNER // P, DIM])
        raw1 = sb("raw1", [P, 2 * HID])
        w1 = sb("w1", [P, 2, 2 * HID], F32R)
        w2 = sb("w2", [P, NPART, DIM])
        vecs = sb("vecs", [P, 3])
        b1 = sb("b1", [P, 2 * NPART])
        bias1 = sb("bias1", [P, 2 * NPART])
        scales = sb("scales", [P, 2, HD])
        split = sb("split", [P, 2, 2, CHUNK], F32R)
        sq = sb("sq", [P, 2, CHUNK])
        rstd = sb("rstd", [P, TILES])
        newt = sb("newt", [P, 2, TILES])
        tA = sb("tA", [P, CHUNK])
        tB = sb("tB", [P, CHUNK])
        kA = sb("kA", [P, CHUNK])
        kB = sb("kB", [P, CHUNK])
        kn = sb("kn", [P, CHUNK])
        qr = sb("qr", [P, 2, CHUNK])
        kr = sb("kr", [P, 2, CHUNK])
        qT = sb("qT", [P, 2, HEADS // 2, P])
        kT = sb("kT", [P, 2, HEADS // 2, WIN + P])
        V = sb("V", [P, 2, INNER])
        VB = sb("VB", [P, 2, INNER])
        ss = sb("ss", [P, 2, 2 * HEADS])
        nt = sb("nt", [P, 2, 2 * HEADS])
        nmax = sb("nmax", [P, 2, HEADS])
        rsum = sb("rsum", [P, 2, HEADS])
        rinv = sb("rinv", [P, 2, HEADS])
        prob = sb("prob", [P, 2, 2, CHUNK])
        pT = sb("pT", [P, 2, CHUNK])
        oT = sb("oT", [P, 2, CHUNK])
        mask_in = A_OUT[:, 0:2 * CHUNK + P]
        gel = (kA, kB, kn)
        hid = prob[:].rearrange("p a b t -> p (a b) t")
        diag = qr
        x_in = XS[0]
        qA, kR = XS[1], D
        qst, xst = kT[:, :, 0, 0:P], qT
        kexp = prob[:, 0]
        pA = prob[:, 1]
        vexp = sb("vexp", [P, 2, BLKS * GROUPS * INGRP * VW])
        amax = nt
        rinvA = sb("rinvA", [P, 2, AH])
        oA = sb("oA", [P, 2, P])
        oAT = sb("oAT", [P, 2, P])

        ps = ctx.enter_context(nc.psum_tensor("ps", [P, 8, CHUNK], F32))

        const_in = sem("const_in")
        ltab_in = sem("ltab_in")
        lnx_in = [sem("lnx_in0"), sem("lnx_in1")]
        attn_in = sem("attn_in")
        wo_in = sem("wo_in")
        ffn_in = sem("ffn_in")
        ones_made = sem("ones_made")
        zeros_made = sem("zeros_made")
        windows_zero = sem("windows_zero")
        vones_made = sem("vones_made")
        const_made = sem("const_made")
        split_hi = sem("split_hi")
        awt_hi = sem("awt_hi")
        awt_made = sem("awt_made")
        wqkv_hi = sem("wqkv_hi")
        wqkv_made = sem("wqkv_made")
        w1_hi = sem("w1_hi")
        w1_made = sem("w1_made")
        bias_made = sem("bias_made")
        bias_mm = sem("bias_mm")
        ln_mean = sem("ln_mean")
        ln_centred = sem("ln_centred")
        ln_squared = sem("ln_squared")
        ln_var = sem("ln_var")
        ln_rstd = sem("ln_rstd")
        ln_diag = sem("ln_diag")
        ln_bcast = sem("ln_bcast")
        ln_scaled = sem("ln_scaled")
        xs_dma = sem("xs_dma")
        ffn_hi = sem("ffn_hi")
        ffn_lo = sem("ffn_lo")
        ffn_g = sem("ffn_g")
        ffn_a = sem("ffn_a")
        ffn_gelu = sem("ffn_gelu")
        ffn_hid = sem("ffn_hid")
        ffn_y = sem("ffn_y")
        x_new = sem("x_new")
        a_hi = sem("a_hi")
        a_split = sem("a_split")
        a_qk_mm = sem("a_qk_mm")
        a_tab = sem("a_tab")
        a_rot = sem("a_rot")
        a_stat = sem("a_stat")
        a_kexp = sem("a_kexp")
        a_score = sem("a_score")
        a_max = sem("a_max")
        a_sub = sem("a_sub")
        a_exp = sem("a_exp")
        a_v = sem("a_v")
        a_vexp = sem("a_vexp")
        a_pT = sem("a_pT")
        a_pTe = sem("a_pTe")
        a_o = sem("a_o")
        a_rinv = sem("a_rinv")
        a_on = sem("a_on")
        a_oT = sem("a_oT")
        a_oTe = sem("a_oTe")
        a_s = sem("a_s")
        a_done = sem("a_done")
        l_split = sem("l_split")
        l_qk = sem("l_qk")
        l_v = sem("l_v")
        l_sq = sem("l_sq")
        l_qm = sem("l_qm")
        l_norm = sem("l_norm")
        l_newton = sem("l_newton")
        l_kn = sem("l_kn")
        l_km = sem("l_km")
        l_qr = sem("l_qr")
        l_qn = sem("l_qn")
        l_kr = sem("l_kr")
        l_tr = sem("l_tr")
        l_tre = sem("l_tre")
        k_prev = [sem("k_prev0"), sem("k_prev1")]
        v_prev = [sem("v_prev0"), sem("v_prev1")]
        l_ve = sem("l_ve")
        l_score = sem("l_score")
        l_max = sem("l_max")
        l_exp = sem("l_exp")
        l_rinv = sem("l_rinv")
        l_prob = sem("l_prob")
        l_pT = sem("l_pT")
        l_pTe = sem("l_pTe")
        l_o = sem("l_o")
        l_oe = sem("l_oe")
        l_y = sem("l_y")
        gate_x = sem("gate_x")
        gate_silu = sem("gate_silu")
        gate_mul = sem("gate_mul")
        gate_out = sem("gate_out")
        stored = sem("stored")

        block = ctx.enter_context(nc.Block())

        def x_before_local(L):
            return CHUNKS + L * (TILES + CHUNKS)

        def x_before_ffn(L):
            return x_before_local(L) + TILES

        N_CONST = 8
        N_FFN = 3 + NPART
        NEWTON = 12

        def rstd_before(L, j):
            return NEWTON * (3 + L * (CHUNKS - 1) + (max(j - 1, 0) if isinstance(j, int) else j - 1))

        def xs_before_local(L):
            return 32 * (CHUNKS + L * (TILES + CHUNKS))

        def xs_before_ffn(L):
            return xs_before_local(L) + 32 * TILES

        SPLITS_BEFORE_L = [L * TILES for L in range(DEPTH)]

        def shifted(xs, j, width):
            per = SEQ // width
            return xs[:, bass.ds((j // per) * ROW + (j % per) * width, width)]

        def part(t, j, width):
            return t[:, bass.ds(j * width, width)]

        def hd(ap):
            return ap.rearrange("p (h d) -> p h d", h=HEADS)

        @block.sync
        def _(sp):
            for j in range(CHUNKS):
                sp.dma_start(part(D, j, CHUNK), part(a["xT"], j, CHUNK)).then_inc(lnx_in[j // 4], 16)
            loads = [(ident[:], a["ident"]), (raw[:, 0:4 * P], a["awt"][:, 0:4 * P]), (mask_in, a["masks"]),
                     (hmask[:], a["hmask"]), (pmask[:], a["pmask"]), (arot[:], a["arot"]),
                     (awv[:], a["awt"][:, 4 * P:5 * P]), (awo[:], a["awo"])]
            for dst, src in loads:
                sp.dma_start(dst, src).then_inc(const_in, 16)
            sp.dma_start(ltab[:], a["ltab"]).then_inc(ltab_in, 16)

            def load_attn(L):
                sp.dma_start(raw[:], a["wqkv"][L]).then_inc(attn_in, 16)
                sp.dma_start(scales[:], a["scales"][L]).then_inc(attn_in, 16)

            def load_wo(L):
                sp.dma_start(wo[:], a["wo"][L].rearrange("(c p) n -> p c n", p=P)).then_inc(wo_in, 16)

            def load_ffn(L):
                sp.dma_start(raw1[:], a["w1"][L]).then_inc(ffn_in, 16)
                for c, (u, n) in enumerate(PARTS):
                    sp.dma_start(w2[0:n, c, :], a["w2"][L, u:u + n, :]).then_inc(ffn_in, 16)
                sp.dma_start(vecs[:], a["vecs"][L]).then_inc(ffn_in, 16)
                sp.dma_start(b1[:], a["b1"][L]).then_inc(ffn_in, 16)

            def held(value):
                return value if isinstance(value, int) else sp.snap(value)

            def copy_shifted(xs, j, width, done, copied=None):
                per = SEQ // width
                col, src, done = held((j // per) * ROW + (j % per) * width), held(j * width), held(done)
                late = held(col + 1)
                if copied is not None:
                    copied = held(copied)
                    sp.wait_ge(xs_dma, copied)
                sp.wait_ge(x_new, done)
                sp.dma_start(xs[0:64, bass.ds(col, width)], X[0:64, bass.ds(src, width)]).then_inc(xs_dma, 16)
                sp.dma_start(xs[64:P, bass.ds(late, width)], X[64:P, bass.ds(src, width)]).then_inc(xs_dma, 16)

            load_wo(0)
            load_ffn(0)
            sp.wait_ge(awt_made, 1)
            load_attn(0)
            with sp.Fori(0, CHUNKS) as j:
                copy_shifted(XS[0], j, CHUNK, j + 1)
            for L in range(DEPTH):
                if L + 1 < DEPTH:
                    sp.wait_ge(wqkv_made, 1 + L)
                    load_attn(L + 1)

                def back(n, par):
                    nxt = 1 - par
                    base = L * TILES
                    turned, done = held(2 * (base + n + 1)), held(base + n + 1)
                    scored, pv1 = held(2 * (base + n)), held(base + n)
                    copied = held(xs_before_local(L) + 32 * (n - 2))
                    if live(n, -3, TILES):
                        sp.wait_ge(xs_dma, copied)
                    if live(n, 0, TILES):
                        sp.wait_ge(l_tre, turned)
                        wait(sp, l_score, scored)
                        sp.dma_start(kT[:, nxt, :, 0:WIN], kT[:, par, :, P:P + WIN]).then_inc(k_prev[nxt], 16)
                        sp.wait_ge(l_ve, done)
                        sp.dma_start(VB[64:P, par, :], V[0:64, par, :]).then_inc(v_prev[par], 16)
                        wait(sp, l_o, pv1)
                        sp.dma_start(VB[0:64, nxt, :], V[64:P, par, :]).then_inc(v_prev[nxt], 16)
                    if live(n, -2, TILES):
                        copy_shifted(XS[1], n - 2, P, x_before_local(L) + n - 1)

                if L == 0:
                    sp.wait_ge(zeros_made, 2)
                    sp.wait_ge(windows_zero, 1)
                    sp.dma_start(kT[:, 0, :, 0:WIN], kT[:, 1, :, P:P + WIN]).then_inc(k_prev[0], 16)
                    sp.dma_start(VB[0:64, 0, :], V[64:P, 1, :]).then_inc(v_prev[0], 16)
                steps(sp, 0, 4, TILES, TILES + 1, back)
                sp.wait_ge(x_new, x_before_ffn(L))
                sp.wait_ge(xs_dma, xs_before_ffn(L))
                if L + 1 < DEPTH:
                    load_wo(L + 1)
                    before = x_before_ffn(L) + 1
                    with sp.Fori(before, before + CHUNKS) as done:
                        copy_shifted(XS[0], done - before, CHUNK, done, xs_before_ffn(L) + 32 * (done - before))
                    load_ffn(L + 1)

            for half in range(2):
                sp.dma_start(part(x_in, half, TOKENS // 2), part(a["xT"], half, TOKENS // 2)).then_inc(gate_x, 16)
            with sp.Fori(0, CHUNKS) as j:
                col, made = held(j * CHUNK), held(j + 1)
                sp.wait_ge(gate_out, made)
                sp.dma_start(out[:, bass.ds(col, CHUNK)], x_in[:, bass.ds(col, CHUNK)]).then_inc(stored, 16)
            sp.wait_ge(k_prev[0], 16 * (TILES * DEPTH // 2 + 1))
            sp.wait_ge(v_prev[0], 32 * TILES * DEPTH // 2 + 16)
            sp.wait_ge(stored, 16 * CHUNKS)

        @block.tensor
        def _(pe):
            def mm(o, l, r, start=True, stop=True):
                return nc.tensor.matmul(o, l, r, start=start, stop=stop, skip_group_check=True)

            def mm3(o, l_hi, l_lo, r_hi, r_lo):
                mm(o, l_hi, r_hi, True, False)
                mm(o, l_hi, r_lo, False, False)
                return mm(o, l_lo, r_hi, False, True)

            def turn(o, i):
                return nc.tensor.matmul(o, i, ident[:], is_transpose=True, start=True, stop=True,
                                        skip_group_check=True)

            def norm_bcast(n, par, base, bank):
                pe.wait_ge(ln_diag, base + n + 1)
                mm(ps[:, bank, :], ones[:], diag[:, par, :]).then_inc(ln_bcast, 1)

            pe.wait_ge(const_made, 1)

            def mean(j, bank):
                mm(ps[:, bank, :], mean_w[:], part(D, j, CHUNK)).then_inc(ln_mean, 1)

            def variance(j, bank):
                pe.wait_ge(ln_squared, j + 1)
                for k in range(4):
                    last = mm(ps[:, bank, j * 4 + k:j * 4 + k + 1], sq[:, j % 2, k * P:(k + 1) * P], mean_c[:])
                last.then_inc(ln_var, 1)

            pe.wait_ge(lnx_in[0], 64)
            for j in range(4):
                mean(j, j)
            for j in range(4):
                variance(j, (7, 5)[j // 2])
            pe.wait_ge(lnx_in[1], 64)

            def a_project(j, par):
                norm = isinstance(j, int) and j in (0, 1)
                if norm:
                    pe.wait_ge(ln_centred, 4 + 2 * j)
                    mean(4 + 2 * j, 6)
                if live(j, 0, CHUNKS):
                    pe.wait_ge(a_split, j + 1)
                    for c in range(4):
                        if norm and c == 2:
                            pe.wait_ge(ln_centred, 5 + 2 * j)
                            mean(5 + 2 * j, 6)
                        wait(pe, a_tab, 4 * j + c - 3)
                        mm3(ps[:, c, :], awt[:, 0, c * P:(c + 1) * P], awt[:, 1, c * P:(c + 1) * P],
                            split[:, par, 0, :], split[:, par, 1, :]).then_inc(a_qk_mm, 1)
                if norm:
                    variance(4 + 2 * j, 7)
                    variance(5 + 2 * j, 7)
                if live(j, 2, CHUNKS):
                    wait(pe, x_new, j + 1)
                    norm_bcast(j + 2, par, 0, 4 + par)

            pe.wait_ge(const_in, 16 * N_CONST)
            pe.wait_ge(vones_made, 1)
            pe.wait_ge(awt_made, 1)
            pe.wait_ge(ln_rstd, NEWTON + 1)
            steps(pe, -2, 2, CHUNKS - 2, CHUNKS - 1, a_project)

            def a_tile(n, par):
                nxt = 1 - par
                if live(n, 1, TILES):
                    pe.wait_ge(a_stat, n + 2)
                    pe.wait_ge(a_kexp, n + 2)
                    wait(pe, a_sub, n + 1)
                    for g in range(GROUPS):
                        mm(ps[:, g, 0:P], ident_bf[:], amask[:], True, False)
                    for g in range(GROUPS):
                        for b in range(BLKS):
                            last = mm(ps[32 * b:32 * b + 32, g, 0:P],
                                      qst[32 * g:32 * g + 32, nxt, 32 * b:32 * b + 32],
                                      kexp[32 * g:32 * g + 32, nxt, P * b:P * b + P], False, True)
                    last.then_inc(a_score, 1)
                if live(n, -1, TILES):
                    pe.wait_ge(a_on, n)
                    wait(pe, a_done, n - 1)
                    turn(ps[:, 7, 0:P], oA[:, nxt, :]).then_inc(a_oT, 1)
                if live(n, 0, TILES):
                    pe.wait_ge(a_exp, n + 1)
                    wait(pe, a_pTe, n)
                    for g in range(GROUPS):
                        last = turn(ps[:, 5, g * P:(g + 1) * P], pA[:, par, g * P:(g + 1) * P])
                    last.then_inc(a_pT, 1)
                if live(n, 1, TILES):
                    wait(pe, a_vexp, n + 1)
                    for b in range(BLKS):
                        last = mm(ps[:, 4, P * b:P * b + P], xst[:, nxt, b, :], awv[:])
                    last.then_inc(a_v, 1)
                if live(n, -1, TILES):
                    pe.wait_ge(a_oTe, n)
                    mm(ps[:, 7, 0:P], awo[:], oAT[:, nxt, :]).then_inc(a_s, 1)
                if live(n, 0, TILES):
                    pe.wait_ge(a_pTe, n + 1)
                    pe.wait_ge(a_vexp, n + 1)
                    wait(pe, a_on, n)
                    ve = vexp[:, par, :].rearrange("p (b g c) -> p b g c", b=BLKS, g=GROUPS)
                    for g in range(GROUPS):
                        for b in range(BLKS):
                            last = mm(ps[32 * b:32 * b + 32, 6, g * 4 * VW:(g + 1) * 4 * VW],
                                      pT[:, par, g * P + 32 * b:g * P + 32 * b + 32], ve[:, b, g, :])
                    last.then_inc(a_o, 1)

            steps(pe, -1, 3, TILES - 1, TILES - 2, a_tile)

            def layer(L, tail):
                pe.wait_ge(wqkv_made, 1 + L)

                base = L * TILES

                def project(c, hi, lo, made):
                    mm3(ps[:, c, :], hi, lo, wqkv[:, 0, c * INNER:(c + 1) * INNER],
                        wqkv[:, 1, c * INNER:(c + 1) * INNER]).then_inc(made, 1)

                def transposed(n, par, src, ready):
                    pe.wait_ge(ready, base + n + 1)
                    for c in range(4):
                        last = turn(ps[:, 3, c * P:(c + 1) * P], src[:, par, c * P:(c + 1) * P])
                    last.then_inc(l_tr, 1)

                def local(n, par):
                    nxt = 1 - par
                    now, ahead = [(split[:, i, 0, 0:P], split[:, i, 1, 0:P]) for i in (par, nxt)]
                    if live(n, 2, TILES):
                        pe.wait_ge(l_split, base + n + 3)
                        wait(pe, l_qm, base + n + 2)
                        project(0, *now, l_qk)
                    if live(n, 0, TILES):
                        wait(pe, x_new, (x_before_local(L) + n - 2) if not isinstance(n, int) or n > 2 else 0)
                        transposed(n, par, qr, l_qn)

                    def scores(grp):
                        if live(n, 0, TILES):
                            if grp == 0:
                                pe.wait_ge(l_tre, 2 * (base + n + 1))
                                pe.wait_ge(k_prev[par], 16 * ((base + n) // 2 + 1))
                            wait(pe, l_exp, 8 * (base + n - 1) + 4 * grp + 4)
                            first = 1 if par else live_mask(n)
                            mm(ps[:, 4 + grp, :], ident_bf[:], lmask[:, bass.ds(first * CHUNK, CHUNK)], True, False)
                            r = slice(64 * grp, 64 * grp + 64)
                            for s in range(4):
                                for w in range(2):
                                    last = mm(ps[64 * w:64 * w + 64, 4 + grp, s * P:(s + 1) * P],
                                              qT[r, par, s, 64 * w:64 * w + 64],
                                              kT[r, par, s, 64 * w:64 * w + P], False, True)
                            last.then_inc(l_score, 1)

                    def turned_probs(grp):
                        if live(n, -1, TILES):
                            pe.wait_ge(l_prob, 2 * (base + n - 1) + grp + 1)
                            wait(pe, l_pTe, 2 * (base + n - 1) + grp)
                            for s in range(4):
                                last = turn(ps[:, 6, s * P:(s + 1) * P], prob[:, nxt, grp, s * P:(s + 1) * P])
                            last.then_inc(l_pT, 1)

                    def output():
                        if not live(n, 0, TILES):
                            pe.wait_ge(x_new, x_before_local(L) + n - 2)
                        pe.wait_ge(l_oe, base + n - 1)
                        if live(n, 0, TILES):
                            pe.wait_ge(l_tre, 2 * (base + n + 1))
                        for c in range(4):
                            last = mm(ps[:, 3, 0:P], wo[:, c, :], oT[:, par, c * P:(c + 1) * P], c == 0, c == 3)
                        last.then_inc(l_y, 1)

                    scores_done = isinstance(n, int) and n == TILES
                    turned_probs(0)
                    if scores_done:
                        bias_products()
                        output()
                    if live(n, 2, TILES):
                        wait(pe, l_kn, base + n + 2)
                        project(1, *now, l_qk)
                    if live(n, 0, TILES):
                        pe.wait_ge(l_tre, 2 * (base + n) + 1)
                        transposed(n, par, kr, l_kr)
                    if live(n, 1, TILES):
                        wait(pe, l_ve, base + n + 1)
                        project(2, *ahead, l_v)
                    turned_probs(1)
                    scores(0)
                    scores(1)
                    if live(n, -2, TILES) and not scores_done:
                        output()
                    if live(n, -1, TILES):
                        wait(pe, l_oe, base + n - 1)
                        m = base + n - 1
                        pe.wait_ge(l_pTe, 2 * m + 2)
                        pe.wait_ge(l_ve, m + 1)
                        pe.wait_ge(v_prev[nxt], 32 * (m // 2 + 1))
                        for s in range(4):
                            for w in range(2):
                                for grp in range(2):
                                    h = 2 * s + grp
                                    vv = (V if w else VB)[:, nxt, h * HD:(h + 1) * HD]
                                    last = mm(ps[64 * grp:64 * grp + 64, 7, s * P + 64 * w:s * P + 64 * w + 64],
                                              vv, pT[:, grp, s * P + 64 * w:s * P + 64 * w + 64])
                        last.then_inc(l_o, 1)

                def bias_products():
                    pe.wait_ge(l_exp, 8 * (base + TILES))
                    pe.wait_ge(ffn_in, 16 * N_FFN * (L + 1))
                    for c in range(2 * NPART):
                        u, n = PARTS[c % NPART]
                        u += (c // NPART) * HID
                        last = mm(ps[0:n, 4, c:c + 1], raw1[:, u:u + n], vecs[:, 1:2])
                    last.then_inc(bias_mm, 1)

                def live_mask(n):
                    if isinstance(n, int):
                        return min(n % TPB, 1)
                    k = n % TPB
                    return ((k + TPB - 1) // TPB)

                if L == 0:
                    pe.wait_ge(a_sub, TILES)
                    local(-2, 0)
                    a_tile(TILES - 1, 1)
                    a_tile(TILES, 0)
                else:
                    pe.wait_ge(ln_scaled, L * CHUNKS)
                    pe.wait_ge(ffn_gelu, NPART * (L * CHUNKS - 1) + 1)
                    local(-2, 0)
                    tail(CHUNKS, 0)
                    pe.wait_ge(ffn_hid, NPART * L * CHUNKS)
                local(-1, 1)
                if L == 0:
                    pe.wait_ge(a_done, TILES)
                else:
                    pe.wait_ge(x_new, x_before_local(L))
                pe.wait_ge(wo_in, 16 * (L + 1))
                steps(pe, 0, 2, TILES - 2, TILES - 2, local, 4)

                fb, nb = L * CHUNKS, (1 + L) * CHUNKS

                def mean(j, bank):
                    pe.wait_ge(xs_dma, xs_before_local(L) + 32 * TPC * (j + 1))
                    mm(ps[:, bank, :], mean_w[:], shifted(XS[1], j, CHUNK)).then_inc(ln_mean, 1)

                def variance(j, bank, slot):
                    pe.wait_ge(ln_squared, nb + j + 1)
                    for k in range(4):
                        last = mm(ps[:, bank, k:k + 1], sq[:, slot, k * P:(k + 1) * P], mean_c[:])
                    last.then_inc(ln_var, 1)

                pe.wait_ge(l_qm, base + TILES)
                pe.wait_ge(l_kn, base + TILES)
                mean(0, 0)
                mean(1, 1)
                local(TILES - 1, 1)
                variance(0, 0, 0)
                variance(1, 1, 1)
                pe.wait_ge(l_ve, base + TILES)
                mean(2, 2)
                local(TILES, 0)
                variance(2, 2, 0)
                pe.wait_ge(ln_rstd, rstd_before(L, 0) + 1)
                norm_bcast(0, 0, nb, 0)
                local(TILES + 1, 1)
                norm_bcast(1, 1, nb, 1)

                def ffn(j, par):
                    def up(c):
                        if live(j, 0, CHUNKS):
                            u, n = PARTS[c]
                            for side, off in ((0, HID), (1, 0)):
                                if side == 0:
                                    wait(pe, ffn_gelu, NPART * (fb + j - 1) + c + 1)
                                else:
                                    wait(pe, ffn_hid, NPART * (fb + j - 1) + c + 1)
                                w = slice(off + u, off + u + n)
                                mm3(ps[0:n, 1 + 2 * c + side, :], w1[:, 0, w], w1[:, 1, w], split[:, par, 0, :],
                                    split[:, par, 1, :]).then_inc(ffn_a if side else ffn_g, 1)

                    if live(j, 3, CHUNKS):
                        wait(pe, ln_scaled, fb + j + 2)
                        mean(j + 3, 0)
                    if live(j, 0, CHUNKS):
                        pe.wait_ge(w1_made, 1 + L)
                        pe.wait_ge(ffn_lo, fb + j + 1)
                    up(0)
                    up(1)
                    if live(j, 3, CHUNKS):
                        variance(j + 3, 0, 1 - par)
                    up(2)
                    if live(j, 2, CHUNKS):
                        if live(j, 3, CHUNKS):
                            pe.wait_ge(ln_rstd, rstd_before(L, j + 3) + 1)
                        norm_bcast(j + 2, par, nb, 0)
                    if live(j, -1, CHUNKS):
                        wait(pe, x_new, (x_before_ffn(L) + j - 1) if not isinstance(j, int) or j > 1 else 0)
                        for c, (u, n) in enumerate(PARTS):
                            pe.wait_ge(ffn_hid, NPART * (fb + j - 1) + c + 1)
                            last = mm(ps[:, 7, :], w2[0:n, c, :], hid[0:n, c, :], c == 0, c == NPART - 1)
                        last.then_inc(ffn_y, 1)

                pe.wait_ge(x_new, x_before_ffn(L))
                pe.wait_ge(ln_rstd, rstd_before(L, 2) + 1)
                pe.wait_ge(ln_scaled, fb + 2)
                pe.wait_ge(bias_made, 1 + L)
                steps(pe, 0, 3, CHUNKS - 3, CHUNKS - 1 if L + 1 < DEPTH else CHUNKS, ffn)
                return ffn

            tail = None
            for L in range(DEPTH):
                tail = layer(L, tail)

        @block.scalar
        def _(act):
            def squares(j):
                act.wait_ge(ln_centred, j + 1)
                wait(act, ln_var, j - 1)
                nc.scalar.activation(sq[:, j % 2, :], part(D, j, CHUNK), ACT.Square).then_inc(ln_squared, 1)

            def a_project(j, par):
                act.wait_ge(x_new, j + 1)
                wait(act, a_qk_mm, 4 * (j - 1))
                nc.scalar.activation(split[:, par, 0, :], part(X, j, CHUNK), ACT.Copy).then_inc(a_hi, 1)

            for j in range(4):
                squares(j)
            a_project(0, 0)
            for j in range(2):
                a_project(j + 1, 1 - j)
                squares(4 + 2 * j)
                squares(5 + 2 * j)
            steps(act, 3, 4, CHUNKS, CHUNKS - 1, a_project)

            def a_tile(n, par):
                nxt = 1 - par
                if live(n, 2, TILES):
                    wait(act, a_score, n + 1)
                    wait(act, a_v, n + 1)
                    nc.scalar.activation(qst[:, par, :], part(qA, n + 2, P), ACT.Copy)
                    nc.scalar.activation(xst[:, par].rearrange("p b (r t) -> p b r t", r=INGRP),
                                         part(X, n + 2, P).rearrange("p (b t) -> p b t", b=BLKS).unsqueeze(2)
                                         .broadcast_to([P, BLKS, INGRP, ABLK]), ACT.Copy).then_inc(a_stat, 1)
                if live(n, -1, TILES):
                    act.wait_ge(a_oT, n)
                    nc.scalar.activation(oAT[:, nxt, :], ps[:, 7, 0:P], ACT.Copy).then_inc(a_oTe, 1)
                if live(n, 0, TILES):
                    act.wait_ge(a_pT, n + 1)
                    wait(act, a_o, n - 1)
                    nc.scalar.activation(pT[:, par, :], ps[:, 5, :], ACT.Copy).then_inc(a_pTe, 1)
                if live(n, 1, TILES):
                    act.wait_ge(a_sub, n + 2)
                    nc.scalar.activation(pA[:, nxt, :], pA[:, nxt, :], ACT.Exp,
                                         scale=float(AHD) ** -0.5).then_inc(a_exp, 1)
                if live(n, -1, TILES):
                    act.wait_ge(a_s, n)
                    nc.scalar.activation(part(A_OUT, n - 1, P), ps[:, 7, 0:P], ACT.Copy).then_inc(a_done, 1)

            act.wait_ge(a_rot, 2 * CHUNKS)
            steps(act, -2, 2, TILES - 2, TILES - 1, a_tile)

            for L in range(DEPTH):
                base = L * TILES

                def local(n, par):
                    nxt = 1 - par

                    def square(c):
                        act.wait_ge(l_qk, 2 * (base + n + 2) + c + 1)
                        wait(act, l_norm, base + n + 2)
                        nc.scalar.activation(sq[:, c, :], ps[:, c, :], ACT.Square).then_inc(l_sq, 1)

                    def turned_probs(grp):
                        act.wait_ge(l_pT, 2 * (base + n - 1) + grp + 1)
                        nc.scalar.activation(pT[:, grp, :], ps[:, 6, :], ACT.Copy).then_inc(l_pTe, 1)

                    def output():
                        act.wait_ge(l_o, base + n - 1)
                        wait(act, l_y, base + n - 3)
                        nc.scalar.activation(oT[:, par, :], ps[:, 7, :], ACT.Copy).then_inc(l_oe, 1)

                    scores_done = isinstance(n, int) and n == TILES
                    if scores_done:
                        output()
                    if live(n, 2, TILES):
                        square(0)
                    if live(n, 0, TILES):
                        act.wait_ge(l_tr, 2 * (base + n) + 1)
                        nc.scalar.activation(qT[:, par, :, :], ps[:, 3, :].rearrange("p (c t) -> p c t", c=4),
                                             ACT.Copy).then_inc(l_tre, 1)
                    if live(n, 0, TILES):
                        act.wait_ge(l_v, base + n + 1)
                        wait(act, l_o, base + n - 1)
                        if live(n, -1, TILES):
                            act.wait_ge(v_prev[nxt], 32 * ((base + n - 1) // 2 + 1))
                        nc.scalar.activation(V[:, par, :], ps[:, 2, :], ACT.Copy).then_inc(l_ve, 1)
                    if live(n, -1, TILES):
                        wait(act, l_o, base + n - 1)
                        turned_probs(0)
                    if live(n, 0, TILES):
                        act.wait_ge(l_tr, 2 * (base + n) + 2)
                        nc.scalar.activation(kT[:, par, :, WIN:WIN + P], ps[:, 3, :].rearrange("p (c t) -> p c t", c=4),
                                             ACT.Copy).then_inc(l_tre, 1)
                    if live(n, 2, TILES):
                        square(1)
                    if live(n, -1, TILES):
                        turned_probs(1)
                    if live(n, -2, TILES) and not scores_done:
                        output()
                    if live(n, 0, TILES):
                        for grp in range(2):
                            act.wait_ge(l_max, 2 * (base + n) + grp + 1)
                            for s in range(4):
                                nc.scalar.activation(prob[:, par, grp, s * P:(s + 1) * P],
                                                     ps[:, 4 + grp, s * P:(s + 1) * P], ACT.Exp,
                                                     bias=nmax[:, par, grp * 4 + s:grp * 4 + s + 1],
                                                     accum_out=rsum[:, par, grp * 4 + s:grp * 4 + s + 1]).then_inc(l_exp, 1)

                local(-2, 0)
                if L == 0:
                    a_tile(TILES, 0)
                local(-1, 1)
                steps(act, 0, 4, TILES - 2, TILES - 2, local)

                fb, nb = L * CHUNKS, (1 + L) * CHUNKS

                def squares(j, slot):
                    act.wait_ge(ln_centred, nb + j + 1)
                    act.wait_ge(ln_var, nb + j - 1)
                    nc.scalar.activation(sq[:, slot, :], part(D, j, CHUNK), ACT.Square).then_inc(ln_squared, 1)

                def ffn(j, par):
                    if live(j, 3, CHUNKS):
                        squares(j + 3, 1 - par)
                    if live(j, 0, CHUNKS):
                        for c, (u, n) in enumerate(PARTS):
                            act.wait_ge(ffn_g, NPART * (fb + j) + c + 1)
                            wait(act, ffn_hid, NPART * (fb + j - 1) + c + 1)
                            nc.scalar.activation(gel[c][0:n, :], ps[0:n, 1 + 2 * c, :], ACT.Gelu,
                                                 bias=bias1[0:n, NPART + c:NPART + c + 1]).then_inc(ffn_gelu, 1)
                    if live(j, 2, CHUNKS):
                        act.wait_ge(ln_scaled, fb + j + 3)
                        wait(act, ffn_a, NPART * (fb + j + 1))
                        nc.scalar.activation(split[:, par, 0, :], tA[:], ACT.Copy).then_inc(ffn_hi, 1)
                    if L + 1 == DEPTH and live(j, -3, CHUNKS):
                        act.wait_ge(x_new, x_before_ffn(L) + j - 2)
                        x = part(X, j - 3, CHUNK)
                        nc.scalar.activation(x, x, ACT.Silu).then_inc(gate_silu, 1)

                squares(0, 0)
                squares(1, 1)
                local(TILES - 1, 1)
                local(TILES, 0)
                squares(2, 0)
                local(TILES + 1, 1)
                for j, t in enumerate((tA, tB)):
                    act.wait_ge(ln_scaled, fb + j + 1)
                    nc.scalar.activation(split[:, j, 0, :], t[:], ACT.Copy).then_inc(ffn_hi, 1)
                act.wait_ge(bias_made, 1 + L)
                if L + 1 < DEPTH:
                    steps(act, 0, 1, CHUNKS - 3, CHUNKS - 1, ffn)
                else:
                    steps(act, 0, 3, CHUNKS - 3, CHUNKS + 2, ffn)

        @block.vector
        def _(dve):
            v = nc.vector

            def rstd_links(variances, j, w, before, first, last):
                y, s, u = newt[:, 0, 0:w], newt[:, 0, 16:16 + w], newt[:, 1, 0:w]
                for k in range(first, last + 1):
                    if not isinstance(before, int) or before + k > 1:
                        dve.wait_ge(ln_rstd, before + k - 1)
                    if k == 1:
                        to = s if len(variances.shape) == 2 else s.rearrange("p (c k) -> p c k", k=4)
                        ins = v.tensor_scalar(to, variances, EPS, None, ALU.add)
                    elif k == 2:
                        ins = v.tensor_scalar(y.bitcast(I32), s.bitcast(I32), 1, None, ALU.logical_shift_right)
                    elif k == 3:
                        ins = v.tensor_scalar(y.bitcast(I32), y.bitcast(I32), -1.0, MAGIC, ALU.mult, ALU.add)
                    elif k % 3 == 1:
                        ins = v.tensor_tensor(u, s, y, ALU.mult)
                    elif k % 3 == 2:
                        ins = v.scalar_tensor_tensor(u, u, -0.5, y, ALU.mult, ALU.mult)
                    else:
                        to = rstd[:, bass.ds(j * 4, w)] if k == NEWTON else y
                        ins = v.scalar_tensor_tensor(to, u, 1.5, y, ALU.add, ALU.mult)
                    ins.then_inc(ln_rstd, 1)

            def split_into(slot, src, width, made, value, between=None):
                hi, lo = split[:, slot, 0, 0:width], split[:, slot, 1, 0:width]
                v.tensor_copy(hi, src).then_inc(split_hi, 1)
                if between is not None:
                    between()
                dve.wait_ge(split_hi, value + 1)
                v.tensor_tensor(lo, src, hi.bitcast(F32), ALU.subtract).then_inc(made, 1)

            def centre(base, j, src, bank):
                dve.wait_ge(ln_mean, base + j + 1)
                v.tensor_tensor(part(D, j, CHUNK), src, ps[:, bank, :], ALU.subtract).then_inc(ln_centred, 1)

            dve.wait_ge(ones_made, 1)
            v.tensor_scalar(mean_c[:], ones[:, 0:1], 1.0 / DIM, None, ALU.mult)
            v.tensor_scalar(mean_w[:], ones[:], 1.0 / DIM, None, ALU.mult).then_inc(const_made, 1)

            def clear_first(xs):
                for b in range(BATCH):
                    last = v.memset(xs[64:P, b * ROW:b * ROW + 1], 0.0)
                last.then_inc(zeros_made, 1)

            clear_first(XS[0])

            dve.wait_ge(lnx_in[0], 64)
            for j in range(4):
                centre(0, j, part(D, j, CHUNK), j)
            dve.wait_ge(ln_var, 2)
            rstd_links(ps[:, 7, 0:8], 0, 8, 0, 1, NEWTON)

            dve.wait_ge(const_in, 16 * N_CONST)
            v.tensor_copy(awt[:, 0, :], raw[:, 0:4 * P]).then_inc(awt_hi, 1)
            v.tensor_copy(ident_bf[:], ident[:])
            v.tensor_copy(lmask[:], mask_in[:, 0:2 * CHUNK])
            v.tensor_copy(amask[:], mask_in[:, 2 * CHUNK:2 * CHUNK + P])
            dve.wait_ge(awt_hi, 1)
            v.tensor_tensor(awt[:, 1, :], raw[:, 0:4 * P], awt[:, 0, :].bitcast(F32), ALU.subtract).then_inc(awt_made, 1)
            dve.wait_ge(ln_var, 4)
            rstd_links(ps[:, 5, 8:16], 2, 8, NEWTON, 1, NEWTON)

            dve.wait_ge(lnx_in[1], 64)

            def a_project(j, par):
                nxt = 1 - par
                norm = isinstance(j, int) and j in (0, 1)

                def rotated(c, t):
                    if live(j, 0, CHUNKS):
                        dve.wait_ge(a_qk_mm, 4 * j + c + 1)
                        wait(dve, a_rot, 2 * j + (c // 2) - 1)
                        v.tensor_tensor(t[:], ps[:, c, :], arot[:, c % 2, bass.ds((j % CPB) * CHUNK, CHUNK)],
                                        ALU.mult).then_inc(a_tab, 1)

                if live(j, 1, CHUNKS):
                    dve.wait_ge(ln_bcast, j + 2)
                    v.tensor_tensor(part(X, j + 1, CHUNK), part(D, j + 1, CHUNK), ps[:, 4 + nxt, :],
                                    ALU.mult).then_inc(x_new, 1)
                rotated(0, tA)
                if norm:
                    centre(0, 4 + 2 * j, part(D, 4 + 2 * j, CHUNK), 6)
                rotated(1, tB)
                if live(j, 1, CHUNKS):
                    dve.wait_ge(a_hi, j + 2)
                    dve.wait_ge(x_new, j + 2)
                    v.tensor_tensor(split[:, nxt, 1, :], part(X, j + 1, CHUNK), split[:, nxt, 0, :].bitcast(F32),
                                    ALU.subtract).then_inc(a_split, 1)
                if norm:
                    centre(0, 5 + 2 * j, part(D, 5 + 2 * j, CHUNK), 6)
                rotated(2, kA)
                rotated(3, kB)

            for j in range(-1, 2):
                a_project(j, j % 2)
            dve.wait_ge(ln_var, CHUNKS)
            rstd_links(ps[:, 7, 16:32], 4, 16, 2 * NEWTON, 1, NEWTON)
            steps(dve, 2, 3, CHUNKS - 1, CHUNKS - 1, a_project)

            def a_tile(n, par):
                nxt = 1 - par
                if live(n, 1, TILES):
                    dve.wait_ge(a_score, n + 2)
                    sc = ps[:, 0:4, 0:P].rearrange("p g (h k) -> p g h k", h=INGRP)
                    v.tensor_reduce(amax[:, nxt, :], sc, AX_X, ALU.max).then_inc(a_max, 1)
                    dve.wait_ge(a_max, n + 2)
                    wait(dve, a_pT, n)
                    v.tensor_tensor(pA[:, nxt, :].rearrange("p (g h k) -> p g h k", g=GROUPS, h=INGRP), sc,
                                    amax[:, nxt, :].rearrange("p (g h) -> p g h", g=GROUPS).unsqueeze(3)
                                    .broadcast_to([P, GROUPS, INGRP, ABLK]), ALU.subtract).then_inc(a_sub, 1)
                    dve.wait_ge(a_v, n + 2)
                    wait(dve, a_o, n)
                    v.tensor_tensor(vexp[:, nxt, :].rearrange("p (b h c) -> p b h c", h=INGRP, c=VW)[:, :, :, 0:AHD],
                                    ps[:, 4, :].rearrange("p (b h c) -> p b h c", h=INGRP, c=AHD),
                                    pmask[:].unsqueeze(1).unsqueeze(3).broadcast_to([P, BLKS * GROUPS, INGRP, AHD]),
                                    ALU.mult).then_inc(a_vexp, 1)
                if live(n, 0, TILES):
                    dve.wait_ge(a_o, n + 1)
                    o = ps[:, 6, 0:AH * VW].rearrange("p (h c) -> p h c", h=AH)
                    v.reciprocal(rinvA[:, par, :], o[:, :, AHD]).then_inc(a_rinv, 1)
                    dve.wait_ge(a_rinv, n + 1)
                    wait(dve, a_oT, n - 1)
                    v.tensor_tensor(oA[:, par, :].rearrange("p (h c) -> p h c", h=AH), o[:, :, 0:AHD],
                                    rinvA[:, par, :].unsqueeze(2).broadcast_to([P, AH, AHD]), ALU.mult).then_inc(a_on, 1)

            def attn_tables(L, i):
                dve.wait_ge(ltab_in, 16)
                dve.wait_ge(attn_in, 32 * (L + 1))
                sc = scales[:, i, :].unsqueeze(1).broadcast_to([P, TPB, HD])
                tab, rot = [t.rearrange("p i (n d) -> p i n d", d=HD) for t in (ltab, lrot)]
                v.tensor_tensor(rot[:, 2 * i], tab[:, 2 * i], sc, ALU.mult)
                for half in range(2):
                    d, o = slice(32 * half, 32 * half + 32), slice(32 - 32 * half, 64 - 32 * half)
                    v.tensor_tensor(rot[:, 2 * i + 1, :, d], tab[:, 2 * i + 1, :, d], sc[:, :, o], ALU.mult)

            def attn_hi(L):
                v.tensor_copy(wqkv[:, 0, :], raw[:]).then_inc(wqkv_hi, 1)

            def attn_lo(L):
                dve.wait_ge(wqkv_hi, 1 + L)
                v.tensor_tensor(wqkv[:, 1, :], raw[:], wqkv[:, 0, :].bitcast(F32), ALU.subtract).then_inc(wqkv_made, 1)

            steps(dve, -1, 3, 7, 6, a_tile)
            attn_tables(0, 0)
            steps(dve, 7, 7, 13, 12, a_tile)
            attn_tables(0, 1)
            steps(dve, 13, 13, 19, 18, a_tile)
            attn_hi(0)
            steps(dve, 19, 19, 23, 22, a_tile)
            attn_lo(0)
            steps(dve, 23, 23, TILES - 1, TILES - 2, a_tile)

            def ffn_weights(L):
                dve.wait_ge(ffn_in, 16 * N_FFN * (L + 1))
                v.tensor_scalar(w1[:, 0, :], raw1[:], vecs[:, 0:1], None, ALU.mult).then_inc(w1_hi, 1)
                dve.wait_ge(w1_hi, 1 + L)
                v.scalar_tensor_tensor(w1[:, 1, :], raw1[:], vecs[:, 0:1], w1[:, 0, :].bitcast(F32), ALU.mult,
                                       ALU.subtract).then_inc(w1_made, 1)

            def ffn_bias(L):
                dve.wait_ge(bias_mm, 1 + L)
                n_last = PARTS[-1][1]
                full = lambda t: t.rearrange("p (s c) -> p s c", s=2)[:, :, 0:NPART - 1]
                rest = lambda t: t.rearrange("p (s c) -> p s c", s=2)[0:n_last, :, NPART - 1:NPART]
                v.tensor_tensor(full(bias1[:]), full(ps[:, 4, 0:2 * NPART]), full(b1[:]), ALU.add)
                v.tensor_tensor(rest(bias1[:]), rest(ps[:, 4, 0:2 * NPART]), rest(b1[:]), ALU.add).then_inc(bias_made, 1)

            def layer(L, tail):
                dve.wait_ge(wqkv_made, 1 + L)
                base = L * TILES

                def link(m, k, slot=0):
                    y, s, u = nt[:, 0, :], nt[:, 1, :], newt[:, 1, 0:2 * HEADS]
                    if k == 1:
                        dve.wait_ge(l_norm, base + m + 1)
                        ins = v.tensor_scalar(s, s, 1e-24, None, ALU.max)
                    else:
                        dve.wait_ge(l_newton, (base + m) * NEWTON + k - 1)
                    if k == 2:
                        ins = v.tensor_scalar(y.bitcast(I32), s.bitcast(I32), 1, None, ALU.logical_shift_right)
                    elif k == 3:
                        ins = v.tensor_scalar(y.bitcast(I32), y.bitcast(I32), -1.0, MAGIC, ALU.mult, ALU.add)
                    elif k == NEWTON:
                        ins = v.scalar_tensor_tensor(ss[:, slot, :], u, 1.5, y, ALU.add, ALU.mult)
                    elif k > 3 and k % 3 == 1:
                        ins = v.tensor_tensor(u, s, y, ALU.mult)
                    elif k > 3 and k % 3 == 2:
                        ins = v.scalar_tensor_tensor(u, u, -0.5, y, ALU.mult, ALU.mult)
                    elif k > 3:
                        ins = v.scalar_tensor_tensor(y, u, 1.5, y, ALU.add, ALU.mult)
                    ins.then_inc(l_newton, 1)

                def inverse_sums(n, slot):
                    dve.wait_ge(l_exp, 8 * (base + n + 1))
                    v.reciprocal(rinv[:, slot, 4:8], rsum[:, slot, 4:8]).then_inc(l_rinv, 1)

                def add_to_x(n):
                    dve.wait_ge(l_y, base + n + 1)
                    x = part(X, n, P)
                    v.tensor_tensor(x, x, ps[:, 3, 0:P], ALU.add).then_inc(x_new, 1)

                def local(n, par):
                    nxt = 1 - par

                    def links(first, last):
                        if live(n, 2, TILES):
                            for k in range(first, last + 1):
                                link(n + 2, k)

                    def maxima(grp):
                        if live(n, 0, TILES):
                            dve.wait_ge(l_score, 2 * (base + n) + grp + 1)
                            v.tensor_reduce(nmax[:, par, 4 * grp:4 * grp + 4],
                                            ps[:, 4 + grp, :].rearrange("p (s k) -> p s k", s=4),
                                            AX_X, ALU.max, negate=True).then_inc(l_max, 1)

                    if live(n, 1, TILES):
                        wait(dve, l_km, base + n + 1)
                        dve.wait_ge(l_newton, (base + n + 2) * NEWTON)
                        v.tensor_tensor(hd(kn[:]), hd(ps[:, 1, :]),
                                        ss[:, nxt, 8:16].unsqueeze(2).broadcast_to([P, HEADS, HD]),
                                        ALU.mult).then_inc(l_kn, 1)
                        wait(dve, l_tr, 2 * (base + n) - 1)
                        dve.wait_ge(l_qm, base + n + 2)
                        v.tensor_tensor(qr[:, nxt, :], tA[:], tB[:], ALU.add).then_inc(l_qr, 1)
                    if live(n, -1, TILES):
                        inverse_sums(n - 1, nxt)
                    if live(n, 2, TILES):
                        pos = ((n + 2) % TPB) * HD
                        dve.wait_ge(l_sq, 2 * (base + n + 2) + 1)
                        wait(dve, l_qr, base + n + 2)
                        v.tensor_tensor(hd(tA[:]), hd(ps[:, 0, :]), row8(0, pos, 0, HD), ALU.mult)
                        v.tensor_tensor(hd(tB[:])[:, :, 0:32], hd(ps[:, 0, :])[:, :, 32:64], row8(1, pos, 0, 32), ALU.mult)
                        v.tensor_tensor(hd(tB[:])[:, :, 32:64], hd(ps[:, 0, :])[:, :, 0:32], row8(1, pos, 32, 32),
                                        ALU.mult).then_inc(l_qm, 1)
                        v.tensor_reduce(nt[:, 1, 0:8], hd(sq[:, 0, :]), AX_X, ALU.add)
                        dve.wait_ge(l_sq, 2 * (base + n + 2) + 2)
                        v.tensor_reduce(nt[:, 1, 8:16], hd(sq[:, 1, :]), AX_X, ALU.add).then_inc(l_norm, 1)
                    links(1, 1)
                    maxima(0)
                    links(2, 2)
                    if live(n, 3, TILES):
                        wait(dve, l_v, base + n + 2)
                        split_into(nxt, shifted(XS[0], n + 3, P), P, l_split, SPLITS_BEFORE_L[L] + n + 3,
                                   lambda: links(3, 3))
                    else:
                        links(3, 3)
                    links(4, 4)
                    maxima(1)
                    links(5, 6)
                    if live(n, -2, TILES):
                        add_to_x(n - 2)
                    links(7, 8)
                    links(9, 9)
                    if live(n, 0, TILES):
                        dve.wait_ge(l_exp, 8 * (base + n) + 4)
                        v.reciprocal(rinv[:, par, 0:4], rsum[:, par, 0:4]).then_inc(l_rinv, 1)
                    links(10, 11)
                    if live(n, 2, TILES):
                        wait(dve, l_qn, base + n + 1)
                        wait(dve, l_kn, base + n + 1)
                        link(n + 2, NEWTON, par)

                def row8(tab, pos, off, width):
                    return lrot[:, tab, bass.ds(pos + off, width)].unsqueeze(1).broadcast_to([P, HEADS, width])

                if L == 0:
                    dve.wait_ge(xs_dma, xs_before_local(0))
                    local(-3, 1)
                    a_tile(TILES - 1, 1)
                    local(-2, 0)
                    local(-1, 1)
                    dve.wait_ge(a_done, TILES)
                    clear_first(XS[1])
                else:
                    dve.wait_ge(xs_dma, xs_before_ffn(L - 1) + 32)
                    local(-3, 1)
                    tail(CHUNKS, 0)
                    local(-2, 0)
                    tail(CHUNKS + 1, 1)
                    local(-1, 1)
                    dve.wait_ge(xs_dma, xs_before_local(L))
                steps(dve, 0, 4, TILES - 4, TILES - 2, local, 8)

                fb, nb = L * CHUNKS, (1 + L) * CHUNKS
                gate = L + 1 == DEPTH

                def links(j, first, last, bank, chunks=1):
                    if first == 1:
                        dve.wait_ge(ln_var, nb + j + chunks)
                    variances = ps[:, bank, 0:4] if chunks == 1 else ps[:, bank:bank + chunks, 0:4]
                    rstd_links(variances, j, 4 * chunks, rstd_before(L, j), first, last)

                def lows(j, slot, t):
                    dve.wait_ge(ln_scaled, fb + j + 1)
                    dve.wait_ge(ffn_hi, fb + j + 1)
                    v.tensor_tensor(split[:, slot, 1, :], t[:], split[:, slot, 0, :].bitcast(F32),
                                    ALU.subtract).then_inc(ffn_lo, 1)

                def ffn(j, par):
                    def hidden(c):
                        if live(j, -1, CHUNKS):
                            u, n = PARTS[c]
                            dve.wait_ge(ffn_gelu, NPART * (fb + j - 1) + c + 1)
                            dve.wait_ge(ffn_a, NPART * (fb + j - 1) + c + 1)
                            v.scalar_tensor_tensor(hid[0:n, c, :], ps[0:n, 2 + 2 * c, :], bias1[0:n, c:c + 1],
                                                   gel[c][0:n, :], ALU.add, ALU.mult).then_inc(ffn_hid, 1)

                    wait(dve, ffn_y, (fb + j - 1) if live(j, -1, CHUNKS) else 0)
                    hidden(0)
                    if live(j, 3, CHUNKS):
                        centre(nb, j + 3, shifted(XS[1], j + 3, CHUNK), 0)
                    hidden(1)
                    hidden(2)
                    if live(j, -2, CHUNKS):
                        dve.wait_ge(ffn_y, fb + j - 1)
                        x = part(X, j - 2, CHUNK)
                        v.scalar_tensor_tensor(x, ps[:, 7, :], vecs[:, 2:3], x, ALU.add, ALU.add).then_inc(x_new, 1)
                    if live(j, 3, CHUNKS):
                        links(j + 3, 1, 6, 0)
                    if live(j, 2, CHUNKS):
                        dve.wait_ge(ln_bcast, nb + j + 3)
                        wait(dve, ffn_hi, fb + j + 2)
                        wait(dve, ffn_lo, fb + j + 2)
                        v.tensor_tensor(tA[:], part(D, j + 2, CHUNK), ps[:, 0, :], ALU.mult).then_inc(ln_scaled, 1)
                    if live(j, 3, CHUNKS):
                        links(j + 3, 7, 9, 0)
                    if live(j, 2, CHUNKS):
                        lows(j + 2, par, tA)
                    if gate and live(j, -4, CHUNKS):
                        dve.wait_ge(gate_silu, j - 3)
                        s, x = part(A_OUT, j - 4, CHUNK), part(x_in, j - 4, CHUNK)
                        v.tensor_tensor(s, s, part(X, j - 4, CHUNK), ALU.mult).then_inc(gate_mul, 1)
                        dve.wait_ge(gate_mul, j - 3)
                        dve.wait_ge(gate_x, 32)
                        v.tensor_tensor(x, x, s, ALU.add).then_inc(gate_out, 1)
                    if live(j, 3, CHUNKS):
                        links(j + 3, 10, 12, 0)

                centre(nb, 0, shifted(XS[1], 0, CHUNK), 0)
                centre(nb, 1, shifted(XS[1], 1, CHUNK), 1)
                local(TILES - 1, 1)
                inverse_sums(TILES - 1, 1)
                ffn_weights(L)
                links(0, 1, NEWTON, 0, 2)
                centre(nb, 2, shifted(XS[1], 2, CHUNK), 2)
                ffn_bias(L)
                add_to_x(TILES - 2)

                def scaled(j, t):
                    dve.wait_ge(ln_bcast, nb + j + 1)
                    v.tensor_tensor(t[:], part(D, j, CHUNK), ps[:, j, :], ALU.mult).then_inc(ln_scaled, 1)

                links(2, 1, 6, 2)
                scaled(0, tA)
                links(2, 7, 9, 2)
                add_to_x(TILES - 1)
                links(2, 10, NEWTON, 2)
                scaled(1, tB)
                lows(0, 0, tA)
                lows(1, 1, tB)
                dve.wait_ge(bias_made, 1 + L)
                if L + 1 < DEPTH:
                    steps(dve, 0, 3, CHUNKS - 3, CHUNKS - 3, ffn)
                    attn_tables(L + 1, 0)
                    attn_tables(L + 1, 1)
                    ffn(CHUNKS - 2, 0)
                    attn_hi(L + 1)
                    attn_lo(L + 1)
                    ffn(CHUNKS - 1, 1)
                else:
                    for j in range(CHUNKS + 4):
                        ffn(j, j % 2)
                return ffn

            tail = None
            for L in range(DEPTH):
                tail = layer(L, tail)


        @block.gpsimd
        def _(pool):
            g = nc.gpsimd
            g.memset(ones[:], 1.0).then_inc(ones_made, 1)
            g.memset(V[:, 1, :], 0.0)
            g.memset(kT[:, 1, :, P:P + WIN], 0.0).then_inc(windows_zero, 1)
            pool.wait_ge(const_in, 16 * N_CONST)
            for s in range(2):
                last = g.tensor_copy(vexp[:, s, :].rearrange("p (b h c) -> p b h c", h=INGRP, c=VW)[:, :, :, AHD],
                                     pmask[:].unsqueeze(1).broadcast_to([P, BLKS * GROUPS, INGRP]))
            last.then_inc(vones_made, 1)

            def norm_diag(j, slot, used):
                wait(pool, ln_bcast, used)
                g.tensor_tensor(diag[:, slot, :].rearrange("p (k t) -> p k t", k=4),
                                ident[:].unsqueeze(1).broadcast_to([P, 4, P]),
                                rstd[:, bass.ds(j * 4, 4)].unsqueeze(2).broadcast_to([P, 4, P]),
                                ALU.mult).then_inc(ln_diag, 1)

            def a_project(j, par):
                if live(j, 2, CHUNKS):
                    norm_diag(j + 2, par, j + 1)
                if live(j, 0, CHUNKS):
                    for i, (dst, s, t) in enumerate(((qA, tA, tB), (kR, kA, kB))):
                        pool.wait_ge(a_tab, 4 * j + 2 * i + 2)
                        g.tensor_tensor(part(dst, j, CHUNK), s[:], t[:], ALU.add).then_inc(a_rot, 1)

            for half in range(3):
                pool.wait_ge(ln_rstd, NEWTON * (half + 1))
                if half < 2:
                    a_project(2 * half - 2, 0)
                    a_project(2 * half - 1, 1)
            steps(pool, 2, 2, CHUNKS - 2, CHUNKS - 1, a_project)
            pool.wait_ge(a_rot, 2 * CHUNKS)

            def a_tile(n, par):
                if live(n, 0, TILES):
                    wait(pool, a_score, n - 1)
                    g.tensor_tensor(kexp[:, par, :].rearrange("p (b h k) -> p b h k", b=BLKS, h=INGRP),
                                    part(kR, n, P).rearrange("p (b k) -> p b k", b=BLKS).unsqueeze(2)
                                    .broadcast_to([P, BLKS, INGRP, ABLK]),
                                    hmask[:].unsqueeze(1).unsqueeze(3).broadcast_to([P, BLKS, INGRP, ABLK]),
                                    ALU.mult).then_inc(a_kexp, 1)

            steps(pool, 0, 2, TILES, TILES - 1, a_tile)

            for L in range(DEPTH):
                base = L * TILES

                def row8(tab, pos, off, width):
                    return lrot[:, tab, bass.ds(pos + off, width)].unsqueeze(1).broadcast_to([P, HEADS, width])

                def normalise(m, slot, grp):
                    pool.wait_ge(l_rinv, 2 * (base + m) + grp + 1)
                    p4 = prob[:, slot, grp, :].rearrange("p (s k) -> p s k", s=4)
                    g.tensor_tensor(p4, p4, rinv[:, slot, 4 * grp:4 * grp + 4].unsqueeze(2).broadcast_to([P, 4, P]),
                                    ALU.mult).then_inc(l_prob, 1)

                def local(n, par):
                    nxt = 1 - par
                    if live(n, -1, TILES):
                        normalise(n - 1, nxt, 1)
                    if live(n, 1, TILES):
                        pos = ((n + 1) % TPB) * HD
                        pool.wait_ge(l_qr, base + n + 2)
                        g.tensor_tensor(hd(qr[:, nxt, :]), hd(qr[:, nxt, :]),
                                        ss[:, nxt, 0:8].unsqueeze(2).broadcast_to([P, HEADS, HD]),
                                        ALU.mult).then_inc(l_qn, 1)
                        pool.wait_ge(l_kn, base + n + 2)
                        wait(pool, l_kr, base + n + 1)
                        g.tensor_tensor(hd(kA[:]), hd(kn[:]), row8(2, pos, 0, HD), ALU.mult)
                        g.tensor_tensor(hd(kB[:])[:, :, 0:32], hd(kn[:])[:, :, 32:64], row8(3, pos, 0, 32), ALU.mult)
                        g.tensor_tensor(hd(kB[:])[:, :, 32:64], hd(kn[:])[:, :, 0:32], row8(3, pos, 32, 32),
                                        ALU.mult).then_inc(l_km, 1)
                        pool.wait_ge(l_km, base + n + 2)
                        wait(pool, l_tr, 2 * (base + n))
                        g.tensor_tensor(kr[:, nxt, :], kA[:], kB[:], ALU.add).then_inc(l_kr, 1)
                    if live(n, 0, TILES):
                        normalise(n, par, 0)

                steps(pool, -1, 2, TILES - 2, TILES - 2, local)
                local(TILES - 1, 1)
                local(TILES, 0)
                pool.wait_ge(l_tr, 2 * (base + TILES))
                nb = (1 + L) * CHUNKS
                pool.wait_ge(ln_rstd, rstd_before(L, 2))
                norm_diag(0, 0, nb - 1)
                norm_diag(1, 1, nb)

                def ffn_norm(j, par):
                    pool.wait_ge(ln_rstd, rstd_before(L, j + 1))
                    norm_diag(j, par, nb + j - 1)

                steps(pool, 2, 2, CHUNKS, CHUNKS - 1, ffn_norm)


def shape_constants():
    f = np.float32
    c = {}
    c["ident"] = np.eye(P, dtype=f)
    i = np.arange(P) % WIN
    k = np.arange(2 * WIN)
    ok = np.where(k[None] < WIN, k[None] >= i[:, None], k[None] - WIN <= i[:, None])
    first = ok & ~((np.arange(P)[:, None] < WIN) & (k[None] < WIN))
    local = [np.tile(np.where(m, 0, NEG), (1, 4)) for m in (first, ok)]
    i, k = np.arange(P) % ABLK, np.arange(ABLK)
    c["masks"] = np.concatenate(local + [np.tile(np.where(k[None] <= i[:, None], 0, NEG), (1, INGRP))], 1).astype(f)
    p = np.arange(P)
    c["hmask"] = (p[:, None] // AHD % INGRP == np.arange(INGRP)[None]).astype(f)
    c["pmask"] = (p[:, None] // ABLK == np.arange(INGRP)[None]).astype(f)
    inv = (f(1.0) / f(10000.0) ** (np.arange(0, AHD, 2, dtype=f) / f(AHD))).astype(f)
    t = (np.arange(SEQ, dtype=f)[None] * inv[p % (AHD // 2)][:, None]).astype(f)
    sign = np.where(p % AHD < AHD // 2, -1, 1).astype(f)[:, None]
    c["arot"] = np.stack([np.cos(t), np.sin(t) * sign], 1).astype(f)
    half = np.arange(0, HD, 2, dtype=f)
    inv = (f(1.0) / f(10000.0) ** (half / f(HD))).astype(f)
    t = np.arange(SEQ, dtype=f)
    fr = (t[:, None] * inv[None]).astype(f)
    b = ((half + f(0.4 * HD)) / f(1.4 * HD)).astype(f)
    power = ((t - SEQ // 2) / f(WIN // 2)).astype(f)
    sc = (b[None] ** power[:, None]).astype(f)
    two = lambda x: np.concatenate([x, x], -1)
    cos, sin, sc = two(np.cos(fr)), np.concatenate([-np.sin(fr), np.sin(fr)], -1), two(sc)
    tabs = np.stack([cos * sc * 8, sin * sc * 8, cos / sc, sin / sc]).astype(f)
    c["ltab"] = np.ascontiguousarray(tabs.reshape(4, TPB, P, HD).transpose(2, 0, 1, 3).reshape(P, 4, TPB * HD))
    return c


def kernel(L0_attn_x, L0_attn_Wqkv, L0_attn_Wout, L0_ffn_wqkv, L0_ffn_q_scale, L0_ffn_k_scale, L0_ffn_wo,
           L0_ffn_ln_g, L0_ffn_ln_b, L0_ffn_w1, L0_ffn_b1, L0_ffn_w2, L0_ffn_b2):
    import concourse.bacc as bacc
    from concourse.bass_utils import run_bass_kernel_spmd

    con = np.ascontiguousarray
    arrays = dict(shape_constants())
    arrays["xT"] = con(np.asarray(L0_attn_x).reshape(TOKENS, DIM).T)
    w = np.asarray(L0_attn_Wqkv).T
    even = np.concatenate([h * AHD + np.r_[0:AHD:2, 1:AHD:2] for h in range(AH)])
    odd = np.concatenate([h * AHD + np.r_[1:AHD:2, 0:AHD:2] for h in range(AH)])
    q, k, v = w[:, 0:P], w[:, P:2 * P], w[:, 2 * P:3 * P]
    arrays["awt"] = con(np.concatenate([q[:, even], q[:, odd], k[:, even], k[:, odd], v], 1))
    arrays["awo"] = con(np.asarray(L0_attn_Wout).T)
    arrays["wqkv"] = con(L0_ffn_wqkv)
    arrays["wo"] = con(L0_ffn_wo)
    arrays["w1"] = con(L0_ffn_w1)
    arrays["w2"] = con(L0_ffn_w2)
    arrays["vecs"] = con(np.stack([L0_ffn_ln_g, L0_ffn_ln_b, L0_ffn_b2], -1))
    b = np.zeros((DEPTH, 2, NPART * P), np.asarray(L0_ffn_b1).dtype)
    b[:, :, 0:HID] = np.asarray(L0_ffn_b1).reshape(DEPTH, 2, HID)
    arrays["b1"] = con(b.reshape(DEPTH, 2 * NPART, P).transpose(0, 2, 1))
    s = np.stack([L0_ffn_q_scale, L0_ffn_k_scale], 1)
    arrays["scales"] = con(np.broadcast_to(s[:, None], (DEPTH, P, 2, HD)))

    nc = bacc.Bacc("TRN2", target_bir_lowering=False, num_devices=1, dynamic_dma_scratch_size=1024)
    ins = {n: nc.dram_tensor(f"in_{n}", x.shape, mybir.dt.from_np(x.dtype), kind="ExternalInput").ap()
           for n, x in arrays.items()}
    out = nc.dram_tensor("out_T", (DIM, TOKENS), F32, kind="ExternalOutput").ap()
    build(nc, ins, out)
    r = run_bass_kernel_spmd(nc, [{f"in_{n}": x for n, x in arrays.items()}], core_ids=[0])
    return con(r.results[0]["out_T"].T).reshape(BATCH, SEQ, DIM)
```
